# Optimizing a Trainium2 kernel written in Bass

```python
import numpy as np
import jax
import jax.numpy as jnp

def _softmax(x, axis=-1):
    return jax.nn.softmax(x, axis=axis)

def _gelu(x):
    return jax.nn.gelu(x, approximate=True)

def _silu(x):
    return jax.nn.silu(x)

def _sigmoid(x):
    return jax.nn.sigmoid(x)

def _layernorm(x, axis=-1, eps=1e-05):
    m = jnp.mean(x, axis=axis, keepdims=True)
    v = jnp.var(x, axis=axis, keepdims=True)
    return (x - m) / jnp.sqrt(v + eps)

def _scatter_add(tgt, idx, src, axis=0):
    return tgt.at[idx].add(src)

def _segment_sum(src, seg, n):
    return jax.ops.segment_sum(src, seg, n)
kernel_name = 'mk_decoder_postln_d2_seqx_r8_1dafcf'

def setup_inputs(seed: int=0):
    np.random.seed(seed)
    _w = jnp.asarray

    def _rec_inputs():
        import jax
        import jax.numpy as jnp
        _rk = jax.random.key(seed)
        x = -0.0005207 + 1.001 * jax.random.normal(jax.random.fold_in(_rk, 1), (2, 256, 128), jnp.float32)
        _lenS = 256 - jax.random.randint(jax.random.fold_in(_rk, 7), (2,), 0, max(1, 256 // 4) + 1, jnp.int32)
        _lenS2 = 512 - jax.random.randint(jax.random.fold_in(_rk, 8), (2,), 0, max(1, 512 // 4) + 1, jnp.int32)
        _ctx_1024P = jax.random.normal(jax.random.fold_in(_rk, 11), (2, 16, 128), jnp.float32)
        _ctx_1024c = jax.random.dirichlet(jax.random.fold_in(_rk, 511), 0.3 * jnp.ones((16,), jnp.float32), (2, 512))
        _ctx_1024t = jnp.einsum('bsk,bkd->bsd', _ctx_1024c, _ctx_1024P)
        _ctx_1024t = _ctx_1024t * jax.lax.rsqrt(jnp.mean(jnp.square(_ctx_1024t)) + 1e-12) * 0.953939
        ctx_1024 = -1.52775e-05 + 0.999936 * (_ctx_1024t + 0.3 * jax.random.normal(jax.random.fold_in(_rk, 611), (2, 512, 128), jnp.float32))
        _validS = jnp.arange(256)[None, :] < _lenS[:, None]
        _validS2 = jnp.arange(512)[None, :] < _lenS2[:, None]
        _causal = jnp.tril(jnp.ones((256, 256), dtype=bool))
        mask_BxSxS2_bk1 = jnp.broadcast_to(_validS2[:, None, :], (2, 256, 512))
        return (x, ctx_1024, mask_BxSxS2_bk1)
    x, ctx_1024, mask_BxSxS2_bk1 = _rec_inputs()

    def _L0_attn_setup():
        import jax, jax.numpy as jnp
        import numpy as np
        D_MODEL = 128
        D_STATE = 16
        B, L = (4, 256)

        def _ln(x, g, b, eps=1e-05):
            mu = x.mean(-1, keepdims=True)
            var = ((x - mu) ** 2).mean(-1, keepdims=True)
            return (x - mu) * jax.lax.rsqrt(var + eps) * g + b

        def _selective_ssm(x, dt_w, dt_b, Bp_w, Bp_b, Cp_w, Cp_b, A_log, D_p):
            delta = jax.nn.softplus(x @ dt_w + dt_b)
            Bt = x @ Bp_w + Bp_b
            Ct = x @ Cp_w + Cp_b
            A = -jnp.exp(A_log)

            def step(h, inp):
                xt, dt, bt, ct = inp
                dA = jnp.exp(dt[..., None] * A)
                dBx = dt[..., None] * bt[:, None, :] * xt[..., None]
                h = dA * h + dBx
                y = jnp.einsum('bdn,bn->bd', h, ct)
                return (h, y)
            xs = (jnp.swapaxes(x, 0, 1), jnp.swapaxes(delta, 0, 1), jnp.swapaxes(Bt, 0, 1), jnp.swapaxes(Ct, 0, 1))
            h0 = jnp.zeros((x.shape[0], D_MODEL, D_STATE), dtype=x.dtype)
            _, ys = jax.lax.scan(step, h0, xs)
            return jnp.swapaxes(ys, 0, 1) + D_p * x

        def _forward(x, ln1_g, ln1_b, ln_g, ln_b, w1_w, w1_b, v1_w, v1_b, w2_w, w2_b, conv_w, dt_w, dt_b, Bp_w, Bp_b, Cp_w, Cp_b, A_log, D_p, ln2_g, ln2_b, ff1_w, ff1_b, ff2_w, ff2_b):
            res = x
            xn = _ln(x, ln1_g, ln1_b)
            xm = _ln(xn, ln_g, ln_b)
            x1 = xm @ w1_w + w1_b
            x1t = jnp.swapaxes(x1, 1, 2)
            xc = jax.lax.conv_general_dilated(x1t, conv_w, window_strides=(1,), padding=[(1, 1)], feature_group_count=D_MODEL, dimension_numbers=('NCH', 'OIH', 'NCH'))
            xc = jax.nn.silu(jnp.swapaxes(xc, 1, 2))
            y = _selective_ssm(xc, dt_w, dt_b, Bp_w, Bp_b, Cp_w, Cp_b, A_log, D_p)
            v = jax.nn.silu(xm @ v1_w + v1_b)
            mo = y * v @ w2_w + w2_b
            x = mo + res
            res2 = x
            xn2 = _ln(x, ln2_g, ln2_b)
            h = jax.nn.gelu(xn2 @ ff1_w + ff1_b, approximate=False)
            return h @ ff2_w + ff2_b + res2
        key = jax.random.key(seed)
        ks = jax.random.split(key, 16)
        s = 0.02
        d, n = (D_MODEL, D_STATE)
        inp = {'x': jax.random.normal(ks[0], (B, L, d), jnp.float32), 'ln1_g': jnp.ones((d,), jnp.float32), 'ln1_b': jnp.zeros((d,), jnp.float32), 'ln_g': jnp.ones((d,), jnp.float32), 'ln_b': jnp.zeros((d,), jnp.float32), 'w1_w': jax.random.normal(ks[1], (d, d), jnp.float32) * s, 'w1_b': jnp.zeros((d,), jnp.float32), 'v1_w': jax.random.normal(ks[2], (d, d), jnp.float32) * s, 'v1_b': jnp.zeros((d,), jnp.float32), 'w2_w': jax.random.normal(ks[3], (d, d), jnp.float32) * s, 'w2_b': jnp.zeros((d,), jnp.float32), 'conv_w': jax.random.normal(ks[4], (d, 1, 3), jnp.float32) * s, 'dt_w': jax.random.normal(ks[5], (d, d), jnp.float32) * s, 'dt_b': jnp.zeros((d,), jnp.float32), 'Bp_w': jax.random.normal(ks[6], (d, n), jnp.float32) * s, 'Bp_b': jnp.zeros((n,), jnp.float32), 'Cp_w': jax.random.normal(ks[7], (d, n), jnp.float32) * s, 'Cp_b': jnp.zeros((n,), jnp.float32), 'A_log': jnp.tile(jnp.log(jnp.arange(1, n + 1, dtype=jnp.float32)), (d, 1)), 'D_p': jnp.ones((d,), jnp.float32), 'ln2_g': jnp.ones((d,), jnp.float32), 'ln2_b': jnp.zeros((d,), jnp.float32), 'ff1_w': jax.random.normal(ks[8], (d, 3 * d), jnp.float32) * s, 'ff1_b': jnp.zeros((3 * d,), jnp.float32), 'ff2_w': jax.random.normal(ks[9], (3 * d, d), jnp.float32) * s, 'ff2_b': jnp.zeros((d,), jnp.float32)}
        return inp
    _L0_attn_all = _L0_attn_setup()
    _L0_attn_in = {k: v for k, v in _L0_attn_all.items() if k in ('ln1_g', 'ln1_b', 'ln_g', 'ln_b', 'w1_w', 'w1_b', 'v1_w', 'v1_b', 'w2_w', 'w2_b', 'conv_w', 'dt_w', 'dt_b', 'Bp_w', 'Bp_b', 'Cp_w', 'Cp_b', 'A_log', 'D_p', 'ln2_g', 'ln2_b', 'ff1_w', 'ff1_b', 'ff2_w', 'ff2_b')}
    del _L0_attn_all

    def _L0_xattn_setup():
        import jax, jax.numpy as jnp
        import numpy as np
        DIM = 128
        HEADS = 16
        DHEAD = 64
        INNER = HEADS * DHEAD
        EPS = 1e-05

        def layer_norm(x, g, b):
            mu = jnp.mean(x, axis=-1, keepdims=True)
            var = jnp.mean(jnp.square(x - mu), axis=-1, keepdims=True)
            return (x - mu) * jax.lax.rsqrt(var + EPS) * g + b

        def apply_rope(x, cos, sin):
            d2 = x.shape[-1] // 2
            x1, x2 = (x[..., :d2], x[..., d2:])
            return jnp.concatenate([x1 * cos - x2 * sin, x2 * cos + x1 * sin], axis=-1)
        key = jax.random.key(seed)
        ks = jax.random.split(key, 10)
        B, N, S = (8, 32, 512)
        latents = jax.random.normal(ks[0], (B, N, DIM), dtype=jnp.float32)
        context = jax.random.normal(ks[1], (B, S, DIM), dtype=jnp.float32)
        cos = jax.random.uniform(ks[2], (S, DHEAD // 2), dtype=jnp.float32)
        sin = jax.random.uniform(ks[3], (S, DHEAD // 2), dtype=jnp.float32)
        init = lambda k, shp, fan_in: jax.random.normal(k, shp, dtype=jnp.float32) / np.sqrt(fan_in)
        return {'latents': latents, 'context': context, 'cos': cos, 'sin': sin, 'ln_lat_g': jnp.ones((DIM,), jnp.float32), 'ln_lat_b': jnp.zeros((DIM,), jnp.float32), 'ln_ctx_g': jnp.ones((DIM,), jnp.float32), 'ln_ctx_b': jnp.zeros((DIM,), jnp.float32), 'Wq': init(ks[4], (DIM, INNER), DIM), 'Wkv': init(ks[5], (DIM, 2 * INNER), DIM), 'Wo': init(ks[6], (INNER, DIM), INNER), 'bo': jnp.zeros((DIM,), jnp.float32)}
    _L0_xattn_all = _L0_xattn_setup()
    _L0_xattn_in = {k: v for k, v in _L0_xattn_all.items() if k in ('cos', 'sin', 'ln_lat_g', 'ln_lat_b', 'ln_ctx_g', 'ln_ctx_b', 'Wq', 'Wkv', 'Wo', 'bo')}
    del _L0_xattn_all

    def _L0_ffn_setup():
        import jax, jax.numpy as jnp
        import numpy as np
        HIDDEN = 128
        NUM_EXPERTS = 8
        TOP_K = 2
        FFN = 512
        BATCH, SEQ = (4, 256)
        key = jax.random.key(seed)
        k_x, k_r, k_w1, k_w2 = jax.random.split(key, 4)
        x = jax.random.normal(k_x, (BATCH, SEQ, HIDDEN), dtype=jnp.float32)
        router_w = jax.random.normal(k_r, (NUM_EXPERTS, HIDDEN), dtype=jnp.float32) * (1.0 / np.sqrt(HIDDEN))
        lim = float(np.sqrt(6.0 / (FFN + HIDDEN)))
        expert_w1 = jax.random.uniform(k_w1, (NUM_EXPERTS, FFN, HIDDEN), dtype=jnp.float32, minval=-lim, maxval=lim)
        expert_w2 = jax.random.uniform(k_w2, (NUM_EXPERTS, HIDDEN, FFN), dtype=jnp.float32, minval=-lim, maxval=lim)
        return {'x': x, 'router_w': router_w, 'expert_w1': expert_w1, 'expert_w2': expert_w2}
    _L0_ffn_all = _L0_ffn_setup()
    _L0_ffn_in = {k: v for k, v in _L0_ffn_all.items() if k in ('router_w', 'expert_w1', 'expert_w2')}
    del _L0_ffn_all

    def _L1_attn_setup():
        import jax, jax.numpy as jnp
        import numpy as np
        NUM_HEAD = 16
        D_Q = 64
        D_KV = 64
        ROPE_BASE = 10000.0

        def _cos_sin(seq_len, dim):
            pos = jnp.arange(seq_len, dtype=jnp.float32)[:, None]
            ids = jnp.arange(dim // 2, dtype=jnp.float32)
            theta = ROPE_BASE ** (-2.0 * ids) / (dim // 2)
            r = pos * theta[None, :]
            return (jnp.cos(r), jnp.sin(r))

        def _rope(x, cos, sin):
            b, s, d = x.shape
            xv = x.reshape(b, s, d // 2, 2)
            x0, x1 = (xv[..., 0], xv[..., 1])
            out = jnp.stack([x0 * cos - x1 * sin, x1 * cos + x0 * sin], axis=-1)
            return out.reshape(b, s, d)
        key = jax.random.key(seed)
        ks = jax.random.split(key, 10)
        d_model, d_q, d_kv = (128, D_Q, D_KV)
        b, s = (2, 256)
        w = lambda k, i, o: jax.random.normal(k, (i, o), dtype=jnp.float32) * 0.02
        return {'x': jax.random.normal(ks[0], (b, s, d_model), dtype=jnp.float32), 'Wd_q_w': w(ks[1], d_model, d_q), 'Wd_q_b': jnp.zeros((d_q,), jnp.float32), 'Wu_q_w': w(ks[2], d_q, d_model), 'Wu_q_b': jnp.zeros((d_model,), jnp.float32), 'Wq_r_w': w(ks[3], d_q, d_model), 'Wq_r_b': jnp.zeros((d_model,), jnp.float32), 'Wk_r_w': w(ks[4], d_model, d_model), 'Wk_r_b': jnp.zeros((d_model,), jnp.float32), 'Wd_kv_w': w(ks[5], d_model, d_kv), 'Wd_kv_b': jnp.zeros((d_kv,), jnp.float32), 'Wu_k_w': w(ks[6], d_kv, d_model), 'Wu_k_b': jnp.zeros((d_model,), jnp.float32), 'Wu_v_w': w(ks[7], d_kv, d_model), 'Wu_v_b': jnp.zeros((d_model,), jnp.float32), 'Wo_w': w(ks[8], d_model, d_model), 'Wo_b': jnp.zeros((d_model,), jnp.float32)}
    _L1_attn_all = _L1_attn_setup()
    _L1_attn_in = {k: v for k, v in _L1_attn_all.items() if k in ('Wd_q_w', 'Wd_q_b', 'Wu_q_w', 'Wu_q_b', 'Wq_r_w', 'Wq_r_b', 'Wk_r_w', 'Wk_r_b', 'Wd_kv_w', 'Wd_kv_b', 'Wu_k_w', 'Wu_k_b', 'Wu_v_w', 'Wu_v_b', 'Wo_w', 'Wo_b')}
    del _L1_attn_all

    def _L1_xattn_setup():
        import jax, jax.numpy as jnp
        import numpy as np
        B, S, D_MODEL, HEADS = (4, 256, 128, 16)
        D_HEAD = D_MODEL // HEADS
        key = jax.random.key(seed)
        ks = jax.random.split(key, 10)
        scale = 1.0 / np.sqrt(D_MODEL)
        return {'query': jax.random.normal(ks[0], (B, S, D_MODEL), dtype=jnp.float32), 'key_': jax.random.normal(ks[1], (B, S, D_MODEL), dtype=jnp.float32), 'value': jax.random.normal(ks[2], (B, S, D_MODEL), dtype=jnp.float32), 'mask': jax.random.randint(ks[3], (B, S, S), 0, 2).astype(bool), 'Wq': jax.random.normal(ks[4], (D_MODEL, HEADS, D_HEAD), dtype=jnp.float32) * scale, 'bq': jnp.zeros((HEADS, D_HEAD), dtype=jnp.float32), 'Wk': jax.random.normal(ks[5], (D_MODEL, HEADS, D_HEAD), dtype=jnp.float32) * scale, 'bk': jnp.zeros((HEADS, D_HEAD), dtype=jnp.float32), 'Wv': jax.random.normal(ks[6], (D_MODEL, HEADS, D_HEAD), dtype=jnp.float32) * scale, 'bv': jnp.zeros((HEADS, D_HEAD), dtype=jnp.float32), 'Wo': jax.random.normal(ks[7], (HEADS, D_HEAD, D_MODEL), dtype=jnp.float32) * (1.0 / np.sqrt(D_MODEL)), 'bo': jnp.zeros((D_MODEL,), dtype=jnp.float32)}
    _L1_xattn_all = _L1_xattn_setup()
    _L1_xattn_in = {k: v for k, v in _L1_xattn_all.items() if k in ('Wq', 'bq', 'Wk', 'bk', 'Wv', 'bv', 'Wo', 'bo')}
    del _L1_xattn_all

    def _L1_ffn_setup():
        import jax, jax.numpy as jnp
        import numpy as np
        HIDDEN = 128
        MOE_INTER = 64
        SHARED_INTER = 256
        N_EXPERTS = 32
        TOP_K = 6
        N_GROUP = 8
        TOPK_GROUP = 4
        ROUTED_SCALE = 2.5

        def _relu2(x):
            return jnp.square(jax.nn.relu(x))

        def _router(x, gate_w, e_bias):
            T = x.shape[0]
            logits = x.astype(jnp.float32) @ gate_w.astype(jnp.float32).T
            scores = jax.nn.sigmoid(logits)
            sc = scores + e_bias[None, :]
            g = sc.reshape(T, N_GROUP, N_EXPERTS // N_GROUP)
            group_scores = jax.lax.top_k(g, 2)[0].sum(-1)
            group_idx = jax.lax.top_k(group_scores, TOPK_GROUP)[1]
            group_mask = jnp.zeros_like(group_scores).at[jnp.arange(T)[:, None], group_idx].set(1.0)
            score_mask = jnp.repeat(group_mask, N_EXPERTS // N_GROUP, axis=1)
            masked = jnp.where(score_mask > 0, sc, 0.0)
            topk_idx = jax.lax.stop_gradient(jax.lax.top_k(masked, TOP_K)[1])
            topk_w = jnp.take_along_axis(scores, topk_idx, axis=1)
            topk_w = topk_w / (topk_w.sum(-1, keepdims=True) + 1e-20)
            topk_w = topk_w * ROUTED_SCALE
            return (topk_idx, topk_w)
        if __name__ == '__main__':
            out = reference(**setup_inputs())
            print(out.shape, out.dtype)
        key = jax.random.key(seed)
        ks = jax.random.split(key, 6)
        s = 0.02
        return {'hidden_states': jax.random.normal(ks[0], (2, 128, HIDDEN), jnp.float32), 'gate_w': jax.random.normal(ks[1], (N_EXPERTS, HIDDEN), jnp.float32) * s, 'e_bias': jnp.zeros((N_EXPERTS,), jnp.float32), 'up_w': jax.random.normal(ks[2], (N_EXPERTS, MOE_INTER, HIDDEN), jnp.float32) * s, 'down_w': jax.random.normal(ks[3], (N_EXPERTS, HIDDEN, MOE_INTER), jnp.float32) * s, 'shared_up_w': jax.random.normal(ks[4], (SHARED_INTER, HIDDEN), jnp.float32) * s, 'shared_down_w': jax.random.normal(ks[5], (HIDDEN, SHARED_INTER), jnp.float32) * s}
    _L1_ffn_all = _L1_ffn_setup()
    _L1_ffn_in = {k: v for k, v in _L1_ffn_all.items() if k in ('gate_w', 'e_bias', 'up_w', 'down_w', 'shared_up_w', 'shared_down_w')}
    del _L1_ffn_all
    return {'x': x, 'ctx_1024': ctx_1024, 'mask_BxSxS2_bk1': mask_BxSxS2_bk1, 'L0_attn_ln1_g': _L0_attn_in['ln1_g'], 'L0_attn_ln1_b': _L0_attn_in['ln1_b'], 'L0_attn_ln_g': _L0_attn_in['ln_g'], 'L0_attn_ln_b': _L0_attn_in['ln_b'], 'L0_attn_w1_w': _L0_attn_in['w1_w'], 'L0_attn_w1_b': _L0_attn_in['w1_b'], 'L0_attn_v1_w': _L0_attn_in['v1_w'], 'L0_attn_v1_b': _L0_attn_in['v1_b'], 'L0_attn_w2_w': _L0_attn_in['w2_w'], 'L0_attn_w2_b': _L0_attn_in['w2_b'], 'L0_attn_conv_w': _L0_attn_in['conv_w'], 'L0_attn_dt_w': _L0_attn_in['dt_w'], 'L0_attn_dt_b': _L0_attn_in['dt_b'], 'L0_attn_Bp_w': _L0_attn_in['Bp_w'], 'L0_attn_Bp_b': _L0_attn_in['Bp_b'], 'L0_attn_Cp_w': _L0_attn_in['Cp_w'], 'L0_attn_Cp_b': _L0_attn_in['Cp_b'], 'L0_attn_A_log': _L0_attn_in['A_log'], 'L0_attn_D_p': _L0_attn_in['D_p'], 'L0_attn_ln2_g': _L0_attn_in['ln2_g'], 'L0_attn_ln2_b': _L0_attn_in['ln2_b'], 'L0_attn_ff1_w': _L0_attn_in['ff1_w'], 'L0_attn_ff1_b': _L0_attn_in['ff1_b'], 'L0_attn_ff2_w': _L0_attn_in['ff2_w'], 'L0_attn_ff2_b': _L0_attn_in['ff2_b'], 'L0_xattn_cos': _L0_xattn_in['cos'], 'L0_xattn_sin': _L0_xattn_in['sin'], 'L0_xattn_ln_lat_g': _L0_xattn_in['ln_lat_g'], 'L0_xattn_ln_lat_b': _L0_xattn_in['ln_lat_b'], 'L0_xattn_ln_ctx_g': _L0_xattn_in['ln_ctx_g'], 'L0_xattn_ln_ctx_b': _L0_xattn_in['ln_ctx_b'], 'L0_xattn_Wq': _L0_xattn_in['Wq'], 'L0_xattn_Wkv': _L0_xattn_in['Wkv'], 'L0_xattn_Wo': _L0_xattn_in['Wo'], 'L0_xattn_bo': _L0_xattn_in['bo'], 'L0_ffn_router_w': _L0_ffn_in['router_w'], 'L0_ffn_expert_w1': _L0_ffn_in['expert_w1'], 'L0_ffn_expert_w2': _L0_ffn_in['expert_w2'], 'L1_attn_Wd_q_w': _L1_attn_in['Wd_q_w'], 'L1_attn_Wd_q_b': _L1_attn_in['Wd_q_b'], 'L1_attn_Wu_q_w': _L1_attn_in['Wu_q_w'], 'L1_attn_Wu_q_b': _L1_attn_in['Wu_q_b'], 'L1_attn_Wq_r_w': _L1_attn_in['Wq_r_w'], 'L1_attn_Wq_r_b': _L1_attn_in['Wq_r_b'], 'L1_attn_Wk_r_w': _L1_attn_in['Wk_r_w'], 'L1_attn_Wk_r_b': _L1_attn_in['Wk_r_b'], 'L1_attn_Wd_kv_w': _L1_attn_in['Wd_kv_w'], 'L1_attn_Wd_kv_b': _L1_attn_in['Wd_kv_b'], 'L1_attn_Wu_k_w': _L1_attn_in['Wu_k_w'], 'L1_attn_Wu_k_b': _L1_attn_in['Wu_k_b'], 'L1_attn_Wu_v_w': _L1_attn_in['Wu_v_w'], 'L1_attn_Wu_v_b': _L1_attn_in['Wu_v_b'], 'L1_attn_Wo_w': _L1_attn_in['Wo_w'], 'L1_attn_Wo_b': _L1_attn_in['Wo_b'], 'L1_xattn_Wq': _L1_xattn_in['Wq'], 'L1_xattn_bq': _L1_xattn_in['bq'], 'L1_xattn_Wk': _L1_xattn_in['Wk'], 'L1_xattn_bk': _L1_xattn_in['bk'], 'L1_xattn_Wv': _L1_xattn_in['Wv'], 'L1_xattn_bv': _L1_xattn_in['bv'], 'L1_xattn_Wo': _L1_xattn_in['Wo'], 'L1_xattn_bo': _L1_xattn_in['bo'], 'L1_ffn_gate_w': _L1_ffn_in['gate_w'], 'L1_ffn_e_bias': _L1_ffn_in['e_bias'], 'L1_ffn_up_w': _L1_ffn_in['up_w'], 'L1_ffn_down_w': _L1_ffn_in['down_w'], 'L1_ffn_shared_up_w': _L1_ffn_in['shared_up_w'], 'L1_ffn_shared_down_w': _L1_ffn_in['shared_down_w']}

def reference(x, ctx_1024, mask_BxSxS2_bk1, L0_attn_ln1_g, L0_attn_ln1_b, L0_attn_ln_g, L0_attn_ln_b, L0_attn_w1_w, L0_attn_w1_b, L0_attn_v1_w, L0_attn_v1_b, L0_attn_w2_w, L0_attn_w2_b, L0_attn_conv_w, L0_attn_dt_w, L0_attn_dt_b, L0_attn_Bp_w, L0_attn_Bp_b, L0_attn_Cp_w, L0_attn_Cp_b, L0_attn_A_log, L0_attn_D_p, L0_attn_ln2_g, L0_attn_ln2_b, L0_attn_ff1_w, L0_attn_ff1_b, L0_attn_ff2_w, L0_attn_ff2_b, L0_xattn_cos, L0_xattn_sin, L0_xattn_ln_lat_g, L0_xattn_ln_lat_b, L0_xattn_ln_ctx_g, L0_xattn_ln_ctx_b, L0_xattn_Wq, L0_xattn_Wkv, L0_xattn_Wo, L0_xattn_bo, L0_ffn_router_w, L0_ffn_expert_w1, L0_ffn_expert_w2, L1_attn_Wd_q_w, L1_attn_Wd_q_b, L1_attn_Wu_q_w, L1_attn_Wu_q_b, L1_attn_Wq_r_w, L1_attn_Wq_r_b, L1_attn_Wk_r_w, L1_attn_Wk_r_b, L1_attn_Wd_kv_w, L1_attn_Wd_kv_b, L1_attn_Wu_k_w, L1_attn_Wu_k_b, L1_attn_Wu_v_w, L1_attn_Wu_v_b, L1_attn_Wo_w, L1_attn_Wo_b, L1_xattn_Wq, L1_xattn_bq, L1_xattn_Wk, L1_xattn_bk, L1_xattn_Wv, L1_xattn_bv, L1_xattn_Wo, L1_xattn_bo, L1_ffn_gate_w, L1_ffn_e_bias, L1_ffn_up_w, L1_ffn_down_w, L1_ffn_shared_up_w, L1_ffn_shared_down_w):
    import jax
    import jax.numpy as jnp

    def _L0_attn_ref(x, ln1_g, ln1_b, ln_g, ln_b, w1_w, w1_b, v1_w, v1_b, w2_w, w2_b, conv_w, dt_w, dt_b, Bp_w, Bp_b, Cp_w, Cp_b, A_log, D_p, ln2_g, ln2_b, ff1_w, ff1_b, ff2_w, ff2_b):
        import jax, jax.numpy as jnp
        import numpy as np
        D_MODEL = 128
        D_STATE = 16
        B, L = (4, 256)

        def _ln(x, g, b, eps=1e-05):
            mu = x.mean(-1, keepdims=True)
            var = ((x - mu) ** 2).mean(-1, keepdims=True)
            return (x - mu) * jax.lax.rsqrt(var + eps) * g + b

        def _selective_ssm(x, dt_w, dt_b, Bp_w, Bp_b, Cp_w, Cp_b, A_log, D_p):
            delta = jax.nn.softplus(x @ dt_w + dt_b)
            Bt = x @ Bp_w + Bp_b
            Ct = x @ Cp_w + Cp_b
            A = -jnp.exp(A_log)

            def step(h, inp):
                xt, dt, bt, ct = inp
                dA = jnp.exp(dt[..., None] * A)
                dBx = dt[..., None] * bt[:, None, :] * xt[..., None]
                h = dA * h + dBx
                y = jnp.einsum('bdn,bn->bd', h, ct)
                return (h, y)
            xs = (jnp.swapaxes(x, 0, 1), jnp.swapaxes(delta, 0, 1), jnp.swapaxes(Bt, 0, 1), jnp.swapaxes(Ct, 0, 1))
            h0 = jnp.zeros((x.shape[0], D_MODEL, D_STATE), dtype=x.dtype)
            _, ys = jax.lax.scan(step, h0, xs)
            return jnp.swapaxes(ys, 0, 1) + D_p * x

        def _forward(x, ln1_g, ln1_b, ln_g, ln_b, w1_w, w1_b, v1_w, v1_b, w2_w, w2_b, conv_w, dt_w, dt_b, Bp_w, Bp_b, Cp_w, Cp_b, A_log, D_p, ln2_g, ln2_b, ff1_w, ff1_b, ff2_w, ff2_b):
            res = x
            xn = _ln(x, ln1_g, ln1_b)
            xm = _ln(xn, ln_g, ln_b)
            x1 = xm @ w1_w + w1_b
            x1t = jnp.swapaxes(x1, 1, 2)
            xc = jax.lax.conv_general_dilated(x1t, conv_w, window_strides=(1,), padding=[(1, 1)], feature_group_count=D_MODEL, dimension_numbers=('NCH', 'OIH', 'NCH'))
            xc = jax.nn.silu(jnp.swapaxes(xc, 1, 2))
            y = _selective_ssm(xc, dt_w, dt_b, Bp_w, Bp_b, Cp_w, Cp_b, A_log, D_p)
            v = jax.nn.silu(xm @ v1_w + v1_b)
            mo = y * v @ w2_w + w2_b
            x = mo + res
            res2 = x
            xn2 = _ln(x, ln2_g, ln2_b)
            h = jax.nn.gelu(xn2 @ ff1_w + ff1_b, approximate=False)
            return h @ ff2_w + ff2_b + res2
        return _forward(x, ln1_g, ln1_b, ln_g, ln_b, w1_w, w1_b, v1_w, v1_b, w2_w, w2_b, conv_w, dt_w, dt_b, Bp_w, Bp_b, Cp_w, Cp_b, A_log, D_p, ln2_g, ln2_b, ff1_w, ff1_b, ff2_w, ff2_b)

    def _L0_xattn_ref(latents, context, cos, sin, ln_lat_g, ln_lat_b, ln_ctx_g, ln_ctx_b, Wq, Wkv, Wo, bo):
        import jax, jax.numpy as jnp
        import numpy as np
        DIM = 128
        HEADS = 16
        DHEAD = 64
        INNER = HEADS * DHEAD
        EPS = 1e-05

        def layer_norm(x, g, b):
            mu = jnp.mean(x, axis=-1, keepdims=True)
            var = jnp.mean(jnp.square(x - mu), axis=-1, keepdims=True)
            return (x - mu) * jax.lax.rsqrt(var + EPS) * g + b

        def apply_rope(x, cos, sin):
            d2 = x.shape[-1] // 2
            x1, x2 = (x[..., :d2], x[..., d2:])
            return jnp.concatenate([x1 * cos - x2 * sin, x2 * cos + x1 * sin], axis=-1)
        b, n, _ = latents.shape
        s = context.shape[1]
        lat = layer_norm(latents, ln_lat_g, ln_lat_b)
        ctx = layer_norm(context, ln_ctx_g, ln_ctx_b)
        q = (lat @ Wq).reshape(b, n, HEADS, DHEAD).transpose(0, 2, 1, 3)
        kv = ctx @ Wkv
        k, v = jnp.split(kv, 2, axis=-1)
        k = k.reshape(b, s, HEADS, DHEAD).transpose(0, 2, 1, 3)
        v = v.reshape(b, s, HEADS, DHEAD).transpose(0, 2, 1, 3)
        k = apply_rope(k, cos[None, None], sin[None, None])
        scale = DHEAD ** (-0.5)
        attn = jnp.einsum('bhnd,bhsd->bhns', q, k) * scale
        attn = jnp.clip(attn, -11.0, 11.0)
        attn = jax.nn.softmax(attn, axis=-1)
        out = jnp.einsum('bhns,bhsd->bhnd', attn, v)
        out = out.transpose(0, 2, 1, 3).reshape(b, n, INNER)
        return out @ Wo + bo

    def _L0_ffn_ref(x, router_w, expert_w1, expert_w2):
        import jax, jax.numpy as jnp
        import numpy as np
        HIDDEN = 128
        NUM_EXPERTS = 8
        TOP_K = 2
        FFN = 512
        BATCH, SEQ = (4, 256)
        B, S, D = x.shape
        xf = x.reshape(-1, D)
        scores = xf @ router_w.T
        top_v, top_i = jax.lax.top_k(scores, TOP_K)
        routing_w = jax.nn.softmax(top_v, axis=-1)
        out = jnp.zeros_like(xf)
        for e in range(NUM_EXPERTS):
            w_e = jnp.sum(jnp.where(top_i == e, routing_w, 0.0), axis=-1)
            h = jax.nn.gelu(xf @ expert_w1[e].T, approximate=False)
            out = out + h @ expert_w2[e].T * w_e[:, None]
        return out.reshape(B, S, D)

    def _L1_attn_ref(x, Wd_q_w, Wd_q_b, Wu_q_w, Wu_q_b, Wq_r_w, Wq_r_b, Wk_r_w, Wk_r_b, Wd_kv_w, Wd_kv_b, Wu_k_w, Wu_k_b, Wu_v_w, Wu_v_b, Wo_w, Wo_b):
        import jax, jax.numpy as jnp
        import numpy as np
        NUM_HEAD = 16
        D_Q = 64
        D_KV = 64
        ROPE_BASE = 10000.0

        def _cos_sin(seq_len, dim):
            pos = jnp.arange(seq_len, dtype=jnp.float32)[:, None]
            ids = jnp.arange(dim // 2, dtype=jnp.float32)
            theta = ROPE_BASE ** (-2.0 * ids) / (dim // 2)
            r = pos * theta[None, :]
            return (jnp.cos(r), jnp.sin(r))

        def _rope(x, cos, sin):
            b, s, d = x.shape
            xv = x.reshape(b, s, d // 2, 2)
            x0, x1 = (xv[..., 0], xv[..., 1])
            out = jnp.stack([x0 * cos - x1 * sin, x1 * cos + x0 * sin], axis=-1)
            return out.reshape(b, s, d)
        b, s, d_model = x.shape
        h = NUM_HEAD
        hd = d_model // h
        scale = jnp.sqrt(jnp.float32(h + D_KV + D_Q))

        def heads(t):
            return t.reshape(b, s, h, hd).transpose(0, 2, 1, 3)
        cos, sin = _cos_sin(s, d_model)
        ct_q = x @ Wd_q_w + Wd_q_b
        qt_c = heads(ct_q @ Wu_q_w + Wu_q_b)
        qt_r = heads(_rope(ct_q @ Wq_r_w + Wq_r_b, cos, sin))
        query = qt_c + qt_r
        ct_kv = x @ Wd_kv_w + Wd_kv_b
        kt_c = heads(ct_kv @ Wu_k_w + Wu_k_b)
        kt_r = heads(_rope(x @ Wk_r_w + Wk_r_b, cos, sin))
        key = kt_c + kt_r
        value = heads(ct_kv @ Wu_v_w + Wu_v_b)
        attn = jnp.einsum('bhqd,bhkd->bhqk', query, key) / scale
        attn = jax.nn.softmax(attn, axis=-1)
        out = jnp.einsum('bhqk,bhkd->bhqd', attn, value)
        out = out.transpose(0, 2, 1, 3).reshape(b, s, d_model)
        return out @ Wo_w + Wo_b

    def _L1_xattn_ref(query, key_, value, mask, Wq, bq, Wk, bk, Wv, bv, Wo, bo):
        import jax, jax.numpy as jnp
        import numpy as np
        B, S, D_MODEL, HEADS = (4, 256, 128, 16)
        D_HEAD = D_MODEL // HEADS
        q = jnp.einsum('bse,ehd->bhsd', query, Wq) + bq[:, None, :]
        k = jnp.einsum('bse,ehd->bhsd', key_, Wk) + bk[:, None, :]
        v = jnp.einsum('bse,ehd->bhsd', value, Wv) + bv[:, None, :]
        logits = jnp.einsum('bhsd,bhtd->bhst', q, k)
        logits = jnp.where(mask[:, None, :, :], jnp.float32(-100000000.0), logits)
        score = jax.nn.softmax(logits, axis=-1)
        attn = jnp.einsum('bhst,bhtd->bhsd', score, v) / jnp.sqrt(jnp.float32(D_HEAD))
        out = jnp.einsum('bhsd,hdo->bso', attn, Wo) + bo
        return out

    def _L1_ffn_ref(hidden_states, gate_w, e_bias, up_w, down_w, shared_up_w, shared_down_w):
        import jax, jax.numpy as jnp
        import numpy as np
        HIDDEN = 128
        MOE_INTER = 64
        SHARED_INTER = 256
        N_EXPERTS = 32
        TOP_K = 6
        N_GROUP = 8
        TOPK_GROUP = 4
        ROUTED_SCALE = 2.5

        def _relu2(x):
            return jnp.square(jax.nn.relu(x))

        def _router(x, gate_w, e_bias):
            T = x.shape[0]
            logits = x.astype(jnp.float32) @ gate_w.astype(jnp.float32).T
            scores = jax.nn.sigmoid(logits)
            sc = scores + e_bias[None, :]
            g = sc.reshape(T, N_GROUP, N_EXPERTS // N_GROUP)
            group_scores = jax.lax.top_k(g, 2)[0].sum(-1)
            group_idx = jax.lax.top_k(group_scores, TOPK_GROUP)[1]
            group_mask = jnp.zeros_like(group_scores).at[jnp.arange(T)[:, None], group_idx].set(1.0)
            score_mask = jnp.repeat(group_mask, N_EXPERTS // N_GROUP, axis=1)
            masked = jnp.where(score_mask > 0, sc, 0.0)
            topk_idx = jax.lax.stop_gradient(jax.lax.top_k(masked, TOP_K)[1])
            topk_w = jnp.take_along_axis(scores, topk_idx, axis=1)
            topk_w = topk_w / (topk_w.sum(-1, keepdims=True) + 1e-20)
            topk_w = topk_w * ROUTED_SCALE
            return (topk_idx, topk_w)
        if __name__ == '__main__':
            out = reference(**setup_inputs())
            print(out.shape, out.dtype)
        B, S, H = hidden_states.shape
        x = hidden_states.reshape(-1, H)
        T = x.shape[0]
        topk_idx, topk_w = _router(x, gate_w, e_bias)
        combine = jnp.zeros((T, N_EXPERTS), topk_w.dtype).at[jnp.arange(T)[:, None], topk_idx].add(topk_w)
        h = _relu2(jnp.einsum('th,eih->tei', x, up_w))
        h = h * combine[:, :, None]
        moe_out = jnp.einsum('tei,ehi->th', h, down_w)
        shared = _relu2(x @ shared_up_w.T) @ shared_down_w.T
        return (moe_out + shared).reshape(B, S, H)
    x = _layernorm(x + _L0_attn_ref(x, L0_attn_ln1_g, L0_attn_ln1_b, L0_attn_ln_g, L0_attn_ln_b, L0_attn_w1_w, L0_attn_w1_b, L0_attn_v1_w, L0_attn_v1_b, L0_attn_w2_w, L0_attn_w2_b, L0_attn_conv_w, L0_attn_dt_w, L0_attn_dt_b, L0_attn_Bp_w, L0_attn_Bp_b, L0_attn_Cp_w, L0_attn_Cp_b, L0_attn_A_log, L0_attn_D_p, L0_attn_ln2_g, L0_attn_ln2_b, L0_attn_ff1_w, L0_attn_ff1_b, L0_attn_ff2_w, L0_attn_ff2_b), axis=-1)
    x = _layernorm(x + _L0_xattn_ref(x, ctx_1024, L0_xattn_cos, L0_xattn_sin, L0_xattn_ln_lat_g, L0_xattn_ln_lat_b, L0_xattn_ln_ctx_g, L0_xattn_ln_ctx_b, L0_xattn_Wq, L0_xattn_Wkv, L0_xattn_Wo, L0_xattn_bo), axis=-1)
    x = _layernorm(x + _L0_ffn_ref(x, L0_ffn_router_w, L0_ffn_expert_w1, L0_ffn_expert_w2), axis=-1)
    x = _layernorm(x + _L1_attn_ref(x, L1_attn_Wd_q_w, L1_attn_Wd_q_b, L1_attn_Wu_q_w, L1_attn_Wu_q_b, L1_attn_Wq_r_w, L1_attn_Wq_r_b, L1_attn_Wk_r_w, L1_attn_Wk_r_b, L1_attn_Wd_kv_w, L1_attn_Wd_kv_b, L1_attn_Wu_k_w, L1_attn_Wu_k_b, L1_attn_Wu_v_w, L1_attn_Wu_v_b, L1_attn_Wo_w, L1_attn_Wo_b), axis=-1)
    x = _layernorm(x + _L1_xattn_ref(x, ctx_1024, ctx_1024, mask_BxSxS2_bk1, L1_xattn_Wq, L1_xattn_bq, L1_xattn_Wk, L1_xattn_bk, L1_xattn_Wv, L1_xattn_bv, L1_xattn_Wo, L1_xattn_bo), axis=-1)
    x = _layernorm(x + _L1_ffn_ref(x, L1_ffn_gate_w, L1_ffn_e_bias, L1_ffn_up_w, L1_ffn_down_w, L1_ffn_shared_up_w, L1_ffn_shared_down_w), axis=-1)
    return x

_drawn_inputs = setup_inputs


def setup_inputs(seed=0):
    import zlib

    import numpy as np

    out = dict(_drawn_inputs(seed))
    spreads = {'L0_attn_ln1_g': (1.0, 0.6),
     'L0_attn_ln1_b': (0.0, 0.8),
     'L0_attn_ln_g': (1.0, 0.6),
     'L0_attn_ln_b': (0.0, 0.8),
     'L0_attn_w1_b': (0.0, 0.8),
     'L0_attn_v1_b': (0.0, 0.8),
     'L0_attn_w2_b': (0.0, 0.1),
     'L0_attn_dt_b': (0.0, 0.8),
     'L0_attn_Bp_b': (0.0, 0.8),
     'L0_attn_Cp_b': (0.0, 0.8),
     'L0_attn_D_p': (1.0, 0.6),
     'L0_attn_ln2_g': (1.0, 0.6),
     'L0_attn_ln2_b': (0.0, 0.774),
     'L0_attn_ff1_b': (0.0, 0.285),
     'L0_attn_ff2_b': (0.0, 0.1),
     'L0_xattn_ln_lat_g': (1.0, 0.2),
     'L0_xattn_ln_lat_b': (0.0, 0.281),
     'L0_xattn_ln_ctx_g': (1.0, 0.2),
     'L0_xattn_ln_ctx_b': (0.0, 0.1),
     'L0_xattn_bo': (0.0, 0.1),
     'L1_attn_Wd_q_b': (0.0, 0.8),
     'L1_attn_Wu_q_b': (0.0, 0.8),
     'L1_attn_Wq_r_b': (0.0, 0.8),
     'L1_attn_Wk_r_b': (0.0, 0.8),
     'L1_attn_Wd_kv_b': (0.0, 0.8),
     'L1_attn_Wu_k_b': (0.0, 0.8),
     'L1_attn_Wu_v_b': (0.0, 0.377),
     'L1_attn_Wo_b': (0.0, 0.1),
     'L1_xattn_bq': (0.0, 0.306),
     'L1_xattn_bk': (0.0, 0.8),
     'L1_xattn_bv': (0.0, 0.1),
     'L1_xattn_bo': (0.0, 0.1),
     'L1_ffn_e_bias': (0.0, 0.8)}
    factors = {'L0_attn_w1_w': 8.0,
     'L0_attn_v1_w': 8.0,
     'L0_attn_w2_w': 8.0,
     'L0_attn_conv_w': 8.0,
     'L0_attn_dt_w': 8.0,
     'L0_attn_Bp_w': 8.0,
     'L0_attn_Cp_w': 8.0,
     'L0_attn_A_log': 8.0,
     'L1_attn_Wd_q_w': 8.0,
     'L1_attn_Wu_q_w': 8.0,
     'L1_attn_Wq_r_w': 8.0,
     'L1_attn_Wk_r_w': 8.0,
     'L1_attn_Wd_kv_w': 8.0,
     'L1_attn_Wu_k_w': 8.0,
     'L1_attn_Wu_v_w': 8.0,
     'L1_ffn_gate_w': 7.334,
     'L1_ffn_up_w': 6.118,
     'L1_ffn_down_w': 5.482,
     'L1_ffn_shared_up_w': 3.034}
    for name, (base, spread) in spreads.items():
        noise = np.random.default_rng([zlib.crc32(name.encode()), seed]).standard_normal(out[name].shape)
        drawn = base * np.exp(spread * noise) if base else spread * noise
        out[name] = jnp.asarray(drawn.astype(out[name].dtype))
    for name, factor in factors.items():
        out[name] = (out[name] * factor).astype(out[name].dtype)
    return out
```

```python
from contextlib import ExitStack

import numpy as np

from concourse import mybir

P = 128
D = 128
B, T = 2, 256
N = B * T
NJ = N // P
CS = 512
NC_TILES = B * CS // P
STATE = 16
GD = P // STATE
NG = D // GD
H = 16
DH0 = 64
DH = 8
NPAIR = H // 2
FF = 3
E0, F0 = 8, 512 // P
E1, I1 = 32, 64
C1 = E1 * I1 // P
SH = 256 // P
PARTS = 3
STACK = PARTS * PARTS * DH
EPS = 1e-5
CLIP = 11.0
BIG = 2.0 ** 100
FAR = 3.0e38

VEC = {}
for _name, _width in (
    ("w1_b", 1), ("v1_b", 1), ("ln_g", 1), ("ln_b", 1), ("conv", 3), ("dt_b", 1), ("Bp_b", 1),
    ("Cp_b", 1), ("A_log", NG), ("D_p", 1), ("ln2_g", 1), ("ln2_b", 1), ("ff1_b", FF),
    ("lat_g", 1), ("lat_b", 1), ("ctx_g", 1), ("ctx_b", 1), ("rope_sign", 1), ("Wd_q_b", 1),
    ("Wd_kv_b", 1), ("Wu_q_b", 1), ("Wq_r_b", 1), ("Wq_s_b", 1), ("Wu_k_b", 1), ("Wk_r_b", 1),
    ("Wk_s_b", 1), ("bq", 1), ("bk", 1),
):
    VEC[_name] = (sum(w for _, w in VEC.values()), _width)
NVEC = sum(w for _, w in VEC.values())
ROWV = ("ln1_g", "ln1_b", "w2_b", "ff2_b", "bo0", "Wu_v_b", "Wo_b", "bv", "bo1")

NORMS = ("ln1", "ln", "ctx", "ln2", "post0", "lat", "post1", "post2", "post3", "post4", "post5")


def program(nc, a, out):
    f32, bf16, u8 = mybir.dt.float32, mybir.dt.bfloat16, mybir.dt.uint8
    ALU, ACT, AX = mybir.AluOpType, mybir.ActivationFunctionType, mybir.AxisListType
    ctx = ExitStack()
    with ctx:
        def sb(name, shape, dt=f32):
            return ctx.enter_context(nc.sbuf_tensor(name, shape, dt))

        def sem(name):
            return ctx.enter_context(nc.semaphore(name))

        def region(name, words):
            t = sb(name, [P, words])

            def take(at, shape, dt=f32):
                n = int(np.prod(shape[1:])) // {f32: 1, bf16: 2, u8: 4}[dt]
                piece = t[0:shape[0], at:at + n]
                names = "abcde"[:len(shape) - 1]
                piece = piece if dt == f32 else piece.bitcast(dt)
                if len(shape) == 2:
                    return piece
                return piece.rearrange(f"p ({' '.join(names)}) -> p {' '.join(names)}",
                                       **dict(zip(names[1:], shape[2:])))
            return take

        vec = sb("vec", [P, NVEC])
        rowv = sb("rowv", [P, len(ROWV), D])
        ident = sb("ident", [P, P])
        w_mix = sb("w_mix", [P, 6, D])
        sel_y = sb("sel_y", [P, NG // 4, 32])
        w_ff = sb("w_ff", [P, 2 * FF, D])
        w_r0 = sb("w_r0", [P, E0])
        w_a1 = sb("w_a1", [P, 2 * 64 + 3 * P])
        w_u1 = sb("w_u1", [64, 5, P])
        rope1 = sb("rope1", [P, 2, T])
        w_x1 = sb("w_x1", [P, 4, D])
        neg_i = sb("neg_i", [P, P], bf16)
        w_g1 = sb("w_g1", [P, E1])
        w_sh = sb("w_sh", [P, 2 * SH, P])
        eb = sb("eb", [P, E1])
        sel = region("sel", 1024)
        sel_g = sel(0, [P, NG, P], bf16)
        sel_e = sel(0, [PARTS * E1, C1, P], bf16)
        attn_w = region("attn_w", 5 * 8 * P)
        w_x0 = attn_w(0, [P, NPAIR, 5, P])
        w_up1 = attn_w(0, [P, C1, P])
        w_dn1 = attn_w(C1 * P, [P, C1, P])
        late = region("late", 8192)
        w_up0 = late(0, [P, E0, F0 * P])
        w_dn0 = late(4096, [P, E0, F0, D])
        qs = late(0, [STACK + PARTS, H, N], bf16)
        v1 = late(4096, [P, NC_TILES, H, 32])
        rl = late(0, [P, 3, N])
        rlc = late(1536, [P, 3, N])
        cms = late(3072, [PARTS * E1, N], bf16)
        cmp_ = late(3328, [E1, PARTS, N], bf16)
        cmf = late(4096, [E1, 2, N])

        def v(name, i=0, rows=P):
            at = VEC[name][0] + i
            return vec[0:rows, at:at + 1]

        def rv4(name):
            return rowv[:, ROWV.index(name):ROWV.index(name) + 1, :].broadcast_to([P, NJ, D])

        x = sb("x", [P, NJ, D])
        x2 = sb("x2", [P, NJ, D])
        resid = sb("resid", [P, NJ, D])
        summed = sb("summed", [P, NJ, D])
        normed = sb("normed", [P, NJ, D])
        stats = sb("stats", [P, NC_TILES, 6])
        meanvar = sb("meanvar", [P, len(NORMS), NC_TILES, 2])
        rstd = sb("rstd", [P, len(NORMS), NC_TILES])
        vareps = sb("vareps", [P, NC_TILES])
        neghalf = sb("neghalf", [P, NC_TILES])
        xT = sb("xT", [P, N])
        cv = sb("cv", [P, 2, N])
        dtmp = sb("dtmp", [P, 3, N])

        mid = region("mid", 6144)
        x1p = mid(0, [P, B, T + 2])
        xc = mid(516, [P, N])
        gate = mid(1028, [P, N])
        Bn = mid(1540, [P, N])
        Cn = mid(2052, [P, N])
        dl = mid(2564, [P, 2, N])
        dparts = mid(3588, [P, 2, PARTS, N], bf16)
        nA = sb("nA", [P, 2, NG])
        big1, big2 = region("big1", 8192), region("big2", 8192)
        dA = big1(0, [P, 2, N])
        dBx = big1(1024, [P, 2, N])
        hs = big1(2048, [P, 4, N])
        hC = big1(4096, [P, 8, N])
        ffh = big2(0, [P, FF, N])

        ctx_r = region("ctx_r", 3 * 1024)
        rope0 = ctx_r(0, [P, 2, CS])
        cxnT = ctx_r(1024, [P, B * CS])
        cx = ctx_r(2048, [P, NC_TILES, D])
        qparts = ctx_r(0, [P, PARTS, B * CS], bf16)
        cxT = attn_w(2 * C1 * P, [P, B * CS])

        kT0 = big1(0, [P, 2, B * CS])
        kt1 = big1(2048, [P, 2, CS])
        kt2 = big1(3072, [P, 2, CS])
        qT0 = big1(4096, [P, 2, N])
        ex = big1(5120, [P, 3, 1024])
        v0 = mid(0, [P, 2, NC_TILES, 2, DH0 + 1])
        rden = sb("rden", [P, NJ, H])
        ao = big2(0, [P, NJ, 1024])
        aoT = big2(4096, [P, NPAIR, N])

        sc0 = sb("sc0", [P, NJ, 2 * E0])
        top0 = sb("top0", [P, NJ, 8])
        pick0 = sb("pick0", [P, NJ, 8])
        mark0 = sb("mark0", [P, NJ, 2 * E0])
        g0 = sb("g0", [P, 4, NJ, E0])
        den0 = sb("den0", [P, 2, NJ])
        eh0 = big1(0, [P, 2, F0, N])

        ks = {"a": big2(0, [P, H, N], bf16), "x": big1(0, [P, H, B * CS], bf16)}
        ks_words = {"a": big2(0, [P, H * N // 2]), "x": big1(0, [P, H * B * CS // 2])}
        ONES2 = float(np.array([0x3F803F80], np.uint32).view(np.float32)[0])
        kxf = big2(0, [P, B * CS])
        kxr = big2(B * CS, [P, B * CS])
        ex1 = big2(4096, [P, 3, 1024])
        qf = mid(0, [P, 2, N])
        cq = mid(1024, [64, 2, N])
        nm = mid(2048, [H, B, 2, T])
        nmp = mid(3072, [H, B, PARTS, T], bf16)
        og = mid(3840, [P, H // 4, N])
        mx = {"a": sb("mx_a", [P, NJ, H]), "x": sb("mx_x", [P, NJ, H])}
        ao1 = x2[:, :, :].rearrange("p j (h d) -> p j h d", h=H)
        aoT1 = w_mix[:, 0:NJ, :].rearrange("p a b -> p (a b)")
        mq8 = ctx_r(2048, [P, NJ, CS], u8)
        mk8 = ctx_r(2560, [P, B, CS // P, T], u8)
        mq = big2(7168, [P, NJ, CS], bf16)
        mk = sel(0, [P, B, CS // P, T], bf16)

        lg1 = late(5120, [P, 4, NJ, E1])
        r1 = sb("r1", [P, 2, NJ, 16])
        sel1 = w_ff[:, 0:4, :].rearrange("p a (j e) -> p (a j) e", e=64).rearrange(
            "p (i j) e -> p i j e", i=2)
        t1 = sb("t1", [P, 4, NJ, 8])
        pr1 = sb("pr1", [P, 2, NJ, 8])
        cmb = sb("cmb", [P, NJ, E1])
        hh = big2(0, [P, C1, N])
        hsh = big1(0, [P, SH, N])

        ps = ctx.enter_context(nc.psum_tensor("ps", [P, 8, 512], f32))

        scr = {k: nc.dram_tensor(f"parts_{k}", [P, PARTS, w], bf16, kind="Internal").ap()
               for k, w in (("qa", N), ("ka", N), ("qx", N), ("kx", B * CS))}

        ld = {k: sem(f"loaded_{k}") for k in (
            "x", "vec", "rowv", "ident", "mix", "sel", "cx", "cxT", "ff", "rope0", "x0", "e0", "a1",
            "x1", "mask", "e1")}
        norm_var = sem("norm_var")
        norm_rstd = sem("norm_rstd")
        norm_out = sem("norm_out")
        consts = sem("consts")
        dve_own, act_own, pool_own = sem("dve_own"), sem("act_own"), sem("pool_own")
        S = {k: sem(k) for k in (
            "xmT_ps", "xmT", "w1_ps", "v1_ps", "x1p_done", "conv_done", "xc_done", "gate_done",
            "dt_ps", "z_done", "BC_ps", "BC_done", "negA", "lg_done", "delta_parts", "dx_parts",
            "spread_d", "spread_x", "dA_done", "dBx_done", "scan_done", "hC_done", "y_ps",
            "yv_done", "mo_ps", "res_ready", "x2_done", "hT_ps", "hT", "ff_ps", "ff_act", "ff2_ps",
            "cxnT_ps", "cxnT_done", "latT_ps", "latT",
            "k0_ps", "k0_mul", "k0_done", "q0_ps", "q0_done", "v0_ps", "v0_done", "s0_ps", "e0_exp",
            "e0_clip", "e0_used", "o0_norm", "o0T_ps", "o0T_done", "y0_ps",
            "xT_ps", "xT_done", "r0_ps", "r0_max", "r0_exp", "up0_ps", "up0_act", "dn0_ps",
            "dn0_acc", "stored",
            "cdown_ps", "cdown_done", "qa_ps", "qa_done", "va_ps", "va_done", "qx_ps", "qx_done",
            "kx_ps", "kx_done", "vx_ps", "vx_done", "mask_done",
            "g1_ps", "g1_exp", "cmb_done", "cmbT_ps", "cms_done", "up1_ps", "relu_done", "cb_ps",
            "cb_mul", "h1_done", "shu_ps", "shr_done", "sh_done", "y1_ps", "rope_signed", "ones")}
        for L in "ax":
            for k in ("q_parts", "k_parts", "q_scr", "k_scr", "q_stack", "k_stack", "smax_ps",
                      "redmax", "mT_ps", "nm_done", "nm_stack0", "nm_stack1", "s_ps", "e_exp", "e_used", "o_sb",
                      "oT_ps", "o_norm", "aT_ps", "aT_done", "y_ps"):
                S[f"{L}_{k}"] = sem(f"{L}_{k}")

        def own(eng, chain):
            count = [0]

            def link(ins):
                count[0] += 1
                ins.then_inc(chain, 1)
                eng.wait_ge(chain, count[0])
            return link

        ORDER = [4 * (s % 4) + s // 4 for s in range(NG)]
        NX = {"a": NORMS.index("post2"), "x": NORMS.index("post3")}
        KEYS = {"a": T, "x": CS}

        block = ctx.enter_context(nc.Block())

        @block.sync
        def _(sp):
            sp.dma_start(x[:], a["x"]).then_inc(ld["x"], 16)
            sp.dma_start(rowv[:], a["rowv"].partition_broadcast(P)).then_inc(ld["rowv"], 16)
            sp.dma_start(vec[:], a["vec"]).then_inc(ld["vec"], 16)
            sp.dma_start(ident[:], a["ident"]).then_inc(ld["ident"], 16)
            sp.dma_start(w_mix[:], a["w_mix"]).then_inc(ld["mix"], 16)
            sp.dma_start(sel_g[:], a["sel_g"]).then_inc(ld["sel"], 16)
            sp.dma_start(sel_y[:], a["sel_y"]).then_inc(ld["sel"], 16)
            sp.dma_start(cx[:], a["cx"]).then_inc(ld["cx"], 16)
            sp.dma_start(w_ff[:], a["w_ff"]).then_inc(ld["ff"], 16)
            sp.dma_start(w_x1[:], a["w_x1"]).then_inc(ld["x1"], 16)
            sp.dma_start(rope0[:], a["rope0"]).then_inc(ld["rope0"], 16)
            sp.dma_start(w_x0[:], a["w_x0"]).then_inc(ld["x0"], 16)
            sp.dma_start(neg_i[:], a["neg_i"]).then_inc(ld["mask"], 16)
            sp.dma_start(w_r0[:], a["w_r0"]).then_inc(ld["e0"], 16)
            sp.dma_start(w_up0[:], a["w_up0"]).then_inc(ld["e0"], 16)
            sp.dma_start(w_dn0[:], a["w_dn0"]).then_inc(ld["e0"], 16)
            sp.dma_start(w_a1[:], a["w_a1"]).then_inc(ld["a1"], 16)
            sp.dma_start(w_u1[:], a["w_u1"]).then_inc(ld["a1"], 16)
            sp.dma_start(rope1[:], a["rope1"]).then_inc(ld["a1"], 16)
            sp.dma_start(w_g1[:], a["w_g1"]).then_inc(ld["e1"], 16)
            sp.dma_start(w_sh[:], a["w_sh"]).then_inc(ld["e1"], 16)
            sp.dma_start(eb[:], a["eb"].partition_broadcast(P)).then_inc(ld["e1"], 16)

            def spread(L, which, dst, width, part_of):
                key, s = f"{which}{L}", f"{L}_{which}"
                sp.wait_ge(S[f"{s}_parts"], 1)
                sp.dma_start(scr[key], qparts[:, :, 0:width]).then_inc(S[f"{s}_scr"], 16)
                sp.wait_ge(S[f"{s}_scr"], 16)
                for c in range(PARTS * PARTS):
                    sp.dma_start(dst[DH * c:DH * c + DH, :, :],
                                 scr[key][:, part_of(c), :].rearrange("(h d) t -> d h t", d=DH)
                                 ).then_inc(S[f"{s}_stack"], 16)

            def spread_max(L):
                for b in range(B):
                    sp.wait_ge(S[f"{L}_nm_done"], b + 1)
                    for i in range(PARTS):
                        sp.dma_start(qs[STACK + i:STACK + i + 1, :, b * T:(b + 1) * T],
                                     nmp[:, b, i, :]).then_inc(S[f"{L}_nm_stack{b}"], 16)

            sp.wait_ge(S["y0_ps"], 1)
            sp.dma_start(mq8, a["mq8"]).then_inc(ld["mask"], 16)
            sp.dma_start(mk8, a["mk8"]).then_inc(ld["mask"], 16)
            sp.dma_start(cxT, a["cxT"]).then_inc(ld["cxT"], 16)
            sp.dma_start(w_up1, a["w_up1"]).then_inc(ld["e1"], 16)
            sp.dma_start(w_dn1, a["w_dn1"]).then_inc(ld["e1"], 16)
            sp.wait_ge(S["ones"], 3)
            spread("a", "q", qs[0:STACK, :, :], N, lambda c: c // PARTS)
            spread("a", "k", ks["a"][0:STACK, :, :], N, lambda c: c % PARTS)
            spread_max("a")
            spread("x", "k", ks["x"][0:STACK, :, :], B * CS, lambda c: c % PARTS)
            sp.wait_ge(S["a_s_ps"], B * (H // 4) * (T // P))
            spread("x", "q", qs[0:STACK, :, :], N, lambda c: c // PARTS)
            spread_max("x")
            sp.wait_ge(S["x_s_ps"], B * (H // 4) * (CS // P))
            sp.dma_start(sel_e, a["sel_e"]).then_inc(ld["e1"], 16)
            sp.wait_ge(norm_out, len(NORMS))
            sp.dma_start(out, normed[:]).then_inc(S["stored"], 16)
            sp.wait_ge(S["stored"], 16)

        @block.gpsimd
        def _(pool):
            link = own(pool, pool_own)
            nc.gpsimd.memset(neghalf[:], -0.5).then_inc(consts, 1)
            nc.gpsimd.memset(x1p[:], 0.0).then_inc(consts, 1)
            nc.gpsimd.memset(sc0[:], -FAR).then_inc(consts, 1)
            nc.gpsimd.memset(pick0[:], -FAR).then_inc(consts, 1)
            nc.gpsimd.memset(r1[:], -FAR).then_inc(consts, 1)
            nc.gpsimd.memset(t1[:], -FAR).then_inc(consts, 1)
            pool.wait_ge(consts, 6)

            def root(name):
                k = NORMS.index(name)
                nt = NC_TILES if name == "ctx" else NJ
                pool.wait_ge(norm_var, k + 1)
                link(nc.gpsimd.tensor_scalar(vareps[:, 0:nt], meanvar[:, k, 0:nt, 1], EPS, None,
                                             ALU.add))
                nc.gpsimd.tensor_tensor(rstd[:, k, 0:nt], vareps[:, 0:nt], neghalf[:, 0:nt],
                                        ALU.pow).then_inc(norm_rstd, 1)
                pool.wait_ge(norm_rstd, k + 1)


            root("ln1")
            root("ln")
            root("ctx")
            pool.wait_ge(ld["x"], 16)
            pool.wait_ge(ld["rowv"], 16)
            nc.gpsimd.tensor_tensor(resid[:], x[:], rv4("w2_b"), ALU.add).then_inc(S["res_ready"], 1)
            for s in range(NG):
                pool.wait_ge(S["scan_done"], s + 1)
                if s == 0:
                    pool.wait_ge(S["BC_done"], 2)
                if s >= 8:
                    pool.wait_ge(S["y_ps"], (s - 8) // 4 + 1)
                nc.gpsimd.tensor_tensor(hC[:, s % 8, :], hs[:, s % 4, :], Cn[:],
                                        ALU.mult).then_inc(S["hC_done"], 1)
            root("ln2")
            pool.wait_ge(S["x2_done"], 1)
            link(nc.gpsimd.tensor_tensor(resid[:], x[:], rv4("ff2_b"), ALU.add))
            nc.gpsimd.tensor_tensor(resid[:], resid[:], x2[:], ALU.add).then_inc(S["res_ready"], 1)
            pool.wait_ge(S["mo_ps"], 1)
            nc.gpsimd.memset(v0, 1.0).then_inc(S["ones"], 1)
            root("post0")
            link(nc.gpsimd.memset(sel1, -FAR))
            root("lat")
            pool.wait_ge(norm_out, NORMS.index("post0") + 1)
            nc.gpsimd.tensor_tensor(resid[:], x[:], rv4("bo0"), ALU.add).then_inc(S["res_ready"], 1)
            for c in range(NPAIR):
                for b in range(B):
                    n = B * c + b
                    pool.wait_ge(S["k0_mul"], 2 * n + 2)
                    if c >= 2:
                        pool.wait_ge(S["s0_ps"], 4 * (c - 1))
                    nc.gpsimd.tensor_tensor(kT0[:, c % 2, b * CS:(b + 1) * CS], kt1[:, n % 2, :],
                                            kt2[:, n % 2, :], ALU.add).then_inc(S["k0_done"], 1)
            root("post1")
            pool.wait_ge(S["y0_ps"], 1)
            nc.gpsimd.memset(ks_words["a"][64:STACK + PARTS, :], ONES2).then_inc(S["ones"], 1)
            pool.wait_ge(S["ones"], 2)
            pool.wait_ge(S["dn0_ps"], E0)
            nc.gpsimd.memset(ks_words["x"][64:STACK + PARTS, :], ONES2).then_inc(S["ones"], 1)
            pool.wait_ge(S["ones"], 3)
            link(nc.gpsimd.memset(v1, 0.0))
            nc.gpsimd.memset(v1[:, :, :, DH:2 * DH], 1.0).then_inc(S["ones"], 1)
            root("post2")
            pool.wait_ge(norm_out, NORMS.index("post2") + 1)
            nc.gpsimd.tensor_tensor(resid[:], x[:], rv4("Wo_b"), ALU.add).then_inc(S["res_ready"], 1)
            root("post3")
            pool.wait_ge(norm_out, NORMS.index("post3") + 1)
            nc.gpsimd.tensor_tensor(resid[:], x[:], rv4("bo1"), ALU.add).then_inc(S["res_ready"], 1)
            root("post4")
            for c in range(C1):
                pool.wait_ge(S["cb_mul"], c + 1)
                nc.gpsimd.tensor_tensor(hh[:, c, :], rlc[:, c % 3, :], rl[:, c % 3, :],
                                        ALU.mult).then_inc(S["h1_done"], 1)
            root("post5")

        @block.scalar
        def _(act):
            link = own(act, act_own)

            def to_cols(dst, bank, ready, done, scale=None, bias=None, n=1):
                act.wait_ge(S[ready], n)
                if scale is None:
                    nc.scalar.activation(dst, ps[:, bank, :], ACT.Copy).then_inc(S[done], 1)
                else:
                    nc.scalar.activation(dst, ps[:, bank, :], ACT.Identity, scale=scale,
                                         bias=bias).then_inc(S[done], 1)

            act.wait_ge(ld["vec"], 16)
            to_cols(xT[:], 0, "xmT_ps", "xmT", v("ln_g"), v("ln_b"))
            act.wait_ge(S["w1_ps"], 1)
            act.wait_ge(consts, 6)
            nc.scalar.activation(x1p[:, :, 1:T + 1], ps[:, 1, :].rearrange("p (b t) -> p b t", b=B),
                                 ACT.Identity, bias=v("w1_b")).then_inc(S["x1p_done"], 1)
            act.wait_ge(S["v1_ps"], 1)
            nc.scalar.activation(gate[:], ps[:, 2, :], ACT.Silu, bias=v("v1_b")
                                 ).then_inc(S["gate_done"], 1)
            act.wait_ge(S["conv_done"], 1)
            nc.scalar.activation(xc[:], cv[:, 0, :], ACT.Silu).then_inc(S["xc_done"], 1)
            link(nc.scalar.activation(nA[:, 0, :], vec[:, VEC["A_log"][0]:VEC["A_log"][0] + NG],
                                      ACT.Exp))
            nc.scalar.mul(nA[:, 1, :], nA[:, 0, :], -1.0).then_inc(S["negA"], 1)
            act.wait_ge(S["z_done"], 1)
            link(nc.scalar.activation(dtmp[:, 0, :], cv[:, 1, :], ACT.Abs))
            link(nc.scalar.activation(dtmp[:, 1, :], dtmp[:, 0, :], ACT.Exp, scale=-1.0))
            nc.scalar.activation(dtmp[:, 2, :], dtmp[:, 1, :], ACT.Ln, bias=1.0
                                 ).then_inc(S["lg_done"], 1)
            act.wait_ge(S["BC_ps"], 1)
            nc.scalar.activation(Bn[:], ps[:, 4, :], ACT.Identity, bias=v("Bp_b")
                                 ).then_inc(S["BC_done"], 1)
            nc.scalar.activation(Cn[:], ps[:, 5, :], ACT.Identity, bias=v("Cp_b")
                                 ).then_inc(S["BC_done"], 1)
            act.wait_ge(S["negA"], 1)
            for s, g in enumerate(ORDER):
                act.wait_ge(S["spread_d"], s + 1)
                if s >= 2:
                    act.wait_ge(S["scan_done"], s - 1)
                nc.scalar.activation(dA[:, s % 2, :], ps[:, s % 2, :], ACT.Exp,
                                     scale=nA[:, 1, g:g + 1]).then_inc(S["dA_done"], 1)
            to_cols(xT[:], 0, "hT_ps", "hT", v("ln2_g"), v("ln2_b"))
            for c in range(FF):
                act.wait_ge(S["ff_ps"], c + 1)
                nc.scalar.activation(ffh[:, c, :], ps[:, 1 + c, :], ACT.Gelu, bias=v("ff1_b", c)
                                     ).then_inc(S["ff_act"], 1)
            for i in range(2):
                to_cols(cxnT[:, i * 512:(i + 1) * 512], 6 + i, "cxnT_ps", "cxnT_done",
                        v("ctx_g"), v("ctx_b"), i + 1)
            to_cols(xT[:], 0, "latT_ps", "latT", v("lat_g"), v("lat_b"))

            def evac0(c, kind):
                if kind == "q":
                    act.wait_ge(S["q0_ps"], c + 1)
                    if c >= 2:
                        act.wait_ge(S["s0_ps"], 4 * (c - 1))
                    nc.scalar.activation(qT0[:, c % 2, :], ps[:, 6, :], ACT.Copy,
                                         scale=DH0 ** -0.5).then_inc(S["q0_done"], 1)
                elif kind in ("v0", "v1"):
                    i = int(kind[1])
                    act.wait_ge(S["v0_ps"], 2 * c + i + 1)
                    if c >= 2:
                        act.wait_ge(S["e0_used"], 4 * (c - 1))
                    nc.scalar.activation(
                        v0[:, c % 2, 4 * i:4 * i + 4, :, 0:DH0],
                        ps[:, 7 - i, :].rearrange("p (k r d) -> p k r d", k=4, r=2), ACT.Copy
                    ).then_inc(S["v0_done"], 1)
                elif kind == "t":
                    act.wait_ge(S["o0T_ps"], c + 1)
                    nc.scalar.activation(aoT[:, c, :], ps[:, 7, :], ACT.Copy).then_inc(S["o0T_done"], 1)

            act.wait_ge(S["ones"], 1)
            for kind in ("q", "v0", "v1"):
                evac0(0, kind)
            for c in range(NPAIR):
                for u in range(4):
                    n = 4 * c + u
                    act.wait_ge(S["s0_ps"], n + 1)
                    if n >= 3:
                        act.wait_ge(S["e0_used"], n - 2)
                    nc.scalar.activation(ex[:, n % 3, :].rearrange("p (r n) -> p r n", r=2),
                                         ps[:, 2 * (n % 2):2 * (n % 2) + 2, :], ACT.Exp
                                         ).then_inc(S["e0_exp"], 1)
                    if c < NPAIR - 1:
                        for kind in ((), ("q",), ("v0",), ("v1",))[u]:
                            evac0(c + 1, kind)
                    if c and u == 0:
                        evac0(c - 1, "t")
            evac0(NPAIR - 1, "t")
            to_cols(xT[:], 0, "xT_ps", "xT_done")
            act.wait_ge(S["r0_max"], 1)
            nc.scalar.activation(g0[:, 1], g0[:, 0], ACT.Exp).then_inc(S["r0_exp"], 1)
            for e in range(E0):
                for c in range(F0):
                    n = F0 * e + c
                    act.wait_ge(S["up0_ps"], n + 1)
                    if e >= 2:
                        act.wait_ge(S["dn0_ps"], e - 1)
                    nc.scalar.activation(eh0[:, e % 2, c, :], ps[:, n % 3, :], ACT.Gelu
                                         ).then_inc(S["up0_act"], 1)
            to_cols(xT[:], 0, "xT_ps", "xT_done", n=2)
            for i, name in enumerate(("Wd_q_b", "Wd_kv_b")):
                act.wait_ge(S["cdown_ps"], i + 1)
                nc.scalar.activation(cq[:, i, :], ps[0:64, 1 + i, :], ACT.Identity,
                                     bias=v(name, rows=64)).then_inc(S["cdown_done"], 1)

            def attend(L):
                nk = KEYS[L] // P
                scale = 1.0 / float(np.sqrt(np.float32(H + 64 + 64))) if L == "a" else 1.0
                for n in range(B * (H // 4) * nk):
                    act.wait_ge(S[f"{L}_s_ps"], n + 1)
                    if n >= 3:
                        act.wait_ge(S[f"{L}_e_used"], n - 2)
                    nc.scalar.activation(ex1[:, n % 3, :].rearrange("p (r n) -> p r n", r=2),
                                         ps[:, 2 * (n % 2):2 * (n % 2) + 2, :], ACT.Exp, scale=scale
                                         ).then_inc(S[f"{L}_e_exp"], 1)
                act.wait_ge(S[f"{L}_aT_ps"], 1)
                nc.scalar.activation(aoT1[:], ps[:, 6, :], ACT.Copy).then_inc(S[f"{L}_aT_done"], 1)

            attend("a")
            to_cols(xT[:], 0, "xT_ps", "xT_done", n=3)
            attend("x")
            to_cols(xT[:], 0, "xT_ps", "xT_done", n=4)
            act.wait_ge(S["g1_ps"], 1)
            nc.scalar.activation(lg1[:, 0], ps[:, 1, 0:NJ * E1].rearrange("p (j e) -> p j e", j=NJ),
                                 ACT.Exp, scale=-1.0).then_inc(S["g1_exp"], 1)
            for c in range(SH):
                act.wait_ge(S["shu_ps"], c + 1)
                nc.scalar.activation(rl[:, c, :], ps[:, 2 + c, :], ACT.Relu).then_inc(S["shr_done"], 1)
            act.wait_ge(S["sh_done"], SH)
            for c in range(C1):
                act.wait_ge(S["up1_ps"], c + 1)
                if c >= 3:
                    act.wait_ge(S["h1_done"], c - 2)
                nc.scalar.activation(rl[:, c % 3, :], ps[:, 2 + c % 2, :], ACT.Relu
                                     ).then_inc(S["relu_done"], 1)

        @block.vector
        def _(dve):
            link = own(dve, dve_own)

            def layernorm(name, src, dst):
                k = NORMS.index(name)
                nt = src.shape[1]
                for j in range(nt):
                    ins = nc.vector.bn_stats(stats[:, j, :], src[:, j, :])
                link(ins)
                for j in range(nt):
                    ins = nc.vector.bn_aggr(meanvar[:, k, j, :], stats[:, j, :])
                ins.then_inc(norm_var, 1)
                dve.wait_ge(norm_var, k + 1)
                dve.wait_ge(norm_rstd, k + 1)
                for j in range(nt):
                    ins = nc.vector.tensor_scalar(dst[:, j, :], src[:, j, :], meanvar[:, k, j, 0:1],
                                                  rstd[:, k, j:j + 1], ALU.subtract, ALU.mult)
                ins.then_inc(norm_out, 1)
                dve.wait_ge(norm_out, k + 1)

            def split(src, parts, rest, done):
                link(nc.vector.tensor_copy(parts[0], src))
                link(nc.vector.tensor_tensor(rest, src, parts[0], ALU.subtract))
                link(nc.vector.tensor_copy(parts[1], rest))
                nc.vector.tensor_tensor(parts[2], rest, parts[1], ALU.subtract).then_inc(done, 1)

            dve.wait_ge(ld["x"], 16)
            layernorm("ln1", x[:], normed)
            dve.wait_ge(ld["rowv"], 16)
            link(nc.vector.tensor_tensor(normed[:], normed[:], rv4("ln1_g"), ALU.mult))
            link(nc.vector.tensor_tensor(summed[:], normed[:], rv4("ln1_b"), ALU.add))
            layernorm("ln", summed[:], normed)
            dve.wait_ge(ld["cx"], 16)
            layernorm("ctx", cx, cx)
            dve.wait_ge(ld["vec"], 16)
            dve.wait_ge(S["x1p_done"], 1)
            cv3 = cv[:, :, :].rearrange("p i (b t) -> p i b t", b=B)
            link(nc.vector.tensor_scalar(cv3[:, 0], x1p[:, :, 0:T], v("conv", 0), None, ALU.mult))
            link(nc.vector.scalar_tensor_tensor(cv3[:, 1], x1p[:, :, 1:T + 1], v("conv", 1),
                                                cv3[:, 0], ALU.mult, ALU.add))
            nc.vector.scalar_tensor_tensor(cv3[:, 0], x1p[:, :, 2:T + 2], v("conv", 2), cv3[:, 1],
                                           ALU.mult, ALU.add).then_inc(S["conv_done"], 1)
            dve.wait_ge(S["dt_ps"], 1)
            nc.vector.tensor_scalar(cv[:, 1, :], ps[:, 3, :], v("dt_b"), None, ALU.add
                                    ).then_inc(S["z_done"], 1)
            dve.wait_ge(S["z_done"], 1)
            dve.wait_ge(S["lg_done"], 1)
            link(nc.vector.scalar_tensor_tensor(dl[:, 0, :], cv[:, 1, :], 0.0, dtmp[:, 2, :],
                                                ALU.max, ALU.add))
            split(dl[:, 0, :], [dparts[:, 0, i, :] for i in range(3)], dtmp[:, 0, :],
                  S["delta_parts"])
            dve.wait_ge(S["xc_done"], 1)
            link(nc.vector.tensor_tensor(dl[:, 1, :], dl[:, 0, :], xc[:], ALU.mult))
            split(dl[:, 1, :], [dparts[:, 1, i, :] for i in range(3)], dtmp[:, 1, :], S["dx_parts"])
            dve.wait_ge(S["BC_done"], 1)
            for s in range(NG):
                dve.wait_ge(S["spread_x"], s + 1)
                if s >= 2:
                    dve.wait_ge(S["scan_done"], s - 1)
                nc.vector.tensor_tensor(dBx[:, s % 2, :], ps[:, 2 + s % 2, :], Bn[:],
                                        ALU.mult).then_inc(S["dBx_done"], 1)
                dve.wait_ge(S["dBx_done"], s + 1)
                dve.wait_ge(S["dA_done"], s + 1)
                if s >= 4:
                    dve.wait_ge(S["hC_done"], s - 3)
                for b in range(B):
                    t = slice(b * T, (b + 1) * T)
                    ins = nc.vector.tensor_tensor_scan(hs[:, s % 4, t], dA[:, s % 2, t],
                                                       dBx[:, s % 2, t], 0.0, ALU.mult, ALU.add)
                ins.then_inc(S["scan_done"], 1)
            dve.wait_ge(S["y_ps"], NG // 4)
            link(nc.vector.scalar_tensor_tensor(cv[:, 0, :], xc[:], v("D_p"), ps[:, 4, :],
                                                ALU.mult, ALU.add))
            dve.wait_ge(S["gate_done"], 1)
            nc.vector.tensor_tensor(cv[:, 1, :], cv[:, 0, :], gate[:], ALU.mult
                                    ).then_inc(S["yv_done"], 1)
            dve.wait_ge(S["mo_ps"], 1)
            dve.wait_ge(S["res_ready"], 1)
            flat = lambda t: t[:, :, :].rearrange("p j d -> p (j d)")
            nc.vector.tensor_tensor(flat(x2), ps[:, 5, :], flat(resid), ALU.add
                                    ).then_inc(S["x2_done"], 1)
            dve.wait_ge(S["x2_done"], 1)
            layernorm("ln2", x2[:], normed)

            def add_and_norm(bank, ready, n, res, name):
                dve.wait_ge(S[ready], n)
                dve.wait_ge(S["res_ready"], res)
                link(nc.vector.tensor_tensor(flat(summed), ps[:, bank, :], flat(resid), ALU.add))
                layernorm(name, summed[:], x)

            add_and_norm(6, "ff2_ps", 1, 2, "post0")
            layernorm("lat", x[:], normed)

            dve.wait_ge(ld["rope0"], 16)
            nc.vector.tensor_scalar(rope0[:, 1, :], rope0[:, 1, :], v("rope_sign"), None,
                                    ALU.mult).then_inc(S["rope_signed"], 1)
            dve.wait_ge(S["rope_signed"], 1)

            def rotary(c, b):
                n = B * c + b
                for i, dst in enumerate((kt1, kt2)):
                    dve.wait_ge(S["k0_ps"], 2 * n + i + 1)
                    if n >= 2:
                        dve.wait_ge(S["k0_done"], n - 1)
                    nc.vector.tensor_tensor(dst[:, n % 2, :], ps[:, 6 + i, :], rope0[:, i, :],
                                            ALU.mult).then_inc(S["k0_mul"], 1)

            for b in range(B):
                rotary(0, b)
            for c in range(NPAIR):
                for u in range(4):
                    n = 4 * c + u
                    dve.wait_ge(S["e0_exp"], n + 1)
                    nc.vector.tensor_scalar(ex[:, n % 3, :], ex[:, n % 3, :], float(np.exp(CLIP)),
                                            float(np.exp(-CLIP)), ALU.min, ALU.max
                                            ).then_inc(S["e0_clip"], 1)
                    if u < 2 and c < NPAIR - 1:
                        rotary(c + 1, u)
                    if u % 2:
                        b = u // 2
                        dve.wait_ge(S["e0_used"], 4 * c + 2 * b + 2)
                        o = ps[:, 4 + b, 0:4 * (DH0 + 1)].rearrange("p (q r d) -> p q r d", q=2, r=2)
                        rd = rden[:, 2 * b:2 * b + 2, 2 * c:2 * c + 2]
                        link(nc.vector.reciprocal(rd, o[:, :, :, DH0]))
                        for q in range(2):
                            ins = nc.vector.tensor_tensor(
                                ao[:, 2 * b + q, c * P:(c + 1) * P].rearrange("p (r d) -> p r d", r=2),
                                o[:, q, :, 0:DH0],
                                rden[:, 2 * b + q, 2 * c:2 * c + 2].rearrange("p (r o) -> p r o", o=1)
                                .broadcast_to([P, 2, DH0]), ALU.mult)
                        ins.then_inc(S["o0_norm"], 1)
            add_and_norm(4, "y0_ps", 1, 3, "post1")

            dve.wait_ge(S["r0_ps"], 1)
            dve.wait_ge(consts, 6)
            link(nc.vector.tensor_copy(sc0[:, :, 0:E0], ps[:, 4, 0:NJ * E0].rearrange(
                "p (j e) -> p j e", j=NJ)))
            for j in range(NJ):
                ins = nc.vector.max(top0[:, j, :], sc0[:, j, 0:E0])
            link(ins)
            link(nc.vector.tensor_copy(pick0[:, :, 0:2], top0[:, :, 0:2]))
            for j in range(NJ):
                ins = nc.vector.match_replace(out=mark0[:, j, :], in_to_replace=pick0[:, j, :],
                                              in_values=sc0[:, j, :], imm_value=FAR)
            nc.vector.tensor_tensor(g0[:, 0], sc0[:, :, 0:E0],
                                    top0[:, :, 0:1].broadcast_to([P, NJ, E0]), ALU.subtract
                                    ).then_inc(S["r0_max"], 1)
            dve.wait_ge(S["r0_exp"], 1)
            dve.wait_ge(S["r0_max"], 1)
            link(nc.vector.scalar_tensor_tensor(g0[:, 2], mark0[:, :, 0:E0], 0.5 * FAR, g0[:, 1],
                                                ALU.is_ge, ALU.mult))
            link(nc.vector.tensor_reduce(den0[:, 0, :], g0[:, 2], AX.X, ALU.add))
            link(nc.vector.reciprocal(den0[:, 1, :], den0[:, 0, :]))
            link(nc.vector.tensor_tensor(
                g0[:, 3], g0[:, 2],
                den0[:, 1, :].rearrange("p (j o) -> p j o", o=1).broadcast_to([P, NJ, E0]), ALU.mult))
            for e in range(E0):
                dve.wait_ge(S["dn0_ps"], e + 1)
                if e:
                    dve.wait_ge(S["dn0_acc"], e)
                for j in range(NJ):
                    ins = nc.vector.scalar_tensor_tensor(
                        summed[:, j, :], ps[:, 5 + e % 2, j * D:(j + 1) * D], g0[:, 3, j, e:e + 1],
                        summed[:, j, :] if e else x[:, j, :], ALU.mult, ALU.add)
                ins.then_inc(S["dn0_acc"], 1)
            dve.wait_ge(S["dn0_acc"], E0)
            layernorm("post2", summed[:], x)

            def rotated(i, biases, dst, done):
                dve.wait_ge(S["qa_ps"], i + 1)
                cos = rope1[:, 0:1, :].broadcast_to([P, B, T])
                sin = rope1[:, 1:2, :].broadcast_to([P, B, T])
                by_b = lambda t: t.rearrange("p (b t) -> p b t", b=B)
                nc.vector.scalar_tensor_tensor(by_b(dtmp[:, 0, :]), by_b(ps[:, 4, :]), v(biases[1]),
                                               cos, ALU.add, ALU.mult)
                link(nc.vector.scalar_tensor_tensor(by_b(dtmp[:, 1, :]), by_b(ps[:, 5, :]),
                                                    v(biases[2]), sin, ALU.add, ALU.mult))
                link(nc.vector.scalar_tensor_tensor(dtmp[:, 2, :], ps[:, 3, :], v(biases[0]),
                                                    dtmp[:, 0, :], ALU.add, ALU.add))
                nc.vector.tensor_tensor(dst, dtmp[:, 2, :], dtmp[:, 1, :], ALU.add).then_inc(done, 1)
                dve.wait_ge(done, i + 1)

            dve.wait_ge(ld["a1"], 48)
            rotated(0, ("Wu_q_b", "Wq_r_b", "Wq_s_b"), qf[:, 0, :], S["qa_done"])
            split(qf[:, 0, :], [qparts[:, i, 0:N] for i in range(3)], cv[:, 0, :], S["a_q_parts"])
            rotated(1, ("Wu_k_b", "Wk_r_b", "Wk_s_b"), qf[:, 1, :], S["qa_done"])
            dve.wait_ge(S["a_q_scr"], 16)
            split(qf[:, 1, :], [qparts[:, i, 0:N] for i in range(3)], cv[:, 1, :], S["a_k_parts"])
            dve.wait_ge(S["va_ps"], 1)
            dve.wait_ge(S["ones"], 4)
            nc.vector.tensor_tensor(
                v1[:, 0:NJ, :, 0:DH], ps[:, 6, :].rearrange("p (j h d) -> p j h d", j=NJ, h=H),
                rv4("Wu_v_b").rearrange("p j (h d) -> p j h d", h=H), ALU.add
            ).then_inc(S["va_done"], 1)

            def maxima(L):
                heads = 512 // KEYS[L]
                n = 0
                for b in range(B):
                    for q in range(2):
                        for h in range(0, H, heads):
                            dve.wait_ge(S[f"{L}_smax_ps"], n + 1)
                            nc.vector.tensor_reduce(
                                mx[L][:, 2 * b + q, h:h + heads],
                                ps[:, n % 4, :].rearrange("p (h k) -> p h k", h=heads), AX.X, ALU.max
                            ).then_inc(S[f"{L}_redmax"], 1)
                            n += 1
                    dve.wait_ge(S[f"{L}_mT_ps"], b + 1)
                    link(nc.vector.tensor_scalar(nm[:, b, 0, :], ps[0:H, 4 + b, 0:T], -1.0, None,
                                                 ALU.mult))
                    split(nm[:, b, 0, :], [nmp[:, b, i, :] for i in range(3)],
                          nm[:, b, 1, :], S[f"{L}_nm_done"])

            def collect(L, factor):
                for i in range(B * (H // 4)):
                    b, g = divmod(i, H // 4)
                    dve.wait_ge(S[f"{L}_e_used"], (KEYS[L] // P) * (i + 1))
                    nc.vector.tensor_copy(og[:, g, b * T:(b + 1) * T], ps[:, 4 + i % 2, 0:T]
                                          ).then_inc(S[f"{L}_o_sb"], 1)
                for g in range(H // 4):
                    dve.wait_ge(S[f"{L}_oT_ps"], g + 1)
                    t = ps[:, 6 + g % 2, :].rearrange("p (j h r) -> p j h r", j=NJ, h=4)
                    rd = rden[:, :, 4 * g:4 * g + 4]
                    link(nc.vector.reciprocal(rd, t[:, :, :, DH]))
                    if factor != 1.0:
                        link(nc.vector.tensor_scalar(rd, rd, factor, None, ALU.mult))
                    for j in range(NJ):
                        ins = nc.vector.tensor_tensor(
                            ao1[:, j, 4 * g:4 * g + 4, :], t[:, j, :, 0:DH],
                            rden[:, j, 4 * g:4 * g + 4].rearrange("p (h o) -> p h o", o=1)
                            .broadcast_to([P, 4, DH]), ALU.mult)
                    ins.then_inc(S[f"{L}_o_norm"], 1)

            maxima("a")
            collect("a", 1.0)
            for i in range(2):
                dve.wait_ge(S["kx_ps"], i + 1)
                nc.vector.tensor_scalar(kxf[:, i * 512:(i + 1) * 512], ps[:, 1 + i, :], v("bk"), None,
                                        ALU.add).then_inc(S["kx_done"], 1)
            dve.wait_ge(S["kx_done"], 2)
            dve.wait_ge(S["a_k_scr"], 16)
            split(kxf, [qparts[:, i, :] for i in range(3)], kxr, S["x_k_parts"])
            for i in range(2):
                dve.wait_ge(S["vx_ps"], i + 1)
                nc.vector.tensor_tensor(
                    v1[:, 4 * i:4 * i + 4, :, 0:DH],
                    ps[:, 3 - i, :].rearrange("p (j h d) -> p j h d", j=4, h=H),
                    rv4("bv").rearrange("p j (h d) -> p j h d", h=H), ALU.add
                ).then_inc(S["vx_done"], 1)
            dve.wait_ge(ld["mask"], 48)
            nc.vector.tensor_copy(mq[:], mq8[:]).then_inc(S["mask_done"], 1)
            nc.vector.tensor_copy(mk[:], mk8[:]).then_inc(S["mask_done"], 1)
            add_and_norm(7, "a_y_ps", 1, 4, "post3")

            dve.wait_ge(S["qx_ps"], 1)
            nc.vector.tensor_scalar(qf[:, 0, :], ps[:, 4, :], v("bq"), None, ALU.add
                                    ).then_inc(S["qx_done"], 1)
            dve.wait_ge(S["qx_done"], 1)
            dve.wait_ge(S["x_k_scr"], 16)
            split(qf[:, 0, :], [qparts[:, i, 0:N] for i in range(3)], cv[:, 0, :], S["x_q_parts"])
            maxima("x")
            collect("x", 1.0 / float(np.sqrt(np.float32(DH))))
            add_and_norm(7, "x_y_ps", 1, 5, "post4")

            dve.wait_ge(S["g1_exp"], 1)
            link(nc.vector.tensor_scalar(lg1[:, 1], lg1[:, 0], 1.0, None, ALU.add))
            link(nc.vector.reciprocal(lg1[:, 2], lg1[:, 1]))
            dve.wait_ge(ld["e1"], 16 * 6)
            link(nc.vector.tensor_tensor(lg1[:, 3], lg1[:, 2],
                                         eb[:, :].rearrange("p (o e) -> p o e", o=1)
                                         .broadcast_to([P, NJ, E1]), ALU.add))
            sc = lg1[:, 3].rearrange("p j (g i) -> p j g i", i=4)
            best, other = pr1[:, 0], pr1[:, 1]
            link(nc.vector.tensor_tensor(best, sc[:, :, :, 0], sc[:, :, :, 1], ALU.add))
            for i, k in ((0, 2), (0, 3), (1, 2), (1, 3), (2, 3)):
                link(nc.vector.tensor_tensor(other, sc[:, :, :, i], sc[:, :, :, k], ALU.add))
                link(nc.vector.tensor_tensor(best, best, other, ALU.max))
            dve.wait_ge(consts, 6)
            link(nc.vector.tensor_copy(r1[:, 0, :, 0:8], best))
            for j in range(NJ):
                ins = nc.vector.max(t1[:, 0, j, :], best[:, j, :])
            link(ins)
            link(nc.vector.tensor_copy(t1[:, 1, :, 0:4], t1[:, 0, :, 0:4]))
            for j in range(NJ):
                ins = nc.vector.match_replace(out=r1[:, 1, j, :], in_to_replace=t1[:, 1, j, :],
                                              in_values=r1[:, 0, j, :], imm_value=FAR)
            link(ins)
            link(nc.vector.tensor_scalar(best, r1[:, 1, :, 0:8], 0.5 * FAR, None, ALU.is_ge))
            for j in range(NJ):
                ins = nc.vector.tensor_tensor(
                    sel1[:, 0, j, 0:E1].rearrange("p (g i) -> p g i", i=4), sc[:, j],
                    best[:, j, :].rearrange("p (g o) -> p g o", o=1).broadcast_to([P, 8, 4]),
                    ALU.mult)
            link(ins)
            for j in range(NJ):
                ins = nc.vector.max(t1[:, 2, j, :], sel1[:, 0, j, 0:E1])
            link(ins)
            link(nc.vector.tensor_copy(t1[:, 3, :, 0:6], t1[:, 2, :, 0:6]))
            for j in range(NJ):
                ins = nc.vector.match_replace(out=sel1[:, 1, j, :], in_to_replace=t1[:, 3, j, :],
                                              in_values=sel1[:, 0, j, :], imm_value=FAR)
            link(ins)
            link(nc.vector.scalar_tensor_tensor(lg1[:, 0], sel1[:, 1, :, 0:E1], 0.5 * FAR, lg1[:, 2],
                                                ALU.is_ge, ALU.mult))
            link(nc.vector.tensor_reduce(den0[:, 0, :], lg1[:, 0], AX.X, ALU.add))
            link(nc.vector.tensor_scalar(den0[:, 0, :], den0[:, 0, :], 1e-20, None, ALU.add))
            link(nc.vector.reciprocal(den0[:, 1, :], den0[:, 0, :]))
            link(nc.vector.tensor_tensor(
                lg1[:, 1], lg1[:, 0],
                den0[:, 1, :].rearrange("p (j o) -> p j o", o=1).broadcast_to([P, NJ, E1]),
                ALU.mult))
            nc.vector.tensor_scalar(cmb[:], lg1[:, 1], 2.5, None, ALU.mult).then_inc(S["cmb_done"], 1)
            for c in range(SH):
                dve.wait_ge(S["shr_done"], c + 1)
                nc.vector.tensor_tensor(hsh[:, c, :], rl[:, c, :], rl[:, c, :], ALU.mult
                                        ).then_inc(S["sh_done"], 1)
            dve.wait_ge(S["cmbT_ps"], 1)
            link(nc.vector.tensor_copy(cmf[:, 0, :], ps[0:E1, 4, :]))
            link(nc.vector.tensor_copy(cmp_[:, 0, :], cmf[:, 0, :]))
            link(nc.vector.tensor_tensor(cmf[:, 1, :], cmf[:, 0, :], cmp_[:, 0, :], ALU.subtract))
            link(nc.vector.tensor_copy(cmp_[:, 1, :], cmf[:, 1, :]))
            link(nc.vector.tensor_tensor(cmp_[:, 2, :], cmf[:, 1, :], cmp_[:, 1, :], ALU.subtract))
            for i in range(PARTS):
                ins = nc.vector.tensor_copy(cms[E1 * i:E1 * (i + 1), :], cmp_[:, i, :])
            ins.then_inc(S["cms_done"], 1)
            for c in range(C1):
                dve.wait_ge(S["cb_ps"], c + 1)
                dve.wait_ge(S["relu_done"], c + 1)
                if c >= 3:
                    dve.wait_ge(S["h1_done"], c - 2)
                nc.vector.tensor_tensor(rlc[:, c % 3, :], ps[:, 5 + c % 2, :], rl[:, c % 3, :],
                                        ALU.mult).then_inc(S["cb_mul"], 1)
            dve.wait_ge(S["y1_ps"], 1)
            link(nc.vector.tensor_tensor(flat(summed), ps[:, 7, :], flat(x), ALU.add))
            layernorm("post5", summed[:], normed)

        @block.tensor
        def _(pe):
            def mm(o, lhsT, rhs, start=True, stop=True, shared=False):
                return nc.tensor.matmul(o, lhsT, rhs, start=start, stop=stop, skip_group_check=shared)

            def to_cols(bank, src, done):
                for j in range(NJ):
                    ins = nc.tensor.transpose(ps[:, bank, j * P:(j + 1) * P], src[:, j, :], ident[:])
                ins.then_inc(S[done], 1)

            def to_rows(bank, cols, w, done):
                for j in range(NJ):
                    for c, (lhs, rhs) in enumerate(zip(cols, w)):
                        ins = mm(ps[:, bank, j * D:(j + 1) * D], lhs[:, j * P:(j + 1) * P], rhs,
                                 c == 0, c == len(w) - 1)
                ins.then_inc(S[done], 1)

            pe.wait_ge(ld["ident"], 16)
            pe.wait_ge(norm_out, NORMS.index("ln") + 1)
            to_cols(0, normed, "xmT_ps")
            pe.wait_ge(ld["mix"], 16)
            pe.wait_ge(S["xmT"], 1)
            mm(ps[:, 1, :], w_mix[:, 0, :], xT[:]).then_inc(S["w1_ps"], 1)
            mm(ps[:, 2, :], w_mix[:, 1, :], xT[:]).then_inc(S["v1_ps"], 1)
            pe.wait_ge(norm_out, NORMS.index("ctx") + 1)
            for i in range(2):
                to_cols(6 + i, cx[:, 4 * i:4 * i + 4, :], "cxnT_ps")
            pe.wait_ge(S["xc_done"], 1)
            mm(ps[:, 3, :], w_mix[:, 2, :], xc[:]).then_inc(S["dt_ps"], 1)
            mm(ps[:, 4, :], w_mix[:, 3, :], xc[:])
            mm(ps[:, 5, :], w_mix[:, 4, :], xc[:]).then_inc(S["BC_ps"], 1)
            pe.wait_ge(ld["sel"], 32)
            pe.wait_ge(S["delta_parts"], 1)
            pe.wait_ge(S["gate_done"], 1)

            def y_of(s0):
                pe.wait_ge(S["hC_done"], s0 + 4)
                if s0 == 0:
                    pe.wait_ge(S["BC_done"], 2)
                for q in range(4):
                    ins = mm(ps[32 * q:32 * q + 32, 4, :], sel_y[:, s0 // 4, :],
                             hC[:, (s0 + q) % 8, :], s0 == 0, s0 == NG - 4)
                ins.then_inc(S["y_ps"], 1)

            for s, g in enumerate(ORDER):
                if s >= 2:
                    pe.wait_ge(S["dA_done"], s - 1)
                for i in range(PARTS):
                    ins = mm(ps[:, s % 2, :], sel_g[:, g, :], dparts[:, 0, i, :], i == 0,
                             i == PARTS - 1)
                ins.then_inc(S["spread_d"], 1)
                if s == 0:
                    pe.wait_ge(S["dx_parts"], 1)
                if s >= 2:
                    pe.wait_ge(S["dBx_done"], s - 1)
                for i in range(PARTS):
                    ins = mm(ps[:, 2 + s % 2, :], sel_g[:, g, :], dparts[:, 1, i, :], i == 0,
                             i == PARTS - 1)
                ins.then_inc(S["spread_x"], 1)
                if s % 4 == 1 and s > 4:
                    y_of(s - 5)
            y_of(NG - 4)
            pe.wait_ge(S["yv_done"], 1)
            to_rows(5, [cv[:, 1, :]], [w_mix[:, 5, :]], "mo_ps")
            pe.wait_ge(norm_out, NORMS.index("ln2") + 1)
            to_cols(0, normed, "hT_ps")
            pe.wait_ge(ld["ff"], 16)
            pe.wait_ge(S["hT"], 1)
            for c in range(FF):
                mm(ps[:, 1 + c, :], w_ff[:, c, :], xT[:]).then_inc(S["ff_ps"], 1)
            pe.wait_ge(S["ff_act"], FF)
            pe.wait_ge(S["cxnT_done"], 1)
            to_rows(6, [ffh[:, c, :] for c in range(FF)], [w_ff[:, FF + c, :] for c in range(FF)],
                    "ff2_ps")
            pe.wait_ge(norm_out, NORMS.index("lat") + 1)
            to_cols(0, normed, "latT_ps")
            pe.wait_ge(ld["x0"], 16)
            pe.wait_ge(S["latT"], 1)
            pe.wait_ge(S["cxnT_done"], 2)

            def project0(c, step):
                if step < 2:
                    n = B * c + step
                    for i in range(2):
                        if n:
                            pe.wait_ge(S["k0_mul"], 2 * (n - 1) + i + 1)
                        if step == 0 and c:
                            pe.wait_ge(S["v0_done"], 2 * c)
                            if c >= 2:
                                pe.wait_ge(S["o0T_done"], c - 1)
                        mm(ps[:, 6 + i, :], w_x0[:, c, i, :], cxnT[:, step * CS:(step + 1) * CS]
                           ).then_inc(S["k0_ps"], 1)
                elif step == 2:
                    pe.wait_ge(S["k0_mul"], 2 * (B * c + 1) + 2)
                    mm(ps[:, 6, :], w_x0[:, c, 3, :], xT[:]).then_inc(S["q0_ps"], 1)
                    for i in range(2):
                        if i == 1:
                            pe.wait_ge(S["q0_done"], c + 1)
                        for k in range(4):
                            t = 4 * i + k
                            ins = mm(ps[:, 7 - i, k * P:(k + 1) * P], cxnT[:, t * P:(t + 1) * P],
                                     w_x0[:, c, 2, :])
                        ins.then_inc(S["v0_ps"], 1)

            def logits0(n):
                c, u = divmod(n, 4)
                b, s = divmod(u, 2)
                if n >= 2:
                    pe.wait_ge(S["e0_exp"], n - 1)
                for r in range(2):
                    for k in range(2):
                        at = b * CS + (2 * s + k) * P
                        ins = mm(ps[:, 2 * (n % 2) + r, k * T:(k + 1) * T],
                                 kT0[64 * r:64 * r + 64, c % 2, at:at + P],
                                 qT0[64 * r:64 * r + 64, c % 2, b * T:(b + 1) * T])
                ins.then_inc(S["s0_ps"], 1)

            def mix0(n):
                c, u = divmod(n, 4)
                b, s = divmod(u, 2)
                pe.wait_ge(S["e0_clip"], n + 1)
                if s == 0 and c:
                    pe.wait_ge(S["o0_norm"], 2 * (c - 1) + b + 1)
                for q in range(2):
                    for r in range(2):
                        o = ps[:, 4 + b, (2 * q + r) * (DH0 + 1):(2 * q + r + 1) * (DH0 + 1)]
                        for k in range(2):
                            e = ex[:, n % 3, r * 512 + k * T + q * P:r * 512 + k * T + (q + 1) * P]
                            ins = mm(o, e, v0[:, c % 2, 4 * b + 2 * s + k, r, :],
                                     s == q == r == k == 0, s == q == r == k == 1, True)
                ins.then_inc(S["e0_used"], 1)

            for step in range(3):
                project0(0, step)
            pe.wait_ge(S["k0_done"], 2)
            pe.wait_ge(S["q0_done"], 1)
            logits0(0)
            for n in range(4 * NPAIR):
                c, u = divmod(n, 4)
                if n + 1 < 4 * NPAIR:
                    if u == 3:
                        pe.wait_ge(S["k0_done"], 2 * (c + 2))
                        pe.wait_ge(S["q0_done"], c + 2)
                    logits0(n + 1)
                if c + 1 < NPAIR and u < 3:
                    project0(c + 1, u)
                if u == 0:
                    pe.wait_ge(S["v0_done"], 2 * (c + 1))
                mix0(n)
                if u == 3:
                    pe.wait_ge(S["o0_norm"], 2 * (c + 1))
                    if c + 1 < NPAIR:
                        pe.wait_ge(S["v0_done"], 2 * (c + 2))
                    else:
                        pe.wait_ge(S["o0T_done"], c)
                    for j in range(NJ):
                        ins = nc.tensor.transpose(ps[:, 7, j * P:(j + 1) * P],
                                                  ao[:, j, c * P:(c + 1) * P], ident[:])
                    ins.then_inc(S["o0T_ps"], 1)
            pe.wait_ge(S["o0T_done"], NPAIR)
            to_rows(4, [aoT[:, c, :] for c in range(NPAIR)], [w_x0[:, c, 4, :] for c in range(NPAIR)],
                    "y0_ps")
            pe.wait_ge(norm_out, NORMS.index("post1") + 1)
            to_cols(0, x, "xT_ps")
            pe.wait_ge(ld["e0"], 48)
            pe.wait_ge(S["xT_done"], 1)
            for j in range(NJ):
                ins = mm(ps[:, 4, j * E0:(j + 1) * E0], xT[:, j * P:(j + 1) * P], w_r0[:])
            ins.then_inc(S["r0_ps"], 1)

            def up0(e):
                for c in range(F0):
                    n = F0 * e + c
                    if n >= 3:
                        pe.wait_ge(S["up0_act"], n - 2)
                    mm(ps[:, n % 3, :], w_up0[:, e, c * P:(c + 1) * P], xT[:]
                       ).then_inc(S["up0_ps"], 1)

            up0(0)
            for e in range(E0):
                if e + 1 < E0:
                    up0(e + 1)
                pe.wait_ge(S["up0_act"], F0 * (e + 1))
                if e >= 2:
                    pe.wait_ge(S["dn0_acc"], e - 1)
                to_rows(5 + e % 2, [eh0[:, e % 2, c, :] for c in range(F0)],
                        [w_dn0[:, e, c, :] for c in range(F0)], "dn0_ps")
            pe.wait_ge(norm_out, NORMS.index("post2") + 1)
            to_cols(0, x, "xT_ps")
            pe.wait_ge(ld["a1"], 48)
            pe.wait_ge(S["xT_done"], 2)
            for i in range(2):
                mm(ps[0:64, 1 + i, :], w_a1[:, 64 * i:64 * i + 64], xT[:]).then_inc(S["cdown_ps"], 1)
            pe.wait_ge(S["cdown_done"], 1)
            for i in range(3):
                ins = mm(ps[:, 3 + i, :], w_u1[:, i, :], cq[:, 0, :])
            ins.then_inc(S["qa_ps"], 1)
            pe.wait_ge(S["cdown_done"], 2)
            for j in range(NJ):
                ins = mm(ps[:, 6, j * D:(j + 1) * D], cq[:, 1, j * P:(j + 1) * P], w_u1[:, 4, :])
            ins.then_inc(S["va_ps"], 1)
            pe.wait_ge(S["qa_done"], 1)
            mm(ps[:, 3, :], w_u1[:, 3, :], cq[:, 1, :])
            mm(ps[:, 4, :], w_a1[:, 128:256], xT[:])
            mm(ps[:, 5, :], w_a1[:, 256:384], xT[:]).then_inc(S["qa_ps"], 1)

            def attend(L):
                heads, nk = 512 // KEYS[L], KEYS[L] // P
                n = 0
                pe.wait_ge(S[f"{L}_q_stack"], 16 * PARTS * PARTS)
                pe.wait_ge(S[f"{L}_k_stack"], 16 * PARTS * PARTS)
                for b in range(B):
                    for q in range(2):
                        j = 2 * b + q
                        for h0 in range(0, H, heads):
                            if n >= 4:
                                pe.wait_ge(S[f"{L}_redmax"], n - 3)
                            for i in range(heads):
                                ins = mm(ps[:, n % 4, i * KEYS[L]:(i + 1) * KEYS[L]],
                                         qs[0:STACK, h0 + i, j * P:(j + 1) * P],
                                         ks[L][0:STACK, h0 + i, b * KEYS[L]:(b + 1) * KEYS[L]],
                                         True, L == "a")
                            if L == "x":
                                ins = mm(ps[:, n % 4, :], neg_i[:], mq[:, j, :], False, True)
                            ins.then_inc(S[f"{L}_smax_ps"], 1)
                            n += 1
                    pe.wait_ge(S[f"{L}_redmax"], n)
                    for q in range(2):
                        ins = nc.tensor.transpose(ps[0:H, 4 + b, q * P:(q + 1) * P],
                                                  mx[L][:, 2 * b + q, :], ident[:])
                    ins.then_inc(S[f"{L}_mT_ps"], 1)

                def logits(n):
                    b, g, k = n // (4 * nk), n // nk % 4, n % nk
                    if n >= 2:
                        pe.wait_ge(S[f"{L}_e_exp"], n - 1)
                    if g == 0 and k == 0:
                        pe.wait_ge(S[f"{L}_nm_stack{b}"], 16 * PARTS)
                    rows = STACK + PARTS
                    for r in range(2):
                        bank = 2 * (n % 2) + r
                        for i in range(2):
                            h = 4 * g + 2 * r + i
                            ins = mm(ps[:, bank, i * T:(i + 1) * T],
                                     ks[L][0:rows, h, b * KEYS[L] + k * P:b * KEYS[L] + (k + 1) * P],
                                     qs[0:rows, h, b * T:(b + 1) * T], L == "a" or i == 0, L == "a", L == "x")
                        if L == "x":
                            for i in range(2):
                                ins = mm(ps[:, bank, i * T:(i + 1) * T], neg_i[:], mk[:, b, k, :],
                                         False, i == 1, True)
                    ins.then_inc(S[f"{L}_s_ps"], 1)

                def values(n):
                    b, g, k = n // (4 * nk), n // nk % 4, n % nk
                    i = n // nk
                    pe.wait_ge(S[f"{L}_e_exp"], n + 1)
                    if k == 0 and i >= 2:
                        pe.wait_ge(S[f"{L}_o_sb"], i - 1)
                    if n == 0:
                        pe.wait_ge(S[f"{L}_nm_done"], B)
                    for r in range(4):
                        ins = mm(ps[32 * r:32 * r + 32, 4 + i % 2, 0:T],
                                 v1[:, b * nk + k, 4 * g + r, :], ex1[:, n % 3, r * T:(r + 1) * T],
                                 k == 0, k == nk - 1)
                    ins.then_inc(S[f"{L}_e_used"], 1)

                total = B * 4 * nk
                logits(0)
                for n in range(total):
                    if n + 1 < total:
                        logits(n + 1)
                    values(n)
                for g in range(4):
                    pe.wait_ge(S[f"{L}_o_sb"], 4 + g + 1)
                    if g >= 2:
                        pe.wait_ge(S[f"{L}_o_norm"], g - 1)
                    for j in range(NJ):
                        ins = nc.tensor.transpose(ps[:, 6 + g % 2, j * P:(j + 1) * P],
                                                  og[:, g, j * P:(j + 1) * P], ident[:])
                    ins.then_inc(S[f"{L}_oT_ps"], 1)
                pe.wait_ge(S[f"{L}_o_norm"], 4)
                for j in range(NJ):
                    ins = nc.tensor.transpose(ps[:, 6, j * P:(j + 1) * P],
                                              ao1[:, j, :, :].rearrange("p h d -> p (h d)"), ident[:])
                ins.then_inc(S[f"{L}_aT_ps"], 1)
                pe.wait_ge(S[f"{L}_aT_done"], 1)
                w_o = w_a1[:, 384:512] if L == "a" else w_x1[:, 3, :]
                to_rows(7, [aoT1], [w_o], f"{L}_y_ps")

            pe.wait_ge(S["va_done"], 1)
            attend("a")
            pe.wait_ge(ld["x1"], 16)
            pe.wait_ge(ld["cxT"], 16)
            for i in range(2):
                mm(ps[:, 1 + i, :], w_x1[:, 1, :], cxT[:, i * 512:(i + 1) * 512]
                   ).then_inc(S["kx_ps"], 1)
            for i in range(2):
                if i:
                    pe.wait_ge(S["kx_done"], 2)
                for k in range(4):
                    t = 4 * i + k
                    ins = mm(ps[:, 3 - i, k * P:(k + 1) * P], cxT[:, t * P:(t + 1) * P], w_x1[:, 2, :])
                ins.then_inc(S["vx_ps"], 1)
            pe.wait_ge(norm_out, NORMS.index("post3") + 1)
            to_cols(0, x, "xT_ps")
            pe.wait_ge(S["xT_done"], 3)
            mm(ps[:, 4, :], w_x1[:, 0, :], xT[:]).then_inc(S["qx_ps"], 1)
            pe.wait_ge(S["mask_done"], 2)
            pe.wait_ge(S["vx_done"], 2)
            attend("x")
            pe.wait_ge(norm_out, NORMS.index("post4") + 1)
            to_cols(0, x, "xT_ps")
            pe.wait_ge(ld["e1"], 96)
            pe.wait_ge(S["xT_done"], 4)
            for j in range(NJ):
                ins = mm(ps[:, 1, j * E1:(j + 1) * E1], xT[:, j * P:(j + 1) * P], w_g1[:])
            ins.then_inc(S["g1_ps"], 1)
            for c in range(SH):
                mm(ps[:, 2 + c, :], w_sh[:, c, :], xT[:]).then_inc(S["shu_ps"], 1)

            def up1(c):
                pe.wait_ge(S["relu_done"] if c >= 2 else S["shr_done"], c - 1 if c >= 2 else SH)
                mm(ps[:, 2 + c % 2, :], w_up1[:, c, :], xT[:]).then_inc(S["up1_ps"], 1)

            for c in range(2):
                up1(c)
            pe.wait_ge(S["cmb_done"], 1)
            for j in range(NJ):
                ins = nc.tensor.transpose(ps[0:E1, 4, j * P:(j + 1) * P], cmb[:, j, :], ident[:])
            ins.then_inc(S["cmbT_ps"], 1)
            pe.wait_ge(S["cms_done"], 1)
            for c in range(C1):
                if c + 2 < C1:
                    up1(c + 2)
                if c >= 2:
                    pe.wait_ge(S["cb_mul"], c - 1)
                mm(ps[:, 5 + c % 2, :], sel_e[:, c, :], cms[:]).then_inc(S["cb_ps"], 1)
            pe.wait_ge(S["sh_done"], SH)
            pe.wait_ge(S["h1_done"], C1)
            to_rows(7, [hh[:, c, :] for c in range(C1)] + [hsh[:, c, :] for c in range(SH)],
                    [w_dn1[:, c, :] for c in range(C1)] + [w_sh[:, SH + c, :] for c in range(SH)],
                    "y1_ps")


def _constants():
    bf16 = mybir.dt.np(mybir.dt.bfloat16)
    p = np.arange(P)
    c = {"ident": np.eye(P, dtype=np.float32), "neg_i": (-BIG * np.eye(P)).astype(bf16)}
    sel = np.zeros((P, NG, P))
    for g in range(NG):
        sel[g * GD + p // STATE, g, p] = 1
    c["sel_g"] = sel.astype(bf16)
    sel = np.zeros((P, NG // 4, 32), np.float32)
    for i in range(NG // 4):
        sel[p, i, GD * i + p // STATE] = 1
    c["sel_y"] = sel
    sel = np.zeros((PARTS, E1, C1, P))
    for i in range(C1):
        sel[:, 2 * i + p // I1, i, p] = 1
    c["sel_e"] = sel.reshape(PARTS * E1, C1, P).astype(bf16)
    ids = np.arange(D // 2, dtype=np.float32)
    theta = np.float32(10000.0) ** (np.float32(-2.0) * ids) / np.float32(D // 2)
    r = np.arange(T, dtype=np.float32)[None, :] * theta[:, None].astype(np.float32)
    cos, sin = np.repeat(np.cos(r), 2, 0), np.repeat(np.sin(r), 2, 0)
    sign = np.where(p % 2 == 0, -1.0, 1.0)[:, None]
    c["rope1"] = np.stack([cos, sin * sign], 1).astype(np.float32)
    c["rope_sign"] = np.where(p % DH0 < DH0 // 2, -1.0, 1.0).astype(np.float32)[:, None]
    return c


def _layout(i):
    c = _constants()
    i = {k: np.asarray(x) for k, x in i.items()}
    L0, X0, F, L1, X1, F1 = (lambda k, q=q: i[q + k] for q in (
        "L0_attn_", "L0_xattn_", "L0_ffn_", "L1_attn_", "L1_xattn_", "L1_ffn_"))
    col = lambda x: x.reshape(-1, 1)
    pad = lambda x: np.concatenate([x, np.zeros(P - len(x), x.dtype)]).reshape(-1, 1)
    half = np.arange(P) ^ (DH0 // 2)
    pair = np.arange(P) ^ 1
    a_log = L0("A_log")
    cols = {
        "w1_b": col(L0("w1_b")), "v1_b": col(L0("v1_b")), "ln_g": col(L0("ln_g")),
        "ln_b": col(L0("ln_b")), "conv": L0("conv_w")[:, 0, :], "dt_b": col(L0("dt_b")),
        "Bp_b": col(np.tile(L0("Bp_b"), GD)), "Cp_b": col(np.tile(L0("Cp_b"), GD)),
        "A_log": a_log.reshape(NG, P).T, "D_p": col(L0("D_p")),
        "ln2_g": col(L0("ln2_g")), "ln2_b": col(L0("ln2_b")), "ff1_b": L0("ff1_b").reshape(FF, P).T,
        "lat_g": col(X0("ln_lat_g")), "lat_b": col(X0("ln_lat_b")), "ctx_g": col(X0("ln_ctx_g")),
        "ctx_b": col(X0("ln_ctx_b")), "rope_sign": c.pop("rope_sign"), "Wd_q_b": pad(L1("Wd_q_b")),
        "Wd_kv_b": pad(L1("Wd_kv_b")), "Wu_q_b": col(L1("Wu_q_b")), "Wq_r_b": col(L1("Wq_r_b")),
        "Wq_s_b": col(L1("Wq_r_b")[pair]), "Wu_k_b": col(L1("Wu_k_b")), "Wk_r_b": col(L1("Wk_r_b")),
        "Wk_s_b": col(L1("Wk_r_b")[pair]), "bq": col(X1("bq")), "bk": col(X1("bk")),
    }
    chunks = lambda w: w.reshape(-1, P, w.shape[-1]).transpose(1, 0, 2)
    a = dict(c)
    a["vec"] = np.concatenate([cols[k] for k in VEC], 1)
    a["rowv"] = np.stack([L0("ln1_g"), L0("ln1_b"), L0("w2_b"), L0("ff2_b"), X0("bo"), L1("Wu_v_b"),
                          L1("Wo_b"), X1("bv").reshape(D), X1("bo")])
    a["x"] = i["x"].reshape(NJ, P, D).transpose(1, 0, 2)
    a["cx"] = i["ctx_1024"].reshape(NC_TILES, P, D).transpose(1, 0, 2)
    a["cxT"] = i["ctx_1024"].reshape(B * CS, D).T
    a["w_mix"] = np.stack([L0("w1_w"), L0("v1_w"), L0("dt_w"), np.tile(L0("Bp_w"), (1, GD)),
                           np.tile(L0("Cp_w"), (1, GD)), L0("w2_w")], 1)
    a["w_ff"] = np.concatenate([L0("ff1_w").reshape(D, FF, P), chunks(L0("ff2_w"))], 1)
    a["rope0"] = np.stack([np.tile(X0("cos").T, (4, 1)), np.tile(X0("sin").T, (4, 1))], 1)
    wk, wv = X0("Wkv")[:, :1024].reshape(D, NPAIR, P), X0("Wkv")[:, 1024:].reshape(D, NPAIR, P)
    a["w_x0"] = np.stack([wk, wk[:, :, half], wv, X0("Wq").reshape(D, NPAIR, P), chunks(X0("Wo"))], 2)
    a["w_r0"] = F("router_w").T
    a["w_up0"] = F("expert_w1").transpose(2, 0, 1)
    a["w_dn0"] = F("expert_w2").reshape(E0, D, F0, P).transpose(3, 0, 2, 1)
    a["w_a1"] = np.concatenate([L1("Wd_q_w"), L1("Wd_kv_w"), L1("Wk_r_w"), L1("Wk_r_w")[:, pair],
                                L1("Wo_w")], 1)
    a["w_u1"] = np.stack([L1("Wu_q_w"), L1("Wq_r_w"), L1("Wq_r_w")[:, pair], L1("Wu_k_w"),
                          L1("Wu_v_w")], 1)
    a["w_x1"] = np.stack([X1("Wq").reshape(D, D), X1("Wk").reshape(D, D), X1("Wv").reshape(D, D),
                          X1("Wo").reshape(D, D)], 1)
    mask = i["mask_BxSxS2_bk1"]
    a["mq8"] = mask.reshape(NJ, P, CS).transpose(1, 0, 2)
    a["mk8"] = mask.reshape(B, T, CS // P, P).transpose(3, 0, 2, 1)
    a["w_g1"] = F1("gate_w").T
    a["eb"] = F1("e_bias")
    a["w_up1"] = F1("up_w").reshape(C1, P, D).transpose(2, 0, 1)
    a["w_dn1"] = F1("down_w").transpose(0, 2, 1).reshape(C1, P, D).transpose(1, 0, 2)
    a["w_sh"] = np.concatenate([F1("shared_up_w").reshape(SH, P, D).transpose(2, 0, 1),
                                chunks(F1("shared_down_w").T)], 1)
    return {k: np.ascontiguousarray(x) for k, x in a.items()}


def kernel(**inputs):
    import concourse.bacc as bacc
    from concourse.bass_utils import run_bass_kernel_spmd

    nc = bacc.Bacc("TRN2", target_bir_lowering=False, num_devices=1)
    arrays = _layout(inputs)
    aps = {k: nc.dram_tensor(f"in_{k}", x.shape, mybir.dt.from_np(x.dtype), kind="ExternalInput").ap()
           for k, x in arrays.items()}
    out = nc.dram_tensor("out", (P, NJ, D), mybir.dt.float32, kind="ExternalOutput").ap()
    program(nc, aps, out)
    r = run_bass_kernel_spmd(nc, [{f"in_{k}": x for k, x in arrays.items()}], core_ids=[0])
    return r.results[0]["out"].transpose(1, 0, 2).reshape(B, T, D)
```

```python
from contextlib import ExitStack

import numpy as np

from concourse import mybir

P = 128
D = 128
B, T = 2, 256
N = B * T
NJ = N // P
CS = 512
NC_TILES = B * CS // P
STATE = 16
GD = P // STATE
NG = D // GD
H = 16
DH0 = 64
DH = 8
NPAIR = H // 2
HB = H // 2
NB = 2 * B
FF = 3
E0, F0 = 8, 512 // P
E1, I1 = 32, 64
C1 = E1 * I1 // P
SH = 256 // P
PARTS = 3
STACK = PARTS * PARTS * DH
EPS = 1e-5
CLIP = 11.0
BIG = 2.0 ** 100
FAR = 3.0e38

VEC = {}
for _name, _width in (
    ("w1_b", 1), ("v1_b", 1), ("ln_g", 1), ("ln_b", 1), ("conv", 3), ("dt_b", 1), ("Bp_b", 1),
    ("Cp_b", 1), ("A_log", NG), ("D_p", 1), ("ln2_g", 1), ("ln2_b", 1), ("ff1_b", FF),
    ("lat_g", 1), ("lat_b", 1), ("ctx_g", 1), ("ctx_b", 1), ("rope_sign", 1), ("Wd_q_b", 1),
    ("Wd_kv_b", 1), ("Wu_q_b", 1), ("Wq_r_b", 1), ("Wq_s_b", 1), ("Wu_k_b", 1), ("Wk_r_b", 1),
    ("Wk_s_b", 1), ("bq", 1), ("bk", 1),
):
    VEC[_name] = (sum(w for _, w in VEC.values()), _width)
NVEC = sum(w for _, w in VEC.values())
ROWV = ("ln1_g", "ln1_b", "w2_b", "ff2_b", "bo0", "Wu_v_b", "Wo_b", "bv", "bo1")

NORMS = ("ln1", "ln", "ctx", "ln2", "post0", "lat", "post1", "post2", "post3", "post4", "post5")


def program(nc, a, out):
    f32, bf16, u8 = mybir.dt.float32, mybir.dt.bfloat16, mybir.dt.uint8
    ALU, ACT, AX = mybir.AluOpType, mybir.ActivationFunctionType, mybir.AxisListType
    ctx = ExitStack()
    with ctx:
        def sb(name, shape, dt=f32):
            return ctx.enter_context(nc.sbuf_tensor(name, shape, dt))

        def sem(name):
            return ctx.enter_context(nc.semaphore(name))

        def region(name, words):
            t = sb(name, [P, words])

            def take(at, shape, dt=f32):
                n = int(np.prod(shape[1:])) // {f32: 1, bf16: 2, u8: 4}[dt]
                piece = t[0:shape[0], at:at + n]
                names = "abcde"[:len(shape) - 1]
                piece = piece if dt == f32 else piece.bitcast(dt)
                if len(shape) == 2:
                    return piece
                return piece.rearrange(f"p ({' '.join(names)}) -> p {' '.join(names)}",
                                       **dict(zip(names[1:], shape[2:])))
            return take

        vec = sb("vec", [P, NVEC])
        rowv = sb("rowv", [P, len(ROWV), D])
        ident = sb("ident", [P, P])
        w_mix = sb("w_mix", [P, 6, D])
        sel_y = sb("sel_y", [P, NG // 4, 32])
        w_ff = sb("w_ff", [P, 2 * FF, D])
        w_r0 = sb("w_r0", [P, E0])
        w_a1 = sb("w_a1", [P, 2 * 64 + 3 * P])
        w_u1 = sb("w_u1", [64, 5, P])
        rope1 = sb("rope1", [P, 2, T])
        w_x1 = sb("w_x1", [P, 4, D])
        neg_i = sb("neg_i", [P, P], bf16)
        w_g1 = sb("w_g1", [P, E1])
        w_sh = sb("w_sh", [P, 2 * SH, P])
        eb = sb("eb", [P, E1])
        sel = region("sel", 1024)
        sel_g = sel(0, [P, NG, P], bf16)
        sel_e = sel(0, [PARTS * E1, C1, P], bf16)
        attn_w = region("attn_w", 5 * 8 * P)
        w_x0 = attn_w(0, [P, NPAIR, 5, P])
        w_up1 = attn_w(0, [P, C1, P])
        w_dn1 = attn_w(C1 * P, [P, C1, P])
        late = region("late", 8192)
        w_up0 = late(0, [P, E0, F0 * P])
        w_dn0 = late(4096, [P, E0, F0, D])
        qs = late(0, [STACK + PARTS, H, N], bf16)
        v1 = {L: late(at, [P, nt, (H + 1) * 2 * DH])
              for L, nt, at in (("x", NC_TILES, 4096), ("a", NJ, 4096 + NC_TILES * (H + 1) * 2 * DH))}
        v1_all = late(4096, [P, (NC_TILES + NJ) * (H + 1) * 2 * DH])
        rl = late(0, [P, 4, N])
        cms = late(3072, [PARTS * E1, N], bf16)
        cmp_ = late(3328, [E1, PARTS, N], bf16)
        cmf = late(4096, [E1, 2, N])

        def v(name, i=0, rows=P):
            at = VEC[name][0] + i
            return vec[0:rows, at:at + 1]

        def rv4(name):
            return rowv[:, ROWV.index(name):ROWV.index(name) + 1, :].broadcast_to([P, NJ, D])

        x = sb("x", [P, NJ, D])
        x2 = sb("x2", [P, NJ, D])
        resid = sb("resid", [P, NJ, D])
        summed = sb("summed", [P, NJ, D])
        normed = sb("normed", [P, NJ, D])
        stats = sb("stats", [P, NC_TILES, 6])
        meanvar = sb("meanvar", [P, len(NORMS), NC_TILES, 2])
        rstd = sb("rstd", [P, len(NORMS), NC_TILES])
        vareps = sb("vareps", [P, NC_TILES])
        neghalf = sb("neghalf", [P, NC_TILES])
        xT = sb("xT", [P, N])
        cv = sb("cv", [P, 2, N])
        dtmp = sb("dtmp", [P, 3, N])

        mid = region("mid", 6144)
        x1p = mid(0, [P, B, T + 2])
        xc = mid(516, [P, N])
        gate = mid(1028, [P, N])
        Bn = mid(1540, [P, N])
        Cn = mid(2052, [P, N])
        dl = mid(2564, [P, 2, N])
        dparts = mid(3588, [P, 2, PARTS, N], bf16)
        nA = sb("nA", [P, 2, NG])
        big1, big2 = region("big1", 8192), region("big2", 8192)
        dA = big1(0, [P, 2, N])
        dBx = big1(1024, [P, 2, N])
        hs = big1(2048, [P, 4, N])
        hC = big1(4096, [P, 8, N])
        ffh = big2(0, [P, FF, N])

        ctx_r = region("ctx_r", 3 * 1024)
        rope0 = ctx_r(0, [P, 2, CS])
        cxnT = ctx_r(1024, [P, B * CS])
        cx = ctx_r(2048, [P, NC_TILES, D])
        parts1 = {"qa": ctx_r(0, [P, PARTS, N], bf16), "ka": ctx_r(768, [P, PARTS, N], bf16),
                  "qx": ctx_r(0, [P, PARTS, N], bf16), "kx": ctx_r(1536, [P, PARTS, B * CS], bf16)}
        cxT = ctx_r(2048, [P, B * CS])

        kT0 = big1(0, [P, 2, B * CS])
        kt1 = big1(2048, [P, 2, CS])
        kt2 = big1(3072, [P, 2, CS])
        qT0 = big1(4096, [P, 2, N])
        ex = big1(5120, [P, 3, 1024])
        v0 = mid(0, [P, 2, NC_TILES, 2, DH0])
        esum = big2(1536, [P, 2, 2 * T])
        etot = big2(2560, [P, 2, 2 * T])
        ones0 = big2(3584, [P, DH0])
        rden = sb("rden", [P, NJ, H])
        aoT = big2(4096, [P, NPAIR, N])

        sc0 = sb("sc0", [P, NJ, 2 * E0])
        top0 = sb("top0", [P, NJ, 8])
        pick0 = sb("pick0", [P, NJ, 8])
        mark0 = sb("mark0", [P, NJ, 2 * E0])
        g0 = sb("g0", [P, 4, NJ, E0])
        den0 = sb("den0", [P, 2, NJ])
        eh0 = big1(0, [P, 2, F0, N])

        ks = {"a": big2(0, [P, H, N], bf16), "x": big1(0, [P, H, B * CS], bf16)}
        kxf = big2(4096, [P, B * CS])
        kxr = big2(4096 + B * CS, [P, B * CS])
        ex1 = big2(4096, [P, 3, 1024])
        qf = mid(0, [P, 2, N])
        cq = mid(1024, [64, 2, N])
        nm = mid(2048, [HB, 2, 2, T])
        nmp = mid(3072, [HB, 2, PARTS, T], bf16)
        og = mid(3840, [P, H // 4, N])
        mx = {"a": sb("mx_a", [P, NJ, H]), "x": sb("mx_x", [P, NJ, H])}
        ao1 = x2[:, :, :].rearrange("p j (h d) -> p j h d", h=H)
        aoT1 = w_mix[:, 0:NJ, :].rearrange("p a b -> p (a b)")
        mq8 = mid(0, [P, NJ, CS], u8)
        mk8 = mid(512, [P, B, CS // P, T], u8)
        mq = big2(7168, [P, NJ, CS], bf16)
        mk = sel(0, [P, B, CS // P, T], bf16)

        lg1 = late(5120, [P, 4, NJ, E1])
        r1 = sb("r1", [P, 2, NJ, 16])
        sel1 = w_ff[:, 0:4, :].rearrange("p a (j e) -> p (a j) e", e=64).rearrange(
            "p (i j) e -> p i j e", i=2)
        t1 = sb("t1", [P, 4, NJ, 8])
        pr1 = sb("pr1", [P, 2, NJ, 8])
        cmb = sb("cmb", [P, NJ, E1])
        hh = big2(0, [P, C1, N])
        hsh = big1(0, [P, SH, N])

        ps = ctx.enter_context(nc.psum_tensor("ps", [P, 8, 512], f32))

        scr = {k: nc.dram_tensor(f"parts_{k}", [P, PARTS, w], bf16, kind="Internal").ap()
               for k, w in (("qa", N), ("ka", N), ("qx", N), ("kx", B * CS))}

        ld = {k: sem(f"loaded_{k}") for k in (
            "x", "vec", "rowv", "ident", "mix", "sel", "cx", "cxT", "ff", "rope0", "x0", "e0", "a1",
            "x1", "mask", "e1", "ones_a", "ones_x")}
        norm_var = sem("norm_var")
        norm_rstd = sem("norm_rstd")
        norm_out = sem("norm_out")
        consts = sem("consts")
        dve_own, act_own, pool_own = sem("dve_own"), sem("act_own"), sem("pool_own")
        S = {k: sem(k) for k in (
            "xmT_ps", "xmT", "w1_ps", "v1_ps", "x1p_done", "conv_done", "xc_done", "gate_done",
            "dt_ps", "z_done", "BC_ps", "BC_done", "negA", "lg_done", "delta_parts", "dx_parts",
            "spread_d", "spread_x", "dA_done", "dBx_done", "scan_done", "hC_done", "y_ps",
            "yv_done", "mo_ps", "res_ready", "x2_done", "hT_ps", "hT", "ff_ps", "ff_act", "ff2_ps",
            "cxnT_ps", "cxnT_done", "latT_ps", "latT",
            "k0_ps", "k0_mul", "k0_done", "q0_ps", "q0_done", "v0_ps", "v0_done", "s0_ps", "e0_exp",
            "e0_clip", "e0_used", "e0_sum", "e0_tot", "o0_ps", "o0_norm", "y0_ps",
            "xT_ps", "xT_done", "r0_ps", "r0_max", "r0_exp", "up0_ps", "up0_act", "dn0_ps",
            "dn0_acc", "stored",
            "cdown_ps", "cdown_done", "qa_ps", "qa_done", "va_ps", "va_done", "qx_ps", "qx_done",
            "kx_ps", "kx_done", "vx_ps", "vx_done", "mask_done",
            "g1_ps", "g1_exp", "cmb_done", "cmbT_ps", "cms_done", "up1_ps", "relu_done", "cb_ps",
            "h1_done", "sq_even", "sq_odd", "y1_ps", "rope_signed", "ones")}
        for L in "ax":
            for k in ("q_parts", "k_parts", "q_scr", "k_scr", "q_stack", "k_stack", "smax_ps",
                      "redmax", "mT_ps", "nm_done", "nm_stack0", "nm_stack1", "s_ps", "e_exp", "e_used", "o_sb",
                      "oT_ps", "o_norm", "aT_ps", "aT_done", "y_ps"):
                S[f"{L}_{k}"] = sem(f"{L}_{k}")

        def normed_tiles(name, j=None):
            tiles = [NC_TILES if n == "ctx" else NJ for n in NORMS[:NORMS.index(name) + 1]]
            return sum(tiles) if j is None else sum(tiles[:-1]) + j + 1

        def own(eng, chain):
            count = [0]

            def link(ins):
                count[0] += 1
                ins.then_inc(chain, 1)
                eng.wait_ge(chain, count[0])
            return link

        ORDER = [4 * (s % 4) + s // 4 for s in range(NG)]
        NX = {"a": NORMS.index("post2"), "x": NORMS.index("post3")}
        KEYS = {"a": T, "x": CS}

        MT_BANK = (4, 7, 7, 7)
        AHEAD = {"a": 12, "x": 16}

        def row_steps(L):
            return 2 * HB * KEYS[L] // 512

        def row_bank(L, m):
            return 6 + m % 2 if m >= row_steps(L) + AHEAD[L] else m % 4

        def rows_beside(L, n):
            m = row_steps(L) + AHEAD[L] + 2 * n
            return [(i,) + divmod(i, row_steps(L)) for i in (m, m + 1) if i < NB * row_steps(L)]

        def last_rows(L, n):
            for _, k, i in rows_beside(L, n):
                if i == row_steps(L) - 1:
                    return [k]
            return []

        UP1 = (2, 3, 0, 1)

        def hidden(m):
            return hsh[:, m, :] if m < SH else hh[:, m - SH, :]

        block = ctx.enter_context(nc.Block())

        def stack(eng, L, which, pieces):
            s = f"{L}_{which}"
            eng.wait_ge(S[f"{s}_scr"], 16)
            dst = qs if which == "q" else ks[L]
            for c in pieces:
                part = c // PARTS if which == "q" else c % PARTS
                eng.dma_start(dst[DH * c:DH * c + DH, :, :],
                              scr[which + L][:, part, :].rearrange("(h d) t -> d h t", d=DH)
                              ).then_inc(S[f"{s}_stack"], 16)

        @block.sync
        def _(sp):
            sp.dma_start(x[:], a["x"]).then_inc(ld["x"], 16)
            sp.dma_start(rowv[:], a["rowv"].partition_broadcast(P)).then_inc(ld["rowv"], 16)
            sp.dma_start(vec[:], a["vec"]).then_inc(ld["vec"], 16)
            sp.dma_start(ident[:], a["ident"]).then_inc(ld["ident"], 16)
            sp.dma_start(w_mix[:], a["w_mix"]).then_inc(ld["mix"], 16)
            sp.dma_start(sel_g[:], a["sel_g"]).then_inc(ld["sel"], 16)
            sp.dma_start(sel_y[:], a["sel_y"]).then_inc(ld["sel"], 16)
            sp.dma_start(cx[:], a["cx"]).then_inc(ld["cx"], 16)
            sp.dma_start(w_ff[:], a["w_ff"]).then_inc(ld["ff"], 16)
            sp.dma_start(w_x1[:], a["w_x1"]).then_inc(ld["x1"], 16)
            sp.dma_start(rope0[:], a["rope0"]).then_inc(ld["rope0"], 16)
            sp.dma_start(w_x0[:], a["w_x0"]).then_inc(ld["x0"], 16)
            sp.dma_start(neg_i[:], a["neg_i"]).then_inc(ld["mask"], 16)
            sp.dma_start(w_r0[:], a["w_r0"]).then_inc(ld["e0"], 16)
            sp.dma_start(w_up0[:], a["w_up0"]).then_inc(ld["e0"], 16)
            sp.dma_start(w_dn0[:], a["w_dn0"]).then_inc(ld["e0"], 16)
            sp.dma_start(w_a1[:], a["w_a1"]).then_inc(ld["a1"], 16)
            sp.dma_start(w_u1[:], a["w_u1"]).then_inc(ld["a1"], 16)
            sp.dma_start(rope1[:], a["rope1"]).then_inc(ld["a1"], 16)
            sp.dma_start(w_g1[:], a["w_g1"]).then_inc(ld["e1"], 16)
            sp.dma_start(w_sh[:], a["w_sh"]).then_inc(ld["e1"], 16)
            sp.dma_start(eb[:], a["eb"].partition_broadcast(P)).then_inc(ld["e1"], 16)

            def park(L, which):
                s = f"{L}_{which}"
                sp.wait_ge(S[f"{s}_parts"], 1)
                sp.dma_start(scr[which + L], parts1[which + L]).then_inc(S[f"{s}_scr"], 16)

            def spread_max(L):
                for k in range(NB):
                    b, h0 = k // 2, HB * (k % 2)
                    sp.wait_ge(S[f"{L}_nm_done"], k + 1)
                    for i in range(PARTS):
                        sp.dma_start(qs[STACK + i:STACK + i + 1, h0:h0 + HB, b * T:(b + 1) * T],
                                     nmp[:, k % 2, i, :]).then_inc(S[f"{L}_nm_stack{k % 2}"], 16)

            sp.wait_ge(S["cxnT_ps"], 2)
            sp.dma_start(cxT, a["cxT"]).then_inc(ld["cxT"], 16)
            sp.wait_ge(S["y0_ps"], 1)
            sp.dma_start(mq8, a["mq8"]).then_inc(ld["mask"], 16)
            sp.dma_start(mk8, a["mk8"]).then_inc(ld["mask"], 16)
            sp.dma_start(ks["a"][STACK:STACK + PARTS, :, :], a["ones"][:, :, 0:N]
                         ).then_inc(ld["ones_a"], 16)
            sp.dma_start(w_up1, a["w_up1"]).then_inc(ld["e1"], 16)
            sp.dma_start(w_dn1, a["w_dn1"]).then_inc(ld["e1"], 16)
            sp.wait_ge(S["dn0_ps"], E0)
            sp.dma_start(ks["x"][STACK:STACK + PARTS, :, :], a["ones"]).then_inc(ld["ones_x"], 16)
            park("x", "k")
            stack(sp, "x", "k", range(0, 9))
            park("a", "q")
            stack(sp, "a", "q", range(0, 5))
            park("a", "k")
            stack(sp, "a", "k", range(0, 5))
            spread_max("a")
            sp.wait_ge(S["a_s_ps"], B * (H // 4) * (T // P))
            park("x", "q")
            stack(sp, "x", "q", range(0, 5))
            spread_max("x")
            sp.wait_ge(S["x_s_ps"], B * (H // 4) * (CS // P))
            sp.dma_start(sel_e, a["sel_e"]).then_inc(ld["e1"], 16)
            sp.wait_ge(norm_out, normed_tiles(NORMS[-1]))
            sp.dma_start(out, normed[:]).then_inc(S["stored"], 16)
            sp.wait_ge(S["stored"], 16)

        @block.gpsimd
        def _(pool):
            link = own(pool, pool_own)
            nc.gpsimd.memset(neghalf[:], -0.5).then_inc(consts, 1)
            nc.gpsimd.memset(x1p[:], 0.0).then_inc(consts, 1)
            nc.gpsimd.memset(sc0[:], -FAR).then_inc(consts, 1)
            nc.gpsimd.memset(pick0[:], -FAR).then_inc(consts, 1)
            nc.gpsimd.memset(r1[:], -FAR).then_inc(consts, 1)
            nc.gpsimd.memset(t1[:], -FAR).then_inc(consts, 1)
            nc.gpsimd.memset(ones0, 1.0).then_inc(consts, 1)
            pool.wait_ge(consts, 7)

            def root(name):
                k = NORMS.index(name)
                nt = NC_TILES if name == "ctx" else NJ
                pool.wait_ge(norm_var, k + 1)
                link(nc.gpsimd.tensor_scalar(vareps[:, 0:nt], meanvar[:, k, 0:nt, 1], EPS, None,
                                             ALU.add))
                nc.gpsimd.tensor_tensor(rstd[:, k, 0:nt], vareps[:, 0:nt], neghalf[:, 0:nt],
                                        ALU.pow).then_inc(norm_rstd, 1)
                pool.wait_ge(norm_rstd, k + 1)


            root("ln1")
            root("ln")
            root("ctx")
            pool.wait_ge(ld["x"], 16)
            pool.wait_ge(ld["rowv"], 16)
            nc.gpsimd.tensor_tensor(resid[:], x[:], rv4("w2_b"), ALU.add).then_inc(S["res_ready"], 1)
            for s in range(NG):
                pool.wait_ge(S["scan_done"], s + 1)
                if s == 0:
                    pool.wait_ge(S["BC_done"], 2)
                if s >= 8:
                    pool.wait_ge(S["y_ps"], (s - 8) // 4 + 1)
                nc.gpsimd.tensor_tensor(hC[:, s % 8, :], hs[:, s % 4, :], Cn[:],
                                        ALU.mult).then_inc(S["hC_done"], 1)
            root("ln2")
            pool.wait_ge(S["x2_done"], 1)
            link(nc.gpsimd.tensor_tensor(resid[:], x[:], rv4("ff2_b"), ALU.add))
            nc.gpsimd.tensor_tensor(resid[:], resid[:], x2[:], ALU.add).then_inc(S["res_ready"], 1)

            def rotated0(c, b):
                n = B * c + b
                pool.wait_ge(S["k0_mul"], 2 * n + 2)
                if c >= 2:
                    pool.wait_ge(S["s0_ps"], 4 * (c - 1))
                nc.gpsimd.tensor_tensor(kT0[:, c % 2, b * CS:(b + 1) * CS], kt1[:, n % 2, :],
                                        kt2[:, n % 2, :], ALU.add).then_inc(S["k0_done"], 1)

            for b in range(B):
                rotated0(0, b)
            root("post0")
            root("lat")
            rotated0(1, 0)
            pool.wait_ge(norm_out, normed_tiles("post0"))
            nc.gpsimd.tensor_tensor(resid[:], x[:], rv4("bo0"), ALU.add).then_inc(S["res_ready"], 1)
            for n in range(4 * NPAIR):
                c, u = divmod(n, 4)
                b, s = divmod(u, 2)
                pool.wait_ge(S["e0_clip"], n + 1)
                if n >= 2:
                    pool.wait_ge(S["e0_tot"], 2 * c + b)
                e = ex[:, n % 3, :].rearrange("p (r k t) -> p r k t", r=2, k=2)
                nc.gpsimd.tensor_tensor(esum[:, s, :].rearrange("p (r t) -> p r t", r=2),
                                        e[:, :, 0, :], e[:, :, 1, :], ALU.add
                                        ).then_inc(S["e0_sum"], 1)
                if s == 1:
                    pool.wait_ge(S["e0_sum"], n + 1)
                    if c:
                        pool.wait_ge(S["o0_ps"], 2 * (c - 1) + b + 1)
                    nc.gpsimd.tensor_tensor(etot[:, b, :], esum[:, 0, :], esum[:, 1, :], ALU.add
                                            ).then_inc(S["e0_tot"], 1)
                if u < 2 and 2 <= c + 1 < NPAIR or n == 1:
                    rotated0(c + 1, u)
            root("post1")
            link(nc.gpsimd.memset(sel1, -FAR))
            pool.wait_ge(S["dn0_ps"], E0)
            nc.gpsimd.memset(v1_all, 1.0).then_inc(S["ones"], 1)
            root("post2")
            pool.wait_ge(norm_out, normed_tiles("post2"))
            nc.gpsimd.tensor_tensor(resid[:], x[:], rv4("Wo_b"), ALU.add).then_inc(S["res_ready"], 1)
            root("post3")
            pool.wait_ge(norm_out, normed_tiles("post3"))
            nc.gpsimd.tensor_tensor(resid[:], x[:], rv4("bo1"), ALU.add).then_inc(S["res_ready"], 1)
            root("post4")
            for m in range(1, SH + C1, 2):
                pool.wait_ge(S["relu_done"], m + 1)
                nc.gpsimd.tensor_tensor(hidden(m), rl[:, m % 4, :], rl[:, m % 4, :],
                                        ALU.mult).then_inc(S["sq_odd"], 1)
            root("post5")

        @block.scalar
        def _(act):
            link = own(act, act_own)

            def to_cols(dst, bank, ready, done, scale=None, bias=None, n=1):
                act.wait_ge(S[ready], n)
                if scale is None:
                    nc.scalar.activation(dst, ps[:, bank, :], ACT.Copy).then_inc(S[done], 1)
                else:
                    nc.scalar.activation(dst, ps[:, bank, :], ACT.Identity, scale=scale,
                                         bias=bias).then_inc(S[done], 1)

            act.wait_ge(ld["vec"], 16)
            to_cols(xT[:], 0, "xmT_ps", "xmT", v("ln_g"), v("ln_b"))
            act.wait_ge(S["w1_ps"], 1)
            act.wait_ge(consts, 7)
            nc.scalar.activation(x1p[:, :, 1:T + 1], ps[:, 1, :].rearrange("p (b t) -> p b t", b=B),
                                 ACT.Identity, bias=v("w1_b")).then_inc(S["x1p_done"], 1)
            act.wait_ge(S["v1_ps"], 1)
            nc.scalar.activation(gate[:], ps[:, 2, :], ACT.Silu, bias=v("v1_b")
                                 ).then_inc(S["gate_done"], 1)
            act.wait_ge(S["conv_done"], 1)
            nc.scalar.activation(xc[:], cv[:, 0, :], ACT.Silu).then_inc(S["xc_done"], 1)
            link(nc.scalar.activation(nA[:, 0, :], vec[:, VEC["A_log"][0]:VEC["A_log"][0] + NG],
                                      ACT.Exp))
            nc.scalar.mul(nA[:, 1, :], nA[:, 0, :], -1.0).then_inc(S["negA"], 1)
            act.wait_ge(S["z_done"], 1)
            link(nc.scalar.activation(dtmp[:, 0, :], cv[:, 1, :], ACT.Abs))
            link(nc.scalar.activation(dtmp[:, 1, :], dtmp[:, 0, :], ACT.Exp, scale=-1.0))
            nc.scalar.activation(dtmp[:, 2, :], dtmp[:, 1, :], ACT.Ln, bias=1.0
                                 ).then_inc(S["lg_done"], 1)
            act.wait_ge(S["BC_ps"], 1)
            nc.scalar.activation(Bn[:], ps[:, 4, :], ACT.Identity, bias=v("Bp_b")
                                 ).then_inc(S["BC_done"], 1)
            nc.scalar.activation(Cn[:], ps[:, 5, :], ACT.Identity, bias=v("Cp_b")
                                 ).then_inc(S["BC_done"], 1)
            act.wait_ge(S["negA"], 1)
            for s, g in enumerate(ORDER):
                act.wait_ge(S["spread_d"], s + 1)
                if s >= 2:
                    act.wait_ge(S["scan_done"], s - 1)
                nc.scalar.activation(dA[:, s % 2, :], ps[:, s % 2, :], ACT.Exp,
                                     scale=nA[:, 1, g:g + 1]).then_inc(S["dA_done"], 1)
            for i in range(2):
                to_cols(cxnT[:, i * 512:(i + 1) * 512], 6 + i, "cxnT_ps", "cxnT_done",
                        v("ctx_g"), v("ctx_b"), i + 1)

            def evac0(c, kind):
                if kind == "q":
                    act.wait_ge(S["q0_ps"], c + 1)
                    if c >= 2:
                        act.wait_ge(S["s0_ps"], 4 * (c - 1))
                    nc.scalar.activation(qT0[:, c % 2, :], ps[:, 6 if c else 3, :], ACT.Copy,
                                         scale=DH0 ** -0.5).then_inc(S["q0_done"], 1)
                elif kind in ("v0", "v1"):
                    i = int(kind[1])
                    act.wait_ge(S["v0_ps"], 2 * c + i + 1)
                    if c >= 2:
                        act.wait_ge(S["e0_used"], 4 * (c - 1))
                    elif c == 0:
                        act.wait_ge(S["mo_ps"], 1)
                    nc.scalar.activation(
                        v0[:, c % 2, 4 * i:4 * i + 4, :, 0:DH0],
                        ps[:, 7 - i, :].rearrange("p (k r d) -> p k r d", k=4, r=2), ACT.Copy
                    ).then_inc(S["v0_done"], 1)

            for kind in ("v0", "v1"):
                evac0(0, kind)
            to_cols(xT[:], 0, "hT_ps", "hT", v("ln2_g"), v("ln2_b"))
            for c in range(FF):
                act.wait_ge(S["ff_ps"], c + 1)
                nc.scalar.activation(ffh[:, c, :], ps[:, 1 + c, :], ACT.Gelu, bias=v("ff1_b", c)
                                     ).then_inc(S["ff_act"], 1)
            for kind in ("v0", "v1"):
                evac0(1, kind)
            to_cols(xT[:], 0, "latT_ps", "latT", v("lat_g"), v("lat_b"))
            evac0(0, "q")
            for c in range(NPAIR):
                for u in range(4):
                    n = 4 * c + u
                    act.wait_ge(S["s0_ps"], n + 1)
                    if n >= 3:
                        act.wait_ge(S["e0_used"], n - 2)
                        act.wait_ge(S["e0_sum"], n - 2)
                    nc.scalar.activation(ex[:, n % 3, :].rearrange("p (r n) -> p r n", r=2),
                                         ps[:, 2 * (n % 2):2 * (n % 2) + 2, :], ACT.Exp
                                         ).then_inc(S["e0_exp"], 1)
                    if c < NPAIR - 1:
                        for kind in ((), ("q",), ("v0",), ("v1",))[u]:
                            if kind == "q" or c:
                                evac0(c + 1, kind)
            for i in range(2):
                act.wait_ge(S["kx_ps"], i + 1)
                nc.scalar.activation(kxf[:, i * 512:(i + 1) * 512], ps[:, 4 + i, :], ACT.Identity,
                                     bias=v("bk")).then_inc(S["kx_done"], 1)
            to_cols(xT[:], 0, "xT_ps", "xT_done")
            act.wait_ge(S["r0_max"], 1)
            nc.scalar.activation(g0[:, 1], g0[:, 0], ACT.Exp).then_inc(S["r0_exp"], 1)
            for e in range(E0):
                for c in range(F0):
                    n = F0 * e + c
                    act.wait_ge(S["up0_ps"], n + 1)
                    if e >= 2:
                        act.wait_ge(S["dn0_ps"], e - 1)
                    nc.scalar.activation(eh0[:, e % 2, c, :], ps[:, n % 3, :], ACT.Gelu
                                         ).then_inc(S["up0_act"], 1)
            to_cols(xT[:], 0, "xT_ps", "xT_done", n=2)
            for i, name in enumerate(("Wd_q_b", "Wd_kv_b")):
                act.wait_ge(S["cdown_ps"], i + 1)
                nc.scalar.activation(cq[:, i, :], ps[0:64, 1 + i, :], ACT.Identity,
                                     bias=v(name, rows=64)).then_inc(S["cdown_done"], 1)

            def attend(L):
                nk = KEYS[L] // P
                scale = 1.0 / float(np.sqrt(np.float32(H + 64 + 64))) if L == "a" else 1.0
                for n in range(B * (H // 4) * nk):
                    act.wait_ge(S[f"{L}_s_ps"], n + 1)
                    if n >= 3:
                        act.wait_ge(S[f"{L}_e_used"], n - 2)
                    nc.scalar.activation(ex1[:, n % 3, :].rearrange("p (r n) -> p r n", r=2),
                                         ps[:, 2 * (n % 2):2 * (n % 2) + 2, :], ACT.Exp, scale=scale
                                         ).then_inc(S[f"{L}_e_exp"], 1)
                act.wait_ge(S[f"{L}_aT_ps"], 1)
                nc.scalar.activation(aoT1[:], ps[:, 6, :], ACT.Copy).then_inc(S[f"{L}_aT_done"], 1)

            stack(act, "a", "q", range(5, 9))
            stack(act, "a", "k", range(5, 9))
            attend("a")
            to_cols(xT[:], 0, "xT_ps", "xT_done", n=3)
            stack(act, "x", "q", range(5, 9))
            attend("x")
            to_cols(xT[:], 0, "xT_ps", "xT_done", n=4)
            act.wait_ge(S["g1_ps"], 1)
            nc.scalar.activation(lg1[:, 0], ps[:, 1, 0:NJ * E1].rearrange("p (j e) -> p j e", j=NJ),
                                 ACT.Exp, scale=-1.0).then_inc(S["g1_exp"], 1)
            for m in range(SH + C1):
                act.wait_ge(S["up1_ps"], m + 1)
                if m >= 4 and m % 2:
                    act.wait_ge(S["sq_odd"], (m - 4) // 2 + 1)
                nc.scalar.activation(rl[:, m % 4, :], ps[:, UP1[m % 4], :], ACT.Relu
                                     ).then_inc(S["relu_done"], 1)
                if m % 2:
                    act.wait_ge(S["relu_done"], m)
                    nc.scalar.activation(hidden(m - 1), rl[:, (m - 1) % 4, :], ACT.Square
                                         ).then_inc(S["sq_even"], 1)

        @block.vector
        def _(dve):
            link = own(dve, dve_own)

            def layernorm(name, src, dst, meanwhile=None):
                k = NORMS.index(name)
                nt = src.shape[1]
                for j in range(nt):
                    ins = nc.vector.bn_stats(stats[:, j, :], src[:, j, :])
                link(ins)
                for j in range(nt):
                    ins = nc.vector.bn_aggr(meanvar[:, k, j, :], stats[:, j, :])
                ins.then_inc(norm_var, 1)
                dve.wait_ge(norm_var, k + 1)
                if meanwhile:
                    meanwhile()
                dve.wait_ge(norm_rstd, k + 1)
                for j in range(nt):
                    nc.vector.tensor_scalar(dst[:, j, :], src[:, j, :], meanvar[:, k, j, 0:1],
                                            rstd[:, k, j:j + 1], ALU.subtract, ALU.mult
                                            ).then_inc(norm_out, 1)
                dve.wait_ge(norm_out, normed_tiles(name))

            def split(src, parts, rest, done):
                link(nc.vector.tensor_copy(parts[0], src))
                link(nc.vector.tensor_tensor(rest, src, parts[0], ALU.subtract))
                link(nc.vector.tensor_copy(parts[1], rest))
                nc.vector.tensor_tensor(parts[2], rest, parts[1], ALU.subtract).then_inc(done, 1)

            dve.wait_ge(ld["x"], 16)
            layernorm("ln1", x[:], normed)
            dve.wait_ge(ld["rowv"], 16)
            link(nc.vector.tensor_tensor(normed[:], normed[:], rv4("ln1_g"), ALU.mult))
            link(nc.vector.tensor_tensor(summed[:], normed[:], rv4("ln1_b"), ALU.add))
            layernorm("ln", summed[:], normed)
            dve.wait_ge(ld["cx"], 16)
            layernorm("ctx", cx, cx)
            dve.wait_ge(ld["vec"], 16)
            dve.wait_ge(S["x1p_done"], 1)
            cv3 = cv[:, :, :].rearrange("p i (b t) -> p i b t", b=B)
            link(nc.vector.tensor_scalar(cv3[:, 0], x1p[:, :, 0:T], v("conv", 0), None, ALU.mult))
            link(nc.vector.scalar_tensor_tensor(cv3[:, 1], x1p[:, :, 1:T + 1], v("conv", 1),
                                                cv3[:, 0], ALU.mult, ALU.add))
            nc.vector.scalar_tensor_tensor(cv3[:, 0], x1p[:, :, 2:T + 2], v("conv", 2), cv3[:, 1],
                                           ALU.mult, ALU.add).then_inc(S["conv_done"], 1)
            dve.wait_ge(S["dt_ps"], 1)
            nc.vector.tensor_scalar(cv[:, 1, :], ps[:, 3, :], v("dt_b"), None, ALU.add
                                    ).then_inc(S["z_done"], 1)
            dve.wait_ge(S["z_done"], 1)
            dve.wait_ge(S["lg_done"], 1)
            link(nc.vector.scalar_tensor_tensor(dl[:, 0, :], cv[:, 1, :], 0.0, dtmp[:, 2, :],
                                                ALU.max, ALU.add))
            split(dl[:, 0, :], [dparts[:, 0, i, :] for i in range(3)], dtmp[:, 0, :],
                  S["delta_parts"])
            dve.wait_ge(S["xc_done"], 1)
            link(nc.vector.tensor_tensor(dl[:, 1, :], dl[:, 0, :], xc[:], ALU.mult))
            split(dl[:, 1, :], [dparts[:, 1, i, :] for i in range(3)], dtmp[:, 1, :], S["dx_parts"])
            dve.wait_ge(S["BC_done"], 1)
            for s in range(NG):
                dve.wait_ge(S["spread_x"], s + 1)
                if s >= 2:
                    dve.wait_ge(S["scan_done"], s - 1)
                nc.vector.tensor_tensor(dBx[:, s % 2, :], ps[:, 2 + s % 2, :], Bn[:],
                                        ALU.mult).then_inc(S["dBx_done"], 1)
                dve.wait_ge(S["dBx_done"], s + 1)
                dve.wait_ge(S["dA_done"], s + 1)
                if s >= 4:
                    dve.wait_ge(S["hC_done"], s - 3)
                for b in range(B):
                    t = slice(b * T, (b + 1) * T)
                    ins = nc.vector.tensor_tensor_scan(hs[:, s % 4, t], dA[:, s % 2, t],
                                                       dBx[:, s % 2, t], 0.0, ALU.mult, ALU.add)
                ins.then_inc(S["scan_done"], 1)
            dve.wait_ge(S["y_ps"], NG // 4)
            link(nc.vector.scalar_tensor_tensor(cv[:, 0, :], xc[:], v("D_p"), ps[:, 4, :],
                                                ALU.mult, ALU.add))
            dve.wait_ge(S["gate_done"], 1)
            nc.vector.tensor_tensor(cv[:, 1, :], cv[:, 0, :], gate[:], ALU.mult
                                    ).then_inc(S["yv_done"], 1)
            dve.wait_ge(S["mo_ps"], 1)
            dve.wait_ge(S["res_ready"], 1)
            flat = lambda t: t[:, :, :].rearrange("p j d -> p (j d)")
            nc.vector.tensor_tensor(flat(x2), ps[:, 5, :], flat(resid), ALU.add
                                    ).then_inc(S["x2_done"], 1)
            dve.wait_ge(S["x2_done"], 1)
            layernorm("ln2", x2[:], normed)
            dve.wait_ge(ld["rope0"], 16)
            nc.vector.tensor_scalar(rope0[:, 1, :], rope0[:, 1, :], v("rope_sign"), None,
                                    ALU.mult).then_inc(S["rope_signed"], 1)
            dve.wait_ge(S["rope_signed"], 1)

            def rotary(c, b):
                n = B * c + b
                for i, dst in enumerate((kt1, kt2)):
                    dve.wait_ge(S["k0_ps"], 2 * n + i + 1)
                    if n >= 2:
                        dve.wait_ge(S["k0_done"], n - 1)
                    nc.vector.tensor_tensor(dst[:, n % 2, :], ps[:, 6 + i, :], rope0[:, i, :],
                                            ALU.mult).then_inc(S["k0_mul"], 1)

            for b in range(B):
                rotary(0, b)

            def add_and_norm(bank, ready, n, res, name, meanwhile=None):
                dve.wait_ge(S[ready], n)
                dve.wait_ge(S["res_ready"], res)
                link(nc.vector.tensor_tensor(flat(summed), ps[:, bank, :], flat(resid), ALU.add))
                layernorm(name, summed[:], x, meanwhile)

            add_and_norm(4, "ff2_ps", 1, 2, "post0", lambda: rotary(1, 0))

            def normed0(c, b):
                dve.wait_ge(S["o0_ps"], 2 * c + b + 1)
                dst = aoT[:, c, b * T:(b + 1) * T]
                link(nc.vector.reciprocal(dst, ps[:, 4 + b, T:2 * T]))
                nc.vector.tensor_tensor(dst, ps[:, 4 + b, 0:T], dst, ALU.mult
                                        ).then_inc(S["o0_norm"], 1)

            layernorm("lat", x[:], normed)
            for c in range(NPAIR):
                for u in range(4):
                    n = 4 * c + u
                    dve.wait_ge(S["e0_exp"], n + 1)
                    nc.vector.tensor_scalar(ex[:, n % 3, :], ex[:, n % 3, :], float(np.exp(CLIP)),
                                            float(np.exp(-CLIP)), ALU.min, ALU.max
                                            ).then_inc(S["e0_clip"], 1)
                    if u < 2 and 2 <= c + 1 < NPAIR or n == 1:
                        rotary(c + 1, u)
                    if u == 3:
                        normed0(c, 0)
                    if u == 1 and c:
                        normed0(c - 1, 1)
            normed0(NPAIR - 1, 1)
            add_and_norm(6, "y0_ps", 1, 3, "post1")

            dve.wait_ge(S["r0_ps"], 1)
            dve.wait_ge(consts, 7)
            link(nc.vector.tensor_copy(sc0[:, :, 0:E0], ps[:, 4, 0:NJ * E0].rearrange(
                "p (j e) -> p j e", j=NJ)))
            for j in range(NJ):
                ins = nc.vector.max(top0[:, j, :], sc0[:, j, 0:E0])
            link(ins)
            link(nc.vector.tensor_copy(pick0[:, :, 0:2], top0[:, :, 0:2]))
            for j in range(NJ):
                ins = nc.vector.match_replace(out=mark0[:, j, :], in_to_replace=pick0[:, j, :],
                                              in_values=sc0[:, j, :], imm_value=FAR)
            nc.vector.tensor_tensor(g0[:, 0], sc0[:, :, 0:E0],
                                    top0[:, :, 0:1].broadcast_to([P, NJ, E0]), ALU.subtract
                                    ).then_inc(S["r0_max"], 1)
            dve.wait_ge(S["r0_exp"], 1)
            dve.wait_ge(S["r0_max"], 1)
            link(nc.vector.scalar_tensor_tensor(g0[:, 2], mark0[:, :, 0:E0], 0.5 * FAR, g0[:, 1],
                                                ALU.is_ge, ALU.mult))
            link(nc.vector.tensor_reduce(den0[:, 0, :], g0[:, 2], AX.X, ALU.add))
            link(nc.vector.reciprocal(den0[:, 1, :], den0[:, 0, :]))
            link(nc.vector.tensor_tensor(
                g0[:, 3], g0[:, 2],
                den0[:, 1, :].rearrange("p (j o) -> p j o", o=1).broadcast_to([P, NJ, E0]), ALU.mult))
            for e in range(E0):
                dve.wait_ge(S["dn0_ps"], e + 1)
                if e:
                    dve.wait_ge(S["dn0_acc"], e)
                for j in range(NJ):
                    ins = nc.vector.scalar_tensor_tensor(
                        summed[:, j, :], ps[:, 5 + e % 2, j * D:(j + 1) * D], g0[:, 3, j, e:e + 1],
                        summed[:, j, :] if e else x[:, j, :], ALU.mult, ALU.add)
                ins.then_inc(S["dn0_acc"], 1)
                if e == 0:
                    dve.wait_ge(ld["mask"], 48)
                    nc.vector.tensor_scalar(mq[:], mq8[:], -BIG, None, ALU.mult
                                            ).then_inc(S["mask_done"], 1)
                    nc.vector.tensor_copy(mk[:], mk8[:]).then_inc(S["mask_done"], 1)
                if e == 1:
                    dve.wait_ge(S["kx_done"], 2)
                    dve.wait_ge(S["vx_ps"], 2)
                    split(kxf, [parts1["kx"][:, i, :] for i in range(3)], kxr, S["x_k_parts"])
            dve.wait_ge(S["dn0_acc"], E0)
            layernorm("post2", summed[:], x)

            def values_of(L):
                return v1[L][:, :, 0:H * 2 * DH].rearrange("p j (h w) -> p j h w", h=H)[:, :, :, 0:DH]

            def rotated(i, biases, dst, done):
                dve.wait_ge(S["qa_ps"], i + 1)
                cos = rope1[:, 0:1, :].broadcast_to([P, B, T])
                sin = rope1[:, 1:2, :].broadcast_to([P, B, T])
                by_b = lambda t: t.rearrange("p (b t) -> p b t", b=B)
                nc.vector.scalar_tensor_tensor(by_b(dtmp[:, 0, :]), by_b(ps[:, 4, :]), v(biases[1]),
                                               cos, ALU.add, ALU.mult)
                link(nc.vector.scalar_tensor_tensor(by_b(dtmp[:, 1, :]), by_b(ps[:, 5, :]),
                                                    v(biases[2]), sin, ALU.add, ALU.mult))
                link(nc.vector.scalar_tensor_tensor(dtmp[:, 2, :], ps[:, 3, :], v(biases[0]),
                                                    dtmp[:, 0, :], ALU.add, ALU.add))
                nc.vector.tensor_tensor(dst, dtmp[:, 2, :], dtmp[:, 1, :], ALU.add).then_inc(done, 1)
                dve.wait_ge(done, i + 1)

            dve.wait_ge(S["ones"], 1)
            for i in range(2):
                dve.wait_ge(S["vx_ps"], i + 1)
                nc.vector.tensor_tensor(
                    values_of("x")[:, 4 * i:4 * i + 4],
                    ps[:, 7 - 4 * i, :].rearrange("p (j h d) -> p j h d", j=4, h=H),
                    rv4("bv").rearrange("p j (h d) -> p j h d", h=H), ALU.add
                ).then_inc(S["vx_done"], 1)
            dve.wait_ge(ld["a1"], 48)
            rotated(0, ("Wu_q_b", "Wq_r_b", "Wq_s_b"), qf[:, 0, :], S["qa_done"])
            split(qf[:, 0, :], [parts1["qa"][:, i, :] for i in range(3)], cv[:, 0, :], S["a_q_parts"])
            rotated(1, ("Wu_k_b", "Wk_r_b", "Wk_s_b"), qf[:, 1, :], S["qa_done"])
            split(qf[:, 1, :], [parts1["ka"][:, i, :] for i in range(3)], cv[:, 1, :], S["a_k_parts"])
            dve.wait_ge(S["va_ps"], 1)
            nc.vector.tensor_tensor(
                values_of("a"), ps[:, 6, :].rearrange("p (j h d) -> p j h d", j=NJ, h=H),
                rv4("Wu_v_b").rearrange("p j (h d) -> p j h d", h=H), ALU.add
            ).then_inc(S["va_done"], 1)

            def row_max(L, m, k, i):
                heads, b = 512 // KEYS[L], k // 2
                q, h = divmod(i * heads, HB)
                h += HB * (k % 2)
                bank = row_bank(L, m)
                dve.wait_ge(S[f"{L}_smax_ps"], m + 1)
                dst = mx[L][:, 2 * b + q, h:h + heads]
                if L == "x":
                    nc.vector.tensor_tensor_reduce(ps[:, bank, :], ps[:, bank, :],
                                                   mq[:, 2 * b + q, :], 1.0, -FAR, ALU.add, ALU.max,
                                                   dst).then_inc(S[f"{L}_redmax"], 1)
                else:
                    nc.vector.tensor_reduce(
                        dst, ps[:, bank, :].rearrange("p (h k) -> p h k", h=heads), AX.X, ALU.max
                    ).then_inc(S[f"{L}_redmax"], 1)

            def minus_max(L, k):
                m = k % 2
                dve.wait_ge(S[f"{L}_mT_ps"], k + 1)
                if k >= 2:
                    dve.wait_ge(S[f"{L}_nm_stack{m}"], 16 * PARTS * (k // 2))
                link(nc.vector.tensor_scalar(nm[:, m, 0, :], ps[0:HB, MT_BANK[k], 0:T], -1.0, None,
                                             ALU.mult))
                split(nm[:, m, 0, :], [nmp[:, m, i, :] for i in range(3)],
                      nm[:, m, 1, :], S[f"{L}_nm_done"])

            def attend(L, factor):
                nk = KEYS[L] // P
                for m in range(row_steps(L) + AHEAD[L]):
                    k, i = divmod(m, row_steps(L))
                    row_max(L, m, k, i)
                    if i == row_steps(L) - 1:
                        minus_max(L, k)
                for n in range(B * 4 * nk):
                    for m, k, i in rows_beside(L, n):
                        row_max(L, m, k, i)
                    if n % nk == nk - 1:
                        i = n // nk
                        b, g = divmod(i, H // 4)
                        dve.wait_ge(S[f"{L}_e_used"], n + 1)
                        nc.vector.tensor_copy(og[:, g, b * T:(b + 1) * T], ps[:, 4 + i % 2, 0:T]
                                              ).then_inc(S[f"{L}_o_sb"], 1)
                    for k in last_rows(L, n):
                        minus_max(L, k)
                for g in range(H // 4):
                    dve.wait_ge(S[f"{L}_oT_ps"], g + 1)
                    t = ps[:, 6 + g % 2, :].rearrange("p (j h r) -> p j h r", j=NJ, h=4)
                    rd = rden[:, :, 4 * g:4 * g + 4]
                    link(nc.vector.reciprocal(rd, t[:, :, :, DH]))
                    if factor != 1.0:
                        link(nc.vector.tensor_scalar(rd, rd, factor, None, ALU.mult))
                    for j in range(NJ):
                        ins = nc.vector.tensor_tensor(
                            ao1[:, j, 4 * g:4 * g + 4, :], t[:, j, :, 0:DH],
                            rden[:, j, 4 * g:4 * g + 4].rearrange("p (h o) -> p h o", o=1)
                            .broadcast_to([P, 4, DH]), ALU.mult)
                    ins.then_inc(S[f"{L}_o_norm"], 1)

            attend("a", 1.0)
            add_and_norm(7, "a_y_ps", 1, 4, "post3")

            dve.wait_ge(S["qx_ps"], 1)
            nc.vector.tensor_scalar(qf[:, 0, :], ps[:, 4, :], v("bq"), None, ALU.add
                                    ).then_inc(S["qx_done"], 1)
            dve.wait_ge(S["qx_done"], 1)
            dve.wait_ge(S["a_q_scr"], 16)
            split(qf[:, 0, :], [parts1["qx"][:, i, :] for i in range(3)], cv[:, 0, :], S["x_q_parts"])
            attend("x", 1.0 / float(np.sqrt(np.float32(DH))))
            add_and_norm(7, "x_y_ps", 1, 5, "post4")

            dve.wait_ge(S["g1_exp"], 1)
            link(nc.vector.tensor_scalar(lg1[:, 1], lg1[:, 0], 1.0, None, ALU.add))
            link(nc.vector.reciprocal(lg1[:, 2], lg1[:, 1]))
            dve.wait_ge(ld["e1"], 16 * 6)
            link(nc.vector.tensor_tensor(lg1[:, 3], lg1[:, 2],
                                         eb[:, :].rearrange("p (o e) -> p o e", o=1)
                                         .broadcast_to([P, NJ, E1]), ALU.add))
            sc = lg1[:, 3].rearrange("p j (g i) -> p j g i", i=4)
            best, other = pr1[:, 0], pr1[:, 1]
            link(nc.vector.tensor_tensor(best, sc[:, :, :, 0], sc[:, :, :, 1], ALU.add))
            for i, k in ((0, 2), (0, 3), (1, 2), (1, 3), (2, 3)):
                link(nc.vector.tensor_tensor(other, sc[:, :, :, i], sc[:, :, :, k], ALU.add))
                link(nc.vector.tensor_tensor(best, best, other, ALU.max))
            dve.wait_ge(consts, 7)
            link(nc.vector.tensor_copy(r1[:, 0, :, 0:8], best))
            for j in range(NJ):
                ins = nc.vector.max(t1[:, 0, j, :], best[:, j, :])
            link(ins)
            link(nc.vector.tensor_copy(t1[:, 1, :, 0:4], t1[:, 0, :, 0:4]))
            for j in range(NJ):
                ins = nc.vector.match_replace(out=r1[:, 1, j, :], in_to_replace=t1[:, 1, j, :],
                                              in_values=r1[:, 0, j, :], imm_value=FAR)
            link(ins)
            link(nc.vector.tensor_scalar(best, r1[:, 1, :, 0:8], 0.5 * FAR, None, ALU.is_ge))
            for j in range(NJ):
                ins = nc.vector.tensor_tensor(
                    sel1[:, 0, j, 0:E1].rearrange("p (g i) -> p g i", i=4), sc[:, j],
                    best[:, j, :].rearrange("p (g o) -> p g o", o=1).broadcast_to([P, 8, 4]),
                    ALU.mult)
            link(ins)
            for j in range(NJ):
                ins = nc.vector.max(t1[:, 2, j, :], sel1[:, 0, j, 0:E1])
            link(ins)
            link(nc.vector.tensor_copy(t1[:, 3, :, 0:6], t1[:, 2, :, 0:6]))
            for j in range(NJ):
                ins = nc.vector.match_replace(out=sel1[:, 1, j, :], in_to_replace=t1[:, 3, j, :],
                                              in_values=sel1[:, 0, j, :], imm_value=FAR)
            link(ins)
            link(nc.vector.scalar_tensor_tensor(lg1[:, 0], sel1[:, 1, :, 0:E1], 0.5 * FAR, lg1[:, 2],
                                                ALU.is_ge, ALU.mult))
            link(nc.vector.tensor_reduce(den0[:, 0, :], lg1[:, 0], AX.X, ALU.add))
            link(nc.vector.tensor_scalar(den0[:, 0, :], den0[:, 0, :], 1e-20, None, ALU.add))
            link(nc.vector.reciprocal(den0[:, 1, :], den0[:, 0, :]))
            link(nc.vector.tensor_tensor(
                lg1[:, 1], lg1[:, 0],
                den0[:, 1, :].rearrange("p (j o) -> p j o", o=1).broadcast_to([P, NJ, E1]),
                ALU.mult))
            nc.vector.tensor_scalar(cmb[:], lg1[:, 1], 2.5, None, ALU.mult).then_inc(S["cmb_done"], 1)
            dve.wait_ge(S["cmbT_ps"], 1)
            link(nc.vector.tensor_copy(cmp_[:, 0, :], ps[0:E1, 4, :]))
            link(nc.vector.tensor_tensor(cmf[:, 1, :], ps[0:E1, 4, :], cmp_[:, 0, :], ALU.subtract))
            link(nc.vector.tensor_copy(cmp_[:, 1, :], cmf[:, 1, :]))
            link(nc.vector.tensor_tensor(cmp_[:, 2, :], cmf[:, 1, :], cmp_[:, 1, :], ALU.subtract))
            for i in range(PARTS):
                ins = nc.vector.tensor_copy(cms[E1 * i:E1 * (i + 1), :], cmp_[:, i, :])
            ins.then_inc(S["cms_done"], 1)
            for c in range(C1):
                dve.wait_ge(S["cb_ps"], c + 1)
                dve.wait_ge(S["sq_even"], (SH + c) // 2 + 1)
                if (SH + c) % 2:
                    dve.wait_ge(S["sq_odd"], (SH + c) // 2 + 1)
                nc.vector.tensor_tensor(hh[:, c, :], ps[:, 5 + c % 2, :], hh[:, c, :],
                                        ALU.mult).then_inc(S["h1_done"], 1)
            dve.wait_ge(S["y1_ps"], 1)
            link(nc.vector.tensor_tensor(flat(summed), ps[:, 7, :], flat(x), ALU.add))
            layernorm("post5", summed[:], normed)

        @block.tensor
        def _(pe):
            def mm(o, lhsT, rhs, start=True, stop=True, shared=False):
                return nc.tensor.matmul(o, lhsT, rhs, start=start, stop=stop, skip_group_check=shared)

            def to_cols(bank, src, done, norm=None):
                for j in range(NJ):
                    if norm:
                        pe.wait_ge(norm_out, normed_tiles(norm, j))
                    ins = nc.tensor.transpose(ps[:, bank, j * P:(j + 1) * P], src[:, j, :], ident[:])
                ins.then_inc(S[done], 1)

            def to_rows(bank, cols, w, done):
                for j in range(NJ):
                    for c, (lhs, rhs) in enumerate(zip(cols, w)):
                        ins = mm(ps[:, bank, j * D:(j + 1) * D], lhs[:, j * P:(j + 1) * P], rhs,
                                 c == 0, c == len(w) - 1)
                ins.then_inc(S[done], 1)

            pe.wait_ge(ld["ident"], 16)
            to_cols(0, normed, "xmT_ps", "ln")
            pe.wait_ge(ld["mix"], 16)
            pe.wait_ge(S["xmT"], 1)
            mm(ps[:, 1, :], w_mix[:, 0, :], xT[:]).then_inc(S["w1_ps"], 1)
            mm(ps[:, 2, :], w_mix[:, 1, :], xT[:]).then_inc(S["v1_ps"], 1)
            pe.wait_ge(norm_out, normed_tiles("ctx"))
            for i in range(2):
                to_cols(6 + i, cx[:, 4 * i:4 * i + 4, :], "cxnT_ps")
            pe.wait_ge(S["xc_done"], 1)
            mm(ps[:, 3, :], w_mix[:, 2, :], xc[:]).then_inc(S["dt_ps"], 1)
            mm(ps[:, 4, :], w_mix[:, 3, :], xc[:])
            mm(ps[:, 5, :], w_mix[:, 4, :], xc[:]).then_inc(S["BC_ps"], 1)
            pe.wait_ge(ld["sel"], 32)
            pe.wait_ge(S["delta_parts"], 1)
            pe.wait_ge(S["gate_done"], 1)

            def y_of(s0):
                pe.wait_ge(S["hC_done"], s0 + 4)
                if s0 == 0:
                    pe.wait_ge(S["BC_done"], 2)
                for q in range(4):
                    ins = mm(ps[32 * q:32 * q + 32, 4, :], sel_y[:, s0 // 4, :],
                             hC[:, (s0 + q) % 8, :], s0 == 0, s0 == NG - 4)
                ins.then_inc(S["y_ps"], 1)

            for s, g in enumerate(ORDER):
                if s >= 2:
                    pe.wait_ge(S["dA_done"], s - 1)
                for i in range(PARTS):
                    ins = mm(ps[:, s % 2, :], sel_g[:, g, :], dparts[:, 0, i, :], i == 0,
                             i == PARTS - 1)
                ins.then_inc(S["spread_d"], 1)
                if s == 0:
                    pe.wait_ge(S["dx_parts"], 1)
                if s >= 2:
                    pe.wait_ge(S["dBx_done"], s - 1)
                for i in range(PARTS):
                    ins = mm(ps[:, 2 + s % 2, :], sel_g[:, g, :], dparts[:, 1, i, :], i == 0,
                             i == PARTS - 1)
                ins.then_inc(S["spread_x"], 1)
                if s % 4 == 1 and s > 4:
                    y_of(s - 5)
            def project0(c, step):
                if step < 2:
                    n = B * c + step
                    for i in range(2):
                        if n:
                            pe.wait_ge(S["k0_mul"], 2 * (n - 1) + i + 1)
                        if step == 0:
                            pe.wait_ge(S["v0_done"], 2 * (c if c >= 2 else c + 1))
                            if c >= 2:
                                pe.wait_ge(S["q0_done"], c)
                        mm(ps[:, 6 + i, :], w_x0[:, c, i, :], cxnT[:, step * CS:(step + 1) * CS]
                           ).then_inc(S["k0_ps"], 1)
                elif step == 2:
                    pe.wait_ge(S["k0_mul"], 2 * (B * c + 1) + 2)
                    mm(ps[:, 6, :], w_x0[:, c, 3, :], xT[:]).then_inc(S["q0_ps"], 1)
                    values0(c, 0)
                else:
                    pe.wait_ge(S["q0_done"], c + 1)
                    values0(c, 1)

            def values0(c, i):
                for k in range(4):
                    t = 4 * i + k
                    ins = mm(ps[:, 7 - i, k * P:(k + 1) * P], cxnT[:, t * P:(t + 1) * P],
                             w_x0[:, c, 2, :])
                ins.then_inc(S["v0_ps"], 1)

            pe.wait_ge(ld["x0"], 16)
            pe.wait_ge(S["cxnT_done"], 2)
            for i in range(B):
                values0(0, i)
            y_of(NG - 4)
            pe.wait_ge(S["yv_done"], 1)
            to_rows(5, [cv[:, 1, :]], [w_mix[:, 5, :]], "mo_ps")
            project0(0, 0)
            to_cols(0, normed, "hT_ps", "ln2")
            pe.wait_ge(ld["ff"], 16)
            pe.wait_ge(S["hT"], 1)
            for c in range(FF):
                mm(ps[:, 1 + c, :], w_ff[:, c, :], xT[:]).then_inc(S["ff_ps"], 1)
            project0(0, 1)
            pe.wait_ge(S["ff_act"], FF)
            to_rows(4, [ffh[:, c, :] for c in range(FF)], [w_ff[:, FF + c, :] for c in range(FF)],
                    "ff2_ps")
            def logits0(n):
                c, u = divmod(n, 4)
                b, s = divmod(u, 2)
                if n >= 2:
                    pe.wait_ge(S["e0_exp"], n - 1)
                for r in range(2):
                    for k in range(2):
                        at = b * CS + (2 * s + k) * P
                        ins = mm(ps[:, 2 * (n % 2) + r, k * T:(k + 1) * T],
                                 kT0[64 * r:64 * r + 64, c % 2, at:at + P],
                                 qT0[64 * r:64 * r + 64, c % 2, b * T:(b + 1) * T])
                ins.then_inc(S["s0_ps"], 1)

            def mix0(n):
                c, u = divmod(n, 4)
                b, s = divmod(u, 2)
                pe.wait_ge(S["e0_clip"], n + 1)
                if s == 0 and c:
                    pe.wait_ge(S["o0_norm"], 2 * (c - 1) + b + 1)
                for k in range(2):
                    for r in range(2):
                        e = ex[:, n % 3, r * 512 + k * T:r * 512 + (k + 1) * T]
                        ins = mm(ps[64 * r:64 * r + 64, 4 + b, 0:T],
                                 v0[:, c % 2, 4 * b + 2 * s + k, r, :], e, s == k == 0, False, True)
                ins.then_inc(S["e0_used"], 1)

            def output0(c):
                pe.wait_ge(S["o0_norm"], 2 * (c + 1))
                if c == 0:
                    pe.wait_ge(S["v0_done"], 2 * NPAIR)
                for j in range(NJ):
                    ins = mm(ps[:, 6, j * D:(j + 1) * D], aoT[:, c, j * P:(j + 1) * P],
                             w_x0[:, c, 4, :], c == j == 0, c == NPAIR - 1 and j == NJ - 1, True)
                return ins

            def denominators0(c, b):
                pe.wait_ge(S["e0_tot"], 2 * c + b + 1)
                for r in range(2):
                    ins = mm(ps[64 * r:64 * r + 64, 4 + b, T:2 * T], ones0,
                             etot[:, b, r * T:(r + 1) * T], False, True, True)
                ins.then_inc(S["o0_ps"], 1)

            pe.wait_ge(S["k0_mul"], 4)
            for i in range(B):
                values0(1, i)
            project0(1, 0)
            to_cols(0, normed, "latT_ps", "lat")
            pe.wait_ge(S["latT"], 1)
            mm(ps[:, 3, :], w_x0[:, 0, 3, :], xT[:]).then_inc(S["q0_ps"], 1)
            pe.wait_ge(S["k0_done"], 2)
            pe.wait_ge(S["q0_done"], 1)
            pe.wait_ge(consts, 7)
            logits0(0)
            for n in range(4 * NPAIR):
                c, u = divmod(n, 4)
                if 2 <= c + 1 < NPAIR or n == 1:
                    project0(c + 1, u)
                elif n == 2:
                    pe.wait_ge(S["k0_mul"], 8)
                    mm(ps[:, 6, :], w_x0[:, 1, 3, :], xT[:]).then_inc(S["q0_ps"], 1)
                elif c + 1 == NPAIR:
                    for i in range(2 * u, min(2 * u + 2, NPAIR - 1)):
                        output0(i)
                if n + 1 < 4 * NPAIR:
                    if u == 3:
                        pe.wait_ge(S["k0_done"], 2 * (c + 2))
                    logits0(n + 1)
                if u == 0:
                    pe.wait_ge(S["v0_done"], 2 * (c + 1))
                mix0(n)
                if u == 2:
                    denominators0(c, 0)
                if u == 0 and c:
                    denominators0(c - 1, 1)
            denominators0(NPAIR - 1, 1)
            output0(NPAIR - 1).then_inc(S["y0_ps"], 1)
            pe.wait_ge(ld["x1"], 16)
            pe.wait_ge(ld["cxT"], 16)
            for i in range(2):
                mm(ps[:, 4 + i, :], w_x1[:, 1, :], cxT[:, i * 512:(i + 1) * 512]
                   ).then_inc(S["kx_ps"], 1)
            for i in range(2):
                for k in range(4):
                    t = 4 * i + k
                    ins = mm(ps[:, 7 - 4 * i, k * P:(k + 1) * P], cxT[:, t * P:(t + 1) * P],
                             w_x1[:, 2, :])
                ins.then_inc(S["vx_ps"], 1)
            to_cols(0, x, "xT_ps", "post1")
            pe.wait_ge(ld["e0"], 48)
            pe.wait_ge(S["xT_done"], 1)
            pe.wait_ge(S["kx_done"], 2)
            for j in range(NJ):
                ins = mm(ps[:, 4, j * E0:(j + 1) * E0], xT[:, j * P:(j + 1) * P], w_r0[:])
            ins.then_inc(S["r0_ps"], 1)

            def up0(e):
                for c in range(F0):
                    n = F0 * e + c
                    if n >= 3:
                        pe.wait_ge(S["up0_act"], n - 2)
                    mm(ps[:, n % 3, :], w_up0[:, e, c * P:(c + 1) * P], xT[:]
                       ).then_inc(S["up0_ps"], 1)

            up0(0)
            for e in range(E0):
                if e + 1 < E0:
                    up0(e + 1)
                pe.wait_ge(S["up0_act"], F0 * (e + 1))
                if e >= 2:
                    pe.wait_ge(S["dn0_acc"], e - 1)
                to_rows(5 + e % 2, [eh0[:, e % 2, c, :] for c in range(F0)],
                        [w_dn0[:, e, c, :] for c in range(F0)], "dn0_ps")
            to_cols(0, x, "xT_ps", "post2")
            pe.wait_ge(ld["a1"], 48)
            pe.wait_ge(S["xT_done"], 2)
            for i in range(2):
                mm(ps[0:64, 1 + i, :], w_a1[:, 64 * i:64 * i + 64], xT[:]).then_inc(S["cdown_ps"], 1)
            pe.wait_ge(S["cdown_done"], 1)
            pe.wait_ge(S["vx_done"], 2)
            for i in range(3):
                ins = mm(ps[:, 3 + i, :], w_u1[:, i, :], cq[:, 0, :])
            ins.then_inc(S["qa_ps"], 1)
            pe.wait_ge(S["cdown_done"], 2)
            for j in range(NJ):
                ins = mm(ps[:, 6, j * D:(j + 1) * D], cq[:, 1, j * P:(j + 1) * P], w_u1[:, 4, :])
            ins.then_inc(S["va_ps"], 1)
            pe.wait_ge(S["qa_done"], 1)
            mm(ps[:, 3, :], w_u1[:, 3, :], cq[:, 1, :])
            mm(ps[:, 4, :], w_a1[:, 128:256], xT[:])
            mm(ps[:, 5, :], w_a1[:, 256:384], xT[:]).then_inc(S["qa_ps"], 1)

            def attend(L):
                heads, nk = 512 // KEYS[L], KEYS[L] // P
                pe.wait_ge(S[f"{L}_q_stack"], 16 * PARTS * PARTS)
                pe.wait_ge(S[f"{L}_k_stack"], 16 * PARTS * PARTS)
                pe.wait_ge(ld[f"ones_{L}"], 16)

                def rows(m, k, i):
                    b = k // 2
                    q, h0 = divmod(i * heads, HB)
                    h0 += HB * (k % 2)
                    j = 2 * b + q
                    bank = row_bank(L, m)
                    if m >= 4:
                        pe.wait_ge(S[f"{L}_redmax"], m - (1 if bank >= 6 else 3))
                    if bank == 7:
                        pe.wait_ge(S[f"{L}_nm_done"], k)
                    for h in range(heads):
                        ins = mm(ps[:, bank, h * KEYS[L]:(h + 1) * KEYS[L]],
                                 qs[0:STACK, h0 + h, j * P:(j + 1) * P],
                                 ks[L][0:STACK, h0 + h, b * KEYS[L]:(b + 1) * KEYS[L]])
                    ins.then_inc(S[f"{L}_smax_ps"], 1)

                def max_cols(k):
                    b, h0 = k // 2, HB * (k % 2)
                    pe.wait_ge(S[f"{L}_redmax"], (k + 1) * row_steps(L))
                    for q in range(2):
                        ins = nc.tensor.transpose(ps[0:HB, MT_BANK[k], q * P:(q + 1) * P],
                                                  mx[L][:, 2 * b + q, h0:h0 + HB], ident[:])
                    ins.then_inc(S[f"{L}_mT_ps"], 1)

                def logits(n):
                    b, g, k = n // (4 * nk), n // nk % 4, n % nk
                    if n >= 2:
                        pe.wait_ge(S[f"{L}_e_exp"], n - 1)
                    if g % 2 == 0 and k == 0:
                        pe.wait_ge(S[f"{L}_nm_stack{g // 2}"], 16 * PARTS * (b + 1))
                    rows = STACK + PARTS
                    for r in range(2):
                        bank = 2 * (n % 2) + r
                        for i in range(2):
                            h = 4 * g + 2 * r + i
                            ins = mm(ps[:, bank, i * T:(i + 1) * T],
                                     ks[L][0:rows, h, b * KEYS[L] + k * P:b * KEYS[L] + (k + 1) * P],
                                     qs[0:rows, h, b * T:(b + 1) * T], L == "a" or i == 0, L == "a", L == "x")
                        if L == "x":
                            for i in range(2):
                                ins = mm(ps[:, bank, i * T:(i + 1) * T], neg_i[:], mk[:, b, k, :],
                                         False, i == 1, True)
                    ins.then_inc(S[f"{L}_s_ps"], 1)

                def values(n):
                    b, g, k = n // (4 * nk), n // nk % 4, n % nk
                    i = n // nk
                    pe.wait_ge(S[f"{L}_e_exp"], n + 1)
                    if k == 0 and i >= 2:
                        pe.wait_ge(S[f"{L}_o_sb"], i - 1)
                    if n == 0:
                        pe.wait_ge(S[f"{L}_nm_done"], 1)
                    for r in range(4):
                        ins = mm(ps[32 * r:32 * r + 32, 4 + i % 2, 0:T],
                                 v1[L][:, b * nk + k, 2 * DH * (4 * g + r):2 * DH * (4 * g + r) + 32],
                             ex1[:, n % 3, r * T:(r + 1) * T],
                                 k == 0, k == nk - 1)
                    ins.then_inc(S[f"{L}_e_used"], 1)

                total = B * 4 * nk
                for m in range(row_steps(L) + AHEAD[L]):
                    k, i = divmod(m, row_steps(L))
                    rows(m, k, i)
                    if i == row_steps(L) - 1:
                        max_cols(k)
                pe.wait_ge(S[f"{L}_redmax"], row_steps(L) + AHEAD[L])
                logits(0)
                for n in range(total):
                    if n + 1 < total:
                        logits(n + 1)
                    for m, k, i in rows_beside(L, n):
                        rows(m, k, i)
                    values(n)
                    for k in last_rows(L, n):
                        max_cols(k)
                pe.wait_ge(S[f"{L}_nm_done"], NB)
                for g in range(4):
                    pe.wait_ge(S[f"{L}_o_sb"], 4 + g + 1)
                    if g >= 2:
                        pe.wait_ge(S[f"{L}_o_norm"], g - 1)
                    for j in range(NJ):
                        ins = nc.tensor.transpose(ps[:, 6 + g % 2, j * P:(j + 1) * P],
                                                  og[:, g, j * P:(j + 1) * P], ident[:])
                    ins.then_inc(S[f"{L}_oT_ps"], 1)
                pe.wait_ge(S[f"{L}_o_norm"], 4)
                for j in range(NJ):
                    ins = nc.tensor.transpose(ps[:, 6, j * P:(j + 1) * P],
                                              ao1[:, j, :, :].rearrange("p h d -> p (h d)"), ident[:])
                ins.then_inc(S[f"{L}_aT_ps"], 1)
                pe.wait_ge(S[f"{L}_aT_done"], 1)
                w_o = w_a1[:, 384:512] if L == "a" else w_x1[:, 3, :]
                to_rows(7, [aoT1], [w_o], f"{L}_y_ps")

            pe.wait_ge(S["va_done"], 1)
            attend("a")
            to_cols(0, x, "xT_ps", "post3")
            pe.wait_ge(S["xT_done"], 3)
            mm(ps[:, 4, :], w_x1[:, 0, :], xT[:]).then_inc(S["qx_ps"], 1)
            pe.wait_ge(S["mask_done"], 2)
            pe.wait_ge(S["vx_done"], 2)
            attend("x")
            to_cols(0, x, "xT_ps", "post4")
            pe.wait_ge(ld["e1"], 96)
            pe.wait_ge(S["xT_done"], 4)
            for j in range(NJ):
                ins = mm(ps[:, 1, j * E1:(j + 1) * E1], xT[:, j * P:(j + 1) * P], w_g1[:])
            ins.then_inc(S["g1_ps"], 1)

            def up1(m):
                if m == 3:
                    pe.wait_ge(S["g1_exp"], 1)
                if m >= 4:
                    pe.wait_ge(S["relu_done"], m - 3)
                w = w_sh[:, m, :] if m < SH else w_up1[:, m - SH, :]
                mm(ps[:, UP1[m % 4], :], w, xT[:]).then_inc(S["up1_ps"], 1)

            def down1(m):
                w = w_sh[:, SH + m, :] if m < SH else w_dn1[:, m - SH, :]
                for j in range(NJ):
                    ins = mm(ps[:, 7, j * D:(j + 1) * D], hidden(m)[:, j * P:(j + 1) * P], w,
                             m == j == 0, m == SH + C1 - 1 and j == NJ - 1, True)
                return ins

            EARLY = 12
            for m in range(EARLY):
                up1(m)
            pe.wait_ge(S["cmb_done"], 1)
            for j in range(NJ):
                ins = nc.tensor.transpose(ps[0:E1, 4, j * P:(j + 1) * P], cmb[:, j, :], ident[:])
            ins.then_inc(S["cmbT_ps"], 1)
            for m in range(EARLY, SH + C1):
                up1(m)
            pe.wait_ge(S["sq_even"], (SH + 1) // 2)
            pe.wait_ge(S["sq_odd"], SH // 2)
            for m in range(SH):
                down1(m)
            pe.wait_ge(S["cms_done"], 1)
            for c in range(C1 + 1):
                if c < C1:
                    if c >= 2:
                        pe.wait_ge(S["h1_done"], c - 1)
                    mm(ps[:, 5 + c % 2, :], sel_e[:, c, :], cms[:]).then_inc(S["cb_ps"], 1)
                if c:
                    pe.wait_ge(S["h1_done"], c)
                    ins = down1(SH + c - 1)
            ins.then_inc(S["y1_ps"], 1)


def _constants():
    bf16 = mybir.dt.np(mybir.dt.bfloat16)
    p = np.arange(P)
    c = {"ident": np.eye(P, dtype=np.float32), "neg_i": (-BIG * np.eye(P)).astype(bf16)}
    sel = np.zeros((P, NG, P))
    for g in range(NG):
        sel[g * GD + p // STATE, g, p] = 1
    c["sel_g"] = sel.astype(bf16)
    sel = np.zeros((P, NG // 4, 32), np.float32)
    for i in range(NG // 4):
        sel[p, i, GD * i + p // STATE] = 1
    c["sel_y"] = sel
    sel = np.zeros((PARTS, E1, C1, P))
    for i in range(C1):
        sel[:, 2 * i + p // I1, i, p] = 1
    c["sel_e"] = sel.reshape(PARTS * E1, C1, P).astype(bf16)
    c["ones"] = np.ones((PARTS, H, B * CS), bf16)
    ids = np.arange(D // 2, dtype=np.float32)
    theta = np.float32(10000.0) ** (np.float32(-2.0) * ids) / np.float32(D // 2)
    r = np.arange(T, dtype=np.float32)[None, :] * theta[:, None].astype(np.float32)
    cos, sin = np.repeat(np.cos(r), 2, 0), np.repeat(np.sin(r), 2, 0)
    sign = np.where(p % 2 == 0, -1.0, 1.0)[:, None]
    c["rope1"] = np.stack([cos, sin * sign], 1).astype(np.float32)
    c["rope_sign"] = np.where(p % DH0 < DH0 // 2, -1.0, 1.0).astype(np.float32)[:, None]
    return c


def _layout(i):
    c = _constants()
    i = {k: np.asarray(x) for k, x in i.items()}
    L0, X0, F, L1, X1, F1 = (lambda k, q=q: i[q + k] for q in (
        "L0_attn_", "L0_xattn_", "L0_ffn_", "L1_attn_", "L1_xattn_", "L1_ffn_"))
    col = lambda x: x.reshape(-1, 1)
    pad = lambda x: np.concatenate([x, np.zeros(P - len(x), x.dtype)]).reshape(-1, 1)
    half = np.arange(P) ^ (DH0 // 2)
    pair = np.arange(P) ^ 1
    a_log = L0("A_log")
    cols = {
        "w1_b": col(L0("w1_b")), "v1_b": col(L0("v1_b")), "ln_g": col(L0("ln_g")),
        "ln_b": col(L0("ln_b")), "conv": L0("conv_w")[:, 0, :], "dt_b": col(L0("dt_b")),
        "Bp_b": col(np.tile(L0("Bp_b"), GD)), "Cp_b": col(np.tile(L0("Cp_b"), GD)),
        "A_log": a_log.reshape(NG, P).T, "D_p": col(L0("D_p")),
        "ln2_g": col(L0("ln2_g")), "ln2_b": col(L0("ln2_b")), "ff1_b": L0("ff1_b").reshape(FF, P).T,
        "lat_g": col(X0("ln_lat_g")), "lat_b": col(X0("ln_lat_b")), "ctx_g": col(X0("ln_ctx_g")),
        "ctx_b": col(X0("ln_ctx_b")), "rope_sign": c.pop("rope_sign"), "Wd_q_b": pad(L1("Wd_q_b")),
        "Wd_kv_b": pad(L1("Wd_kv_b")), "Wu_q_b": col(L1("Wu_q_b")), "Wq_r_b": col(L1("Wq_r_b")),
        "Wq_s_b": col(L1("Wq_r_b")[pair]), "Wu_k_b": col(L1("Wu_k_b")), "Wk_r_b": col(L1("Wk_r_b")),
        "Wk_s_b": col(L1("Wk_r_b")[pair]), "bq": col(X1("bq")), "bk": col(X1("bk")),
    }
    chunks = lambda w: w.reshape(-1, P, w.shape[-1]).transpose(1, 0, 2)
    a = dict(c)
    a["vec"] = np.concatenate([cols[k] for k in VEC], 1)
    a["rowv"] = np.stack([L0("ln1_g"), L0("ln1_b"), L0("w2_b"), L0("ff2_b"), X0("bo"), L1("Wu_v_b"),
                          L1("Wo_b"), X1("bv").reshape(D), X1("bo")])
    a["x"] = i["x"].reshape(NJ, P, D).transpose(1, 0, 2)
    a["cx"] = i["ctx_1024"].reshape(NC_TILES, P, D).transpose(1, 0, 2)
    a["cxT"] = i["ctx_1024"].reshape(B * CS, D).T
    a["w_mix"] = np.stack([L0("w1_w"), L0("v1_w"), L0("dt_w"), np.tile(L0("Bp_w"), (1, GD)),
                           np.tile(L0("Cp_w"), (1, GD)), L0("w2_w")], 1)
    a["w_ff"] = np.concatenate([L0("ff1_w").reshape(D, FF, P), chunks(L0("ff2_w"))], 1)
    a["rope0"] = np.stack([np.tile(X0("cos").T, (4, 1)), np.tile(X0("sin").T, (4, 1))], 1)
    wk, wv = X0("Wkv")[:, :1024].reshape(D, NPAIR, P), X0("Wkv")[:, 1024:].reshape(D, NPAIR, P)
    a["w_x0"] = np.stack([wk, wk[:, :, half], wv, X0("Wq").reshape(D, NPAIR, P), chunks(X0("Wo"))], 2)
    a["w_r0"] = F("router_w").T
    a["w_up0"] = F("expert_w1").transpose(2, 0, 1)
    a["w_dn0"] = F("expert_w2").reshape(E0, D, F0, P).transpose(3, 0, 2, 1)
    a["w_a1"] = np.concatenate([L1("Wd_q_w"), L1("Wd_kv_w"), L1("Wk_r_w"), L1("Wk_r_w")[:, pair],
                                L1("Wo_w")], 1)
    a["w_u1"] = np.stack([L1("Wu_q_w"), L1("Wq_r_w"), L1("Wq_r_w")[:, pair], L1("Wu_k_w"),
                          L1("Wu_v_w")], 1)
    a["w_x1"] = np.stack([X1("Wq").reshape(D, D), X1("Wk").reshape(D, D), X1("Wv").reshape(D, D),
                          X1("Wo").reshape(D, D)], 1)
    mask = i["mask_BxSxS2_bk1"]
    a["mq8"] = mask.reshape(NJ, P, CS).transpose(1, 0, 2)
    a["mk8"] = mask.reshape(B, T, CS // P, P).transpose(3, 0, 2, 1)
    a["w_g1"] = F1("gate_w").T
    a["eb"] = F1("e_bias")
    a["w_up1"] = F1("up_w").reshape(C1, P, D).transpose(2, 0, 1)
    a["w_dn1"] = F1("down_w").transpose(0, 2, 1).reshape(C1, P, D).transpose(1, 0, 2)
    a["w_sh"] = np.concatenate([F1("shared_up_w").reshape(SH, P, D).transpose(2, 0, 1),
                                chunks(F1("shared_down_w").T)], 1)
    return {k: np.ascontiguousarray(x) for k, x in a.items()}


def kernel(**inputs):
    import concourse.bacc as bacc
    from concourse.bass_utils import run_bass_kernel_spmd

    nc = bacc.Bacc("TRN2", target_bir_lowering=False, num_devices=1)
    arrays = _layout(inputs)
    aps = {k: nc.dram_tensor(f"in_{k}", x.shape, mybir.dt.from_np(x.dtype), kind="ExternalInput").ap()
           for k, x in arrays.items()}
    out = nc.dram_tensor("out", (P, NJ, D), mybir.dt.float32, kind="ExternalOutput").ap()
    program(nc, aps, out)
    r = run_bass_kernel_spmd(nc, [{f"in_{k}": x for k, x in arrays.items()}], core_ids=[0])
    return r.results[0]["out"].transpose(1, 0, 2).reshape(B, T, D)
```

```python
from contextlib import ExitStack

import numpy as np

from concourse import mybir

P = 128
D = 128
B, T = 2, 256
N = B * T
NJ = N // P
CS = 512
NC_TILES = B * CS // P
STATE = 16
GD = P // STATE
NG = D // GD
H = 16
DH0 = 64
DH = 8
NPAIR = H // 2
HB = H // 2
NB = 2 * B
FF = 3
E0, F0 = 8, 512 // P
E1, I1 = 32, 64
C1 = E1 * I1 // P
SH = 256 // P
PARTS = 3
STACK = PARTS * PARTS * DH
EPS = 1e-5
CLIP = 11.0
BIG = 2.0 ** 100
FAR = 3.0e38

VEC = {}
for _name, _width in (
    ("w1_b", 1), ("v1_b", 1), ("ln_g", 1), ("ln_b", 1), ("conv", 3), ("dt_b", 1), ("Bp_b", 1),
    ("Cp_b", 1), ("A_log", NG), ("D_p", 1), ("ln2_g", 1), ("ln2_b", 1), ("ff1_b", FF),
    ("lat_g", 1), ("lat_b", 1), ("ctx_g", 1), ("ctx_b", 1), ("rope_sign", 1), ("Wd_b", 1),
    ("Wu_q_b", 1), ("Wq_r_b", 1), ("Wq_s_b", 1), ("Wu_k_b", 1), ("Wk_r_b", 1), ("Wk_s_b", 1),
    ("bq", 1), ("bk", 1),
):
    VEC[_name] = (sum(w for _, w in VEC.values()), _width)
NVEC = sum(w for _, w in VEC.values())
ROWV = ("ln1_g", "ln1_b", "w2_b", "ff2_b", "bo0", "Wu_v_b", "Wo_b", "bv", "bo1")

NORMS = ("ln1", "ln", "ctx", "ln2", "post0", "lat", "post1", "post2", "post3", "post4", "post5")


def program(nc, a, out):
    f32, bf16, u8 = mybir.dt.float32, mybir.dt.bfloat16, mybir.dt.uint8
    ALU, ACT, AX = mybir.AluOpType, mybir.ActivationFunctionType, mybir.AxisListType
    ctx = ExitStack()
    with ctx:
        def sb(name, shape, dt=f32):
            return ctx.enter_context(nc.sbuf_tensor(name, shape, dt))

        def sem(name):
            return ctx.enter_context(nc.semaphore(name))

        def region(name, words):
            t = sb(name, [P, words])

            def take(at, shape, dt=f32):
                n = int(np.prod(shape[1:])) // {f32: 1, bf16: 2, u8: 4}[dt]
                piece = t[0:shape[0], at:at + n]
                names = "abcde"[:len(shape) - 1]
                piece = piece if dt == f32 else piece.bitcast(dt)
                if len(shape) == 2:
                    return piece
                return piece.rearrange(f"p ({' '.join(names)}) -> p {' '.join(names)}",
                                       **dict(zip(names[1:], shape[2:])))
            return take

        vec = sb("vec", [P, NVEC])
        rowv = sb("rowv", [P, len(ROWV), D])
        ident = sb("ident", [P, P])
        w_mix = sb("w_mix", [P, 6, D])
        sel_y = sb("sel_y", [P, NG // 4, 32])
        w_ff = sb("w_ff", [P, 2 * FF, D])
        w_r0 = sb("w_r0", [P, E0])
        w_a1 = sb("w_a1", [P, 2 * 64 + 3 * P])
        w_u1 = sb("w_u1", [P, 3, P])
        rope1 = sb("rope1", [P, 2, T])
        w_x1 = sb("w_x1", [P, 4, D])
        neg_i = sb("neg_i", [P, P], bf16)
        w_g1 = sb("w_g1", [P, E1])
        w_sh = sb("w_sh", [P, 2 * SH, P])
        eb = sb("eb", [P, E1])
        sel = region("sel", 1024)
        sel_g = sel(0, [PARTS * 32, 4, P], bf16)
        sel_e = sel(0, [PARTS * E1, C1, P], bf16)
        attn_w = region("attn_w", 5 * 8 * P)
        w_x0 = attn_w(0, [P, NPAIR, 5, P])
        w_up1 = attn_w(0, [P, C1, P])
        w_dn1 = attn_w(C1 * P, [P, C1, P])
        late = region("late", 8192)
        w_up0 = late(0, [P, E0, F0 * P])
        w_dn0 = late(4096, [P, E0, F0, D])
        qs = late(0, [P, H, N], bf16)
        v1 = {L: late(at, [P, nt, (H + 1) * 2 * DH])
              for L, nt, at in (("x", NC_TILES, 4096), ("a", NJ, 4096 + NC_TILES * (H + 1) * 2 * DH))}
        v1_all = late(4096, [P, (NC_TILES + NJ) * (H + 1) * 2 * DH])
        sel_s = late(7680, [PARTS * 32, 4, P], bf16)
        rl = late(0, [P, 4, N])
        cms = late(3072, [PARTS * E1, N], bf16)
        cmp_ = late(3328, [E1, PARTS, N], bf16)
        cmf = late(4096, [E1, 2, N])

        def v(name, i=0, rows=P):
            at = VEC[name][0] + i
            return vec[0:rows, at:at + 1]

        def rv4(name):
            return rowv[:, ROWV.index(name):ROWV.index(name) + 1, :].broadcast_to([P, NJ, D])

        x = sb("x", [P, NJ, D])
        x2 = sb("x2", [P, NJ, D])
        resid = sb("resid", [P, NJ, D])
        summed = sb("summed", [P, NJ, D])
        normed = sb("normed", [P, NJ, D])
        stats = sb("stats", [P, NC_TILES, 6])
        meanvar = sb("meanvar", [P, len(NORMS), NC_TILES, 2])
        rstd = sb("rstd", [P, len(NORMS), NC_TILES])
        vareps = sb("vareps", [P, NC_TILES])
        neghalf = sb("neghalf", [P, NC_TILES])
        xT = sb("xT", [P, N])
        cv = sb("cv", [P, 2, N])
        dtmp = sb("dtmp", [P, 3, N])

        mid = region("mid", 6144)
        x1p = mid(0, [P, B, T + 2])
        xc = mid(516, [P, N])
        gate = mid(1028, [P, N])
        Bn = mid(1540, [P, N])
        Cn = mid(2052, [P, N])
        dl = mid(2564, [P, 2, N])
        dparts = mid(3588, [P, 2, PARTS, N], bf16)
        nA = sb("nA", [P, 2, NG])
        big1, big2 = region("big1", 8192), region("big2", 8192)
        dA = big1(0, [P, 2, N])
        dBx = big1(1024, [P, 2, N])
        hs = big1(2048, [P, 4, N])
        hC = big1(4096, [P, 8, N])
        ffh = big2(0, [P, FF, N])
        quads = big2(4096, [PARTS * 32, 2, D // 32, N], bf16)

        ctx_r = region("ctx_r", 3 * 1024)
        rope0 = ctx_r(0, [P, 2, CS])
        cxnT = ctx_r(1024, [P, B * CS])
        cx = ctx_r(2048, [P, NC_TILES, D])
        parts1 = {"qa": ctx_r(0, [P, PARTS, N], bf16), "ka": ctx_r(768, [P, PARTS, N], bf16),
                  "qx": ctx_r(0, [P, PARTS, N], bf16), "kx": ctx_r(1536, [P, PARTS, B * CS], bf16)}
        fours = attn_w(2 * C1 * P, [PARTS * 32, H // 4, N], bf16)
        cxT = ctx_r(2048, [P, B * CS])

        kT0 = big1(0, [P, 2, B * CS])
        kt1 = big1(2048, [P, 2, CS])
        kt2 = big1(3072, [P, 2, CS])
        qT0 = big1(4096, [P, 2, N])
        ex = big1(5120, [P, 3, 1024])
        v0 = mid(0, [P, 2, NC_TILES, 2, DH0])
        esum = big2(1536, [P, 2, 2 * T])
        etot = big2(2560, [P, 2, 2 * T])
        ones0 = big2(3584, [P, DH0])
        rden = sb("rden", [P, NJ, H])
        aoT = big2(4096, [P, NPAIR, N])

        sc0 = sb("sc0", [P, NJ, 2 * E0])
        top0 = sb("top0", [P, NJ, 8])
        pick0 = sb("pick0", [P, NJ, 8])
        mark0 = sb("mark0", [P, NJ, 2 * E0])
        g0 = sb("g0", [P, 4, NJ, E0])
        den0 = sb("den0", [P, 2, NJ])
        eh0 = big1(0, [P, 2, F0, N])

        ks = {"a": big2(0, [P, H, N], bf16), "x": big1(0, [P, H, B * CS], bf16)}
        kxf = big2(4096, [P, B * CS])
        kxr = big2(4096 + B * CS, [P, B * CS])
        ex1 = big2(4096, [P, 3, 1024])
        qf = mid(0, [P, 2, N])
        latent = mid(1024, [P, N])
        nm = mid(2048, [HB, 2, T])
        nmp = mid(3072, [HB, 2, PARTS, T], bf16)
        og = mid(3840, [P, H // 4, N])
        mx = {"a": sb("mx_a", [P, NJ, H]), "x": sb("mx_x", [P, NJ, H])}
        ao1 = x2[:, :, :].rearrange("p j (h d) -> p j h d", h=H)
        aoT1 = w_mix[:, 0:NJ, :].rearrange("p a b -> p (a b)")
        mq8 = mid(0, [P, NJ, CS], u8)
        mk8 = mid(512, [P, B, CS // P, T], u8)
        mq = big2(7168, [P, NJ, CS], bf16)
        mk = sel(0, [P, B, CS // P, T], bf16)

        lg1 = late(5120, [P, 4, NJ, E1])
        r1 = sb("r1", [P, 2, NJ, 16])
        sel1 = w_ff[:, 0:4, :].rearrange("p a (j e) -> p (a j) e", e=64).rearrange(
            "p (i j) e -> p i j e", i=2)
        t1 = sb("t1", [P, 4, NJ, 8])
        pr1 = sb("pr1", [P, 2, NJ, 8])
        cmb = sb("cmb", [P, NJ, E1])
        hh = big2(0, [P, C1, N])
        hsh = big1(0, [P, SH, N])

        ps = ctx.enter_context(nc.psum_tensor("ps", [P, 8, 512], f32))

        SPREADS = B * H // 2

        scr = {k: nc.dram_tensor(f"parts_{k}", [P, PARTS, w], bf16, kind="Internal").ap()
               for k, w in (("ka", N), ("kx", B * CS))}

        ld = {k: sem(f"loaded_{k}") for k in (
            "x", "vec", "rowv", "ident", "mix", "sel", "cx", "cxT", "ff", "rope0", "x0", "e0", "a1",
            "x1", "mask", "e1", "sel_s")}
        norm_var = sem("norm_var")
        norm_rstd = sem("norm_rstd")
        norm_out = sem("norm_out")
        consts = sem("consts")
        dve_own, act_own, pool_own = sem("dve_own"), sem("act_own"), sem("pool_own")
        S = {k: sem(k) for k in (
            "w1_ps", "v1_ps", "x1p_done", "conv_done", "xc_done", "gate_done",
            "dt_ps", "z_done", "BC_ps", "BC_done", "negA", "lg_done", "delta_parts", "dx_parts",
            "delta_quads", "dx_quads", "late_quads",
            "spread_d", "spread_x", "dA_done", "dBx_done", "scan_done", "hC_done", "y_ps",
            "yv_done", "mo_ps", "res_ready", "x2_done", "ff_ps", "ff_act", "ff2_ps",
            "cxnT_ps", "cxnT_done",
            "k0_ps", "k0_mul", "k0_done", "q0_ps", "q0_done", "v0_ps", "v0_done", "s0_ps", "e0_exp",
            "e0_clip", "e0_used", "e0_sum", "e0_tot", "o0_ps", "o0_norm", "y0_ps",
            "xT_ps", "xT_done", "r0_ps", "r0_max", "r0_exp", "up0_ps", "up0_act", "dn0_ps",
            "dn0_acc", "stored",
            "cdown_ps", "cdown_done", "qk_ps", "qk_done", "va_ps", "va_done",
            "kx_ps", "kx_done", "vx_ps", "vx_done", "mask_done",
            "g1_ps", "g1_exp", "cmb_done", "cmbT_ps", "cms_done", "up1_ps", "relu_done", "cb_ps",
            "h1_done", "sq_even", "sq_odd", "y1_ps", "rope_signed", "ones",
            "x_scr", "a_scr0", "a_scr1", "a_scr2")}
        for L in "ax":
            for k in ("ones", "q_parts", "k_parts", "stack", "fours", "spread_ps", "spread", "smax_ps",
                      "redmax", "mT_ps", "nm_done", "nm_stack0", "nm_stack1", "s_ps", "e_exp",
                      "e_used", "o_sb",
                      "oT_ps", "o_norm", "aT_ps", "aT_done", "y_ps"):
                S[f"{L}_{k}"] = sem(f"{L}_{k}")

        def normed_tiles(name, j=None):
            tiles = [NC_TILES if n == "ctx" else NJ for n in NORMS[:NORMS.index(name) + 1]]
            return sum(tiles) if j is None else sum(tiles[:-1]) + j + 1

        def own(eng, chain):
            count = [0]

            def link(ins):
                count[0] += 1
                ins.then_inc(chain, 1)
                eng.wait_ge(chain, count[0])
            return link

        ORDER = ([(q, i) for two in ((0, 1), (2, 3)) for i in range(2) for q in two]
                 + [(q, i) for i in (2, 3) for q in range(4)])
        SUMMED = ((0, 1, 4, 5), (2, 3, 6, 7), (8, 9, 10, 11), (12, 13, 14, 15))
        KEYS = {"a": T, "x": CS}

        MT_BANK = (4, 7, 7, 7)
        AHEAD = {"a": 8, "x": 13}

        def row_steps(L):
            return 2 * HB * KEYS[L] // 512

        def row_bank(L, m):
            return 6 + m % 2 if m >= row_steps(L) + AHEAD[L] else m % 4

        def rows_beside(L, n):
            m = row_steps(L) + AHEAD[L] + 2 * n
            return [(i,) + divmod(i, row_steps(L)) for i in (m, m + 1) if i < NB * row_steps(L)]

        def last_rows(L, n):
            for _, k, i in rows_beside(L, n):
                if i == row_steps(L) - 1:
                    return [k]
            return []

        UP1 = (2, 3, 0, 1)

        def hidden(m):
            return hsh[:, m, :] if m < SH else hh[:, m - SH, :]

        block = ctx.enter_context(nc.Block())

        def stack(eng, L, pieces):
            for c in pieces:
                eng.wait_ge(S[f"a_scr{c // PARTS}" if L == "a" else "x_scr"], 16)
                if DH * c == 64:
                    eng.wait_ge(S[f"{L}_ones"], 1)
                eng.dma_start(ks[L][DH * c:DH * c + DH, :, :],
                              scr["k" + L][:, c // PARTS, :].rearrange("(h d) t -> d h t", d=DH)
                              ).then_inc(S[f"{L}_stack"], 16)

        @block.sync
        def _(sp):
            sp.dma_start(x[:], a["x"]).then_inc(ld["x"], 16)
            sp.dma_start(rowv[:], a["rowv"].partition_broadcast(P)).then_inc(ld["rowv"], 16)
            sp.dma_start(vec[:], a["vec"]).then_inc(ld["vec"], 16)
            sp.dma_start(ident[:], a["ident"]).then_inc(ld["ident"], 16)
            sp.dma_start(w_mix[:], a["w_mix"]).then_inc(ld["mix"], 16)
            sp.dma_start(sel_g[:], a["sel_g"]).then_inc(ld["sel"], 16)
            sp.dma_start(sel_y[:], a["sel_y"]).then_inc(ld["sel"], 16)
            sp.dma_start(cx[:], a["cx"]).then_inc(ld["cx"], 16)
            sp.dma_start(w_ff[:], a["w_ff"]).then_inc(ld["ff"], 16)
            sp.dma_start(w_x1[:], a["w_x1"]).then_inc(ld["x1"], 16)
            sp.dma_start(rope0[:], a["rope0"]).then_inc(ld["rope0"], 16)
            sp.dma_start(w_x0[:], a["w_x0"]).then_inc(ld["x0"], 16)
            sp.dma_start(neg_i[:], a["neg_i"]).then_inc(ld["mask"], 16)
            sp.dma_start(w_r0[:], a["w_r0"]).then_inc(ld["e0"], 16)
            sp.dma_start(w_up0[:], a["w_up0"]).then_inc(ld["e0"], 16)
            sp.dma_start(w_dn0[:], a["w_dn0"]).then_inc(ld["e0"], 16)
            sp.dma_start(w_a1[:], a["w_a1"]).then_inc(ld["a1"], 16)
            sp.dma_start(w_u1[:], a["w_u1"]).then_inc(ld["a1"], 16)
            sp.dma_start(rope1[:], a["rope1"]).then_inc(ld["a1"], 16)
            sp.dma_start(w_g1[:], a["w_g1"]).then_inc(ld["e1"], 16)
            sp.dma_start(w_sh[:], a["w_sh"]).then_inc(ld["e1"], 16)
            sp.dma_start(eb[:], a["eb"].partition_broadcast(P)).then_inc(ld["e1"], 16)

            for kind, parts in enumerate(("delta_parts", "dx_parts")):
                for q in (2, 3):
                    for i in range(PARTS):
                        sp.wait_ge(S[parts], i + 1)
                        sp.dma_start(quads[32 * i:32 * i + 32, kind, q, :],
                                     dparts[32 * q:32 * q + 32, kind, i, :]
                                     ).then_inc(S["late_quads"], 16)

            def spread_max(L):
                for k in range(NB):
                    b, h0 = k // 2, HB * (k % 2)
                    for i in range(PARTS):
                        sp.wait_ge(S[f"{L}_nm_done"], PARTS * k + i + 1)
                        sp.dma_start(qs[STACK + i:STACK + i + 1, h0:h0 + HB, b * T:(b + 1) * T],
                                     nmp[:, k % 2, i, :]).then_inc(S[f"{L}_nm_stack{k % 2}"], 16)

            sp.wait_ge(S["cxnT_ps"], 2)
            sp.dma_start(cxT, a["cxT"]).then_inc(ld["cxT"], 16)
            sp.wait_ge(S["y0_ps"], 1)
            sp.dma_start(mq8, a["mq8"]).then_inc(ld["mask"], 16)
            sp.dma_start(mk8, a["mk8"]).then_inc(ld["mask"], 16)
            sp.dma_start(w_up1, a["w_up1"]).then_inc(ld["e1"], 16)
            sp.dma_start(w_dn1, a["w_dn1"]).then_inc(ld["e1"], 16)
            sp.wait_ge(S["x_k_parts"], PARTS)
            sp.dma_start(scr["kx"], parts1["kx"]).then_inc(S["x_scr"], 16)
            sp.wait_ge(S["dn0_ps"], E0)
            sp.dma_start(sel_s, a["sel_s"]).then_inc(ld["sel_s"], 16)
            stack(sp, "x", range(0, 8))
            for i in range(PARTS):
                sp.wait_ge(S["a_k_parts"], i + 1)
                sp.dma_start(scr["ka"][:, i, :], parts1["ka"][:, i, :]
                             ).then_inc(S[f"a_scr{i}"], 16)
            stack(sp, "a", range(0, 5))
            stack(sp, "x", (8,))
            spread_max("a")
            spread_max("x")
            sp.wait_ge(S["x_s_ps"], B * (H // 4) * (CS // P))
            sp.dma_start(sel_e, a["sel_e"]).then_inc(ld["e1"], 16)
            sp.wait_ge(norm_out, normed_tiles(NORMS[-1]))
            sp.dma_start(out, normed[:]).then_inc(S["stored"], 16)
            sp.wait_ge(S["stored"], 16)

        @block.gpsimd
        def _(pool):
            link = own(pool, pool_own)
            nc.gpsimd.memset(neghalf[:], -0.5).then_inc(consts, 1)
            nc.gpsimd.memset(x1p[:], 0.0).then_inc(consts, 1)
            nc.gpsimd.memset(sc0[:], -FAR).then_inc(consts, 1)
            nc.gpsimd.memset(pick0[:], -FAR).then_inc(consts, 1)
            nc.gpsimd.memset(r1[:], -FAR).then_inc(consts, 1)
            nc.gpsimd.memset(t1[:], -FAR).then_inc(consts, 1)
            nc.gpsimd.memset(ones0, 1.0).then_inc(consts, 1)
            pool.wait_ge(consts, 7)

            def root(name):
                k = NORMS.index(name)
                nt = NC_TILES if name == "ctx" else NJ
                pool.wait_ge(norm_var, k + 1)
                link(nc.gpsimd.tensor_scalar(vareps[:, 0:nt], meanvar[:, k, 0:nt, 1], EPS, None,
                                             ALU.add))
                nc.gpsimd.tensor_tensor(rstd[:, k, 0:nt], vareps[:, 0:nt], neghalf[:, 0:nt],
                                        ALU.pow).then_inc(norm_rstd, 1)
                pool.wait_ge(norm_rstd, k + 1)


            root("ln1")
            root("ln")
            root("ctx")
            pool.wait_ge(ld["x"], 16)
            pool.wait_ge(ld["rowv"], 16)
            nc.gpsimd.tensor_tensor(resid[:], x[:], rv4("w2_b"), ALU.add).then_inc(S["res_ready"], 1)
            for s in range(NG):
                pool.wait_ge(S["scan_done"], s + 1)
                if s == 0:
                    pool.wait_ge(S["BC_done"], 2)
                if s >= 8:
                    pool.wait_ge(S["y_ps"], 1 if s < 10 else 2)
                nc.gpsimd.tensor_tensor(hC[:, s % 8, :], hs[:, s % 4, :], Cn[:],
                                        ALU.mult).then_inc(S["hC_done"], 1)
            root("ln2")
            pool.wait_ge(S["x2_done"], 1)
            link(nc.gpsimd.tensor_tensor(resid[:], x[:], rv4("ff2_b"), ALU.add))
            nc.gpsimd.tensor_tensor(resid[:], resid[:], x2[:], ALU.add).then_inc(S["res_ready"], 1)

            def rotated0(c, b):
                n = B * c + b
                pool.wait_ge(S["k0_mul"], 2 * n + 2)
                if c >= 2:
                    pool.wait_ge(S["s0_ps"], 4 * (c - 1))
                nc.gpsimd.tensor_tensor(kT0[:, c % 2, b * CS:(b + 1) * CS], kt1[:, n % 2, :],
                                        kt2[:, n % 2, :], ALU.add).then_inc(S["k0_done"], 1)

            for b in range(B):
                rotated0(0, b)
            root("post0")
            root("lat")
            rotated0(1, 0)
            pool.wait_ge(norm_out, normed_tiles("post0"))
            nc.gpsimd.tensor_tensor(resid[:], x[:], rv4("bo0"), ALU.add).then_inc(S["res_ready"], 1)
            for n in range(4 * NPAIR):
                c, u = divmod(n, 4)
                b, s = divmod(u, 2)
                pool.wait_ge(S["e0_clip"], n + 1)
                if n >= 2:
                    pool.wait_ge(S["e0_tot"], 2 * c + b)
                e = ex[:, n % 3, :].rearrange("p (r k t) -> p r k t", r=2, k=2)
                nc.gpsimd.tensor_tensor(esum[:, s, :].rearrange("p (r t) -> p r t", r=2),
                                        e[:, :, 0, :], e[:, :, 1, :], ALU.add
                                        ).then_inc(S["e0_sum"], 1)
                if s == 1:
                    pool.wait_ge(S["e0_sum"], n + 1)
                    if c:
                        pool.wait_ge(S["o0_ps"], 2 * (c - 1) + b + 1)
                    nc.gpsimd.tensor_tensor(etot[:, b, :], esum[:, 0, :], esum[:, 1, :], ALU.add
                                            ).then_inc(S["e0_tot"], 1)
                if u < 2 and 2 <= c + 1 < NPAIR or n == 1:
                    rotated0(c + 1, u)
            root("post1")
            link(nc.gpsimd.memset(sel1, -FAR))
            pool.wait_ge(S["y0_ps"], 1)
            nc.gpsimd.memset(ks["a"][64:P, :, :], 1.0).then_inc(S["a_ones"], 1)
            pool.wait_ge(S["a_ones"], 1)
            pool.wait_ge(S["dn0_ps"], E0)
            nc.gpsimd.memset(v1_all, 1.0).then_inc(S["ones"], 1)
            root("post2")
            pool.wait_ge(norm_out, normed_tiles("post2"))
            nc.gpsimd.tensor_tensor(resid[:], x[:], rv4("Wo_b"), ALU.add).then_inc(S["res_ready"], 1)
            pool.wait_ge(S["res_ready"], 4)
            nc.gpsimd.memset(ks["x"][64:P, :, :], 1.0).then_inc(S["x_ones"], 1)
            pool.wait_ge(S["x_ones"], 1)
            root("post3")
            pool.wait_ge(norm_out, normed_tiles("post3"))
            nc.gpsimd.tensor_tensor(resid[:], x[:], rv4("bo1"), ALU.add).then_inc(S["res_ready"], 1)
            root("post4")
            for m in range(1, SH + C1, 2):
                pool.wait_ge(S["relu_done"], m + 1)
                nc.gpsimd.tensor_tensor(hidden(m), rl[:, m % 4, :], rl[:, m % 4, :],
                                        ALU.mult).then_inc(S["sq_odd"], 1)
            root("post5")

        @block.scalar
        def _(act):
            link = own(act, act_own)

            def to_cols(dst, bank, ready, done, scale=None, bias=None, n=1):
                act.wait_ge(S[ready], n)
                if scale is None:
                    nc.scalar.activation(dst, ps[:, bank, :], ACT.Copy).then_inc(S[done], 1)
                else:
                    nc.scalar.activation(dst, ps[:, bank, :], ACT.Identity, scale=scale,
                                         bias=bias).then_inc(S[done], 1)

            act.wait_ge(ld["vec"], 16)
            to_cols(xT[:], 0, "xT_ps", "xT_done", v("ln_g"), v("ln_b"), 1)
            act.wait_ge(S["w1_ps"], 1)
            act.wait_ge(consts, 7)
            nc.scalar.activation(x1p[:, :, 1:T + 1], ps[:, 1, :].rearrange("p (b t) -> p b t", b=B),
                                 ACT.Identity, bias=v("w1_b")).then_inc(S["x1p_done"], 1)
            act.wait_ge(S["v1_ps"], 1)
            nc.scalar.activation(gate[:], ps[:, 2, :], ACT.Silu, bias=v("v1_b")
                                 ).then_inc(S["gate_done"], 1)
            act.wait_ge(S["conv_done"], 1)
            nc.scalar.activation(xc[:], cv[:, 0, :], ACT.Silu).then_inc(S["xc_done"], 1)
            link(nc.scalar.activation(nA[:, 0, :], vec[:, VEC["A_log"][0]:VEC["A_log"][0] + NG],
                                      ACT.Exp))
            nc.scalar.mul(nA[:, 1, :], nA[:, 0, :], -1.0).then_inc(S["negA"], 1)
            act.wait_ge(S["z_done"], 1)
            link(nc.scalar.activation(dtmp[:, 0, :], cv[:, 1, :], ACT.Abs))
            link(nc.scalar.activation(dtmp[:, 1, :], dtmp[:, 0, :], ACT.Exp, scale=-1.0))
            nc.scalar.activation(dtmp[:, 2, :], dtmp[:, 1, :], ACT.Ln, bias=1.0
                                 ).then_inc(S["lg_done"], 1)
            act.wait_ge(S["BC_ps"], 1)
            nc.scalar.activation(Bn[:], ps[:, 4, :], ACT.Identity, bias=v("Bp_b")
                                 ).then_inc(S["BC_done"], 1)
            nc.scalar.activation(Cn[:], ps[:, 5, :], ACT.Identity, bias=v("Cp_b")
                                 ).then_inc(S["BC_done"], 1)
            for i in range(2):
                to_cols(cxnT[:, i * 512:(i + 1) * 512], 6 + i, "cxnT_ps", "cxnT_done",
                        v("ctx_g"), v("ctx_b"), i + 1)
            act.wait_ge(S["negA"], 1)
            for s, (q, i) in enumerate(ORDER):
                act.wait_ge(S["spread_d"], s + 1)
                if s >= 2:
                    act.wait_ge(S["scan_done"], s - 1)
                nc.scalar.activation(dA[:, s % 2, :], ps[:, s % 2, :], ACT.Exp,
                                     scale=nA[:, 1, 4 * q + i:4 * q + i + 1]).then_inc(S["dA_done"], 1)

            def evac0(c, kind):
                if kind == "q":
                    act.wait_ge(S["q0_ps"], c + 1)
                    if c >= 2:
                        act.wait_ge(S["s0_ps"], 4 * (c - 1))
                    nc.scalar.activation(qT0[:, c % 2, :], ps[:, 6 if c else 3, :], ACT.Copy,
                                         scale=DH0 ** -0.5).then_inc(S["q0_done"], 1)
                elif kind in ("v0", "v1"):
                    i = int(kind[1])
                    act.wait_ge(S["v0_ps"], 2 * c + i + 1)
                    if c >= 2:
                        act.wait_ge(S["e0_used"], 4 * (c - 1))
                    elif c == 0:
                        act.wait_ge(S["mo_ps"], 1)
                    nc.scalar.activation(
                        v0[:, c % 2, 4 * i:4 * i + 4, :, 0:DH0],
                        ps[:, 7 - i, :].rearrange("p (k r d) -> p k r d", k=4, r=2), ACT.Copy
                    ).then_inc(S["v0_done"], 1)

            for kind in ("v0", "v1"):
                evac0(0, kind)
            to_cols(xT[:], 0, "xT_ps", "xT_done", v("ln2_g"), v("ln2_b"), 2)
            for c in range(FF):
                act.wait_ge(S["ff_ps"], c + 1)
                nc.scalar.activation(ffh[:, c, :], ps[:, 1 + c, :], ACT.Gelu, bias=v("ff1_b", c)
                                     ).then_inc(S["ff_act"], 1)
            for kind in ("v0", "v1"):
                evac0(1, kind)
            to_cols(xT[:], 0, "xT_ps", "xT_done", v("lat_g"), v("lat_b"), 3)
            evac0(0, "q")
            for c in range(NPAIR):
                for u in range(4):
                    n = 4 * c + u
                    act.wait_ge(S["s0_ps"], n + 1)
                    if n >= 3:
                        act.wait_ge(S["e0_used"], n - 2)
                        act.wait_ge(S["e0_sum"], n - 2)
                    nc.scalar.activation(ex[:, n % 3, :].rearrange("p (r n) -> p r n", r=2),
                                         ps[:, 2 * (n % 2):2 * (n % 2) + 2, :], ACT.Exp
                                         ).then_inc(S["e0_exp"], 1)
                    if c < NPAIR - 1:
                        for kind in ((), ("q",), ("v0",), ("v1",))[u]:
                            if kind == "q" or c:
                                evac0(c + 1, kind)
            for i in range(2):
                act.wait_ge(S["kx_ps"], i + 1)
                nc.scalar.activation(kxf[:, i * 512:(i + 1) * 512], ps[:, 4 + i, :], ACT.Identity,
                                     bias=v("bk")).then_inc(S["kx_done"], 1)
            to_cols(xT[:], 0, "xT_ps", "xT_done", n=4)
            act.wait_ge(S["r0_max"], 1)
            nc.scalar.activation(g0[:, 1], g0[:, 0], ACT.Exp).then_inc(S["r0_exp"], 1)
            for e in range(E0):
                for c in range(F0):
                    n = F0 * e + c
                    act.wait_ge(S["up0_ps"], n + 1)
                    if e >= 2:
                        act.wait_ge(S["dn0_ps"], e - 1)
                    nc.scalar.activation(eh0[:, e % 2, c, :], ps[:, n % 3, :], ACT.Gelu
                                         ).then_inc(S["up0_act"], 1)
            to_cols(xT[:], 0, "xT_ps", "xT_done", n=5)
            act.wait_ge(S["cdown_ps"], 1)
            nc.scalar.activation(latent, ps[:, 1, :], ACT.Identity, bias=v("Wd_b")
                                 ).then_inc(S["cdown_done"], 1)

            def attend(L):
                for n in range(SPREADS):
                    b, h = divmod(2 * n, H)
                    act.wait_ge(S[f"{L}_spread_ps"], n + 1)
                    nc.scalar.activation(
                        qs[:, h:h + 2, b * T:(b + 1) * T],
                        ps[:, 5 + n % 2, :].rearrange("p (h t) -> p h t", h=2), ACT.Copy
                    ).then_inc(S[f"{L}_spread"], 1)
                nk = KEYS[L] // P
                scale = 1.0 / float(np.sqrt(np.float32(H + 64 + 64))) if L == "a" else 1.0
                for n in range(B * (H // 4) * nk):
                    act.wait_ge(S[f"{L}_s_ps"], n + 1)
                    if n >= 3:
                        act.wait_ge(S[f"{L}_e_used"], n - 2)
                    nc.scalar.activation(ex1[:, n % 3, :].rearrange("p (r n) -> p r n", r=2),
                                         ps[:, 2 * (n % 2):2 * (n % 2) + 2, :], ACT.Exp, scale=scale
                                         ).then_inc(S[f"{L}_e_exp"], 1)
                act.wait_ge(S[f"{L}_aT_ps"], 1)
                nc.scalar.activation(aoT1[:], ps[:, 6, :], ACT.Copy).then_inc(S[f"{L}_aT_done"], 1)

            stack(act, "a", range(5, 9))
            attend("a")
            to_cols(xT[:], 0, "xT_ps", "xT_done", n=6)
            attend("x")
            to_cols(xT[:], 0, "xT_ps", "xT_done", n=7)
            act.wait_ge(S["g1_ps"], 1)
            nc.scalar.activation(lg1[:, 0], ps[:, 1, 0:NJ * E1].rearrange("p (j e) -> p j e", j=NJ),
                                 ACT.Exp, scale=-1.0).then_inc(S["g1_exp"], 1)
            for m in range(SH + C1):
                act.wait_ge(S["up1_ps"], m + 1)
                if m >= 4 and m % 2:
                    act.wait_ge(S["sq_odd"], (m - 4) // 2 + 1)
                nc.scalar.activation(rl[:, m % 4, :], ps[:, UP1[m % 4], :], ACT.Relu
                                     ).then_inc(S["relu_done"], 1)
                if m % 2:
                    act.wait_ge(S["relu_done"], m)
                    nc.scalar.activation(hidden(m - 1), rl[:, (m - 1) % 4, :], ACT.Square
                                         ).then_inc(S["sq_even"], 1)

        @block.vector
        def _(dve):
            link = own(dve, dve_own)

            def layernorm(name, src, dst, meanwhile=None):
                k = NORMS.index(name)
                nt = src.shape[1]
                for j in range(nt):
                    ins = nc.vector.bn_stats(stats[:, j, :], src[:, j, :])
                link(ins)
                for j in range(nt):
                    ins = nc.vector.bn_aggr(meanvar[:, k, j, :], stats[:, j, :])
                ins.then_inc(norm_var, 1)
                dve.wait_ge(norm_var, k + 1)
                if meanwhile:
                    meanwhile()
                dve.wait_ge(norm_rstd, k + 1)
                for j in range(nt):
                    nc.vector.tensor_scalar(dst[:, j, :], src[:, j, :], meanvar[:, k, j, 0:1],
                                            rstd[:, k, j:j + 1], ALU.subtract, ALU.mult
                                            ).then_inc(norm_out, 1)
                dve.wait_ge(norm_out, normed_tiles(name))

            def split(src, parts, rest, done, before=0, op=None, by=None):
                if op is None:
                    nc.vector.tensor_copy(parts[0], src).then_inc(done, 1)
                    dve.wait_ge(done, before + 1)
                    link(nc.vector.tensor_tensor(rest, src, parts[0], ALU.subtract))
                else:
                    nc.vector.tensor_scalar(parts[0], src, by, None, op).then_inc(done, 1)
                    dve.wait_ge(done, before + 1)
                    link(nc.vector.scalar_tensor_tensor(rest, src, by, parts[0], op, ALU.subtract))
                nc.vector.tensor_copy(parts[1], rest).then_inc(done, 1)
                dve.wait_ge(done, before + 2)
                nc.vector.tensor_tensor(parts[2], rest, parts[1], ALU.subtract).then_inc(done, 1)

            def gather_fours(L, fs=range(H // 4)):
                for f in fs:
                    for i in range(PARTS):
                        ins = nc.vector.tensor_copy(fours[32 * i:32 * i + 32, f, :],
                                                    parts1["q" + L][32 * f:32 * f + 32, i, :])
                    ins.then_inc(S[f"{L}_fours"], 1)

            dve.wait_ge(ld["x"], 16)
            layernorm("ln1", x[:], normed)
            dve.wait_ge(ld["rowv"], 16)
            link(nc.vector.tensor_tensor(normed[:], normed[:], rv4("ln1_g"), ALU.mult))
            link(nc.vector.tensor_tensor(summed[:], normed[:], rv4("ln1_b"), ALU.add))
            layernorm("ln", summed[:], normed)
            dve.wait_ge(ld["cx"], 16)
            layernorm("ctx", cx, cx)
            dve.wait_ge(ld["vec"], 16)
            dve.wait_ge(S["x1p_done"], 1)
            cv3 = cv[:, :, :].rearrange("p i (b t) -> p i b t", b=B)
            link(nc.vector.tensor_scalar(cv3[:, 0], x1p[:, :, 0:T], v("conv", 0), None, ALU.mult))
            link(nc.vector.scalar_tensor_tensor(cv3[:, 1], x1p[:, :, 1:T + 1], v("conv", 1),
                                                cv3[:, 0], ALU.mult, ALU.add))
            nc.vector.scalar_tensor_tensor(cv3[:, 0], x1p[:, :, 2:T + 2], v("conv", 2), cv3[:, 1],
                                           ALU.mult, ALU.add).then_inc(S["conv_done"], 1)
            dve.wait_ge(S["dt_ps"], 1)
            nc.vector.tensor_scalar(cv[:, 1, :], ps[:, 3, :], v("dt_b"), None, ALU.add
                                    ).then_inc(S["z_done"], 1)
            dve.wait_ge(S["z_done"], 1)
            dve.wait_ge(S["lg_done"], 1)
            link(nc.vector.scalar_tensor_tensor(dl[:, 0, :], cv[:, 1, :], 0.0, dtmp[:, 2, :],
                                                ALU.max, ALU.add))
            split(dl[:, 0, :], [dparts[:, 0, i, :] for i in range(3)], dtmp[:, 0, :],
                  S["delta_parts"])

            def quad(kind, q, done):
                for i in range(PARTS):
                    ins = nc.vector.tensor_copy(quads[32 * i:32 * i + 32, kind, q, :],
                                                dparts[32 * q:32 * q + 32, kind, i, :])
                ins.then_inc(S[done], 1)

            dve.wait_ge(S["delta_parts"], PARTS)
            quad(0, 0, "delta_quads")
            dve.wait_ge(S["xc_done"], 1)
            link(nc.vector.tensor_tensor(dl[:, 1, :], dl[:, 0, :], xc[:], ALU.mult))
            split(dl[:, 1, :], [dparts[:, 1, i, :] for i in range(3)], dtmp[:, 1, :], S["dx_parts"])
            dve.wait_ge(S["dx_parts"], PARTS)
            quad(1, 0, "dx_quads")
            quad(0, 1, "delta_quads")
            quad(1, 1, "dx_quads")
            dve.wait_ge(S["BC_done"], 1)
            for s in range(NG):
                dve.wait_ge(S["spread_x"], s + 1)
                if s >= 2:
                    dve.wait_ge(S["scan_done"], s - 1)
                nc.vector.tensor_tensor(dBx[:, s % 2, :], ps[:, 2 + s % 2, :], Bn[:],
                                        ALU.mult).then_inc(S["dBx_done"], 1)
                dve.wait_ge(S["dBx_done"], s + 1)
                dve.wait_ge(S["dA_done"], s + 1)
                if s >= 4:
                    dve.wait_ge(S["hC_done"], s - 3)
                for b in range(B):
                    t = slice(b * T, (b + 1) * T)
                    ins = nc.vector.tensor_tensor_scan(hs[:, s % 4, t], dA[:, s % 2, t],
                                                       dBx[:, s % 2, t], 0.0, ALU.mult, ALU.add)
                ins.then_inc(S["scan_done"], 1)
            dve.wait_ge(S["y_ps"], NG // 4)
            link(nc.vector.scalar_tensor_tensor(cv[:, 0, :], xc[:], v("D_p"), ps[:, 4, :],
                                                ALU.mult, ALU.add))
            dve.wait_ge(S["gate_done"], 1)
            nc.vector.tensor_tensor(cv[:, 1, :], cv[:, 0, :], gate[:], ALU.mult
                                    ).then_inc(S["yv_done"], 1)
            dve.wait_ge(S["mo_ps"], 1)
            dve.wait_ge(S["res_ready"], 1)
            flat = lambda t: t[:, :, :].rearrange("p j d -> p (j d)")
            nc.vector.tensor_tensor(flat(x2), ps[:, 5, :], flat(resid), ALU.add
                                    ).then_inc(S["x2_done"], 1)
            dve.wait_ge(S["x2_done"], 1)
            layernorm("ln2", x2[:], normed)
            dve.wait_ge(ld["rope0"], 16)
            nc.vector.tensor_scalar(rope0[:, 1, :], rope0[:, 1, :], v("rope_sign"), None,
                                    ALU.mult).then_inc(S["rope_signed"], 1)
            dve.wait_ge(S["rope_signed"], 1)

            def rotary(c, b):
                n = B * c + b
                for i, dst in enumerate((kt1, kt2)):
                    dve.wait_ge(S["k0_ps"], 2 * n + i + 1)
                    if n >= 2:
                        dve.wait_ge(S["k0_done"], n - 1)
                    nc.vector.tensor_tensor(dst[:, n % 2, :], ps[:, 6 + i, :], rope0[:, i, :],
                                            ALU.mult).then_inc(S["k0_mul"], 1)

            for b in range(B):
                rotary(0, b)

            def add_and_norm(bank, ready, n, res, name, meanwhile=None):
                dve.wait_ge(S[ready], n)
                dve.wait_ge(S["res_ready"], res)
                link(nc.vector.tensor_tensor(flat(summed), ps[:, bank, :], flat(resid), ALU.add))
                layernorm(name, summed[:], x, meanwhile)

            add_and_norm(4, "ff2_ps", 1, 2, "post0")

            def normed0(c, b):
                dve.wait_ge(S["o0_ps"], 2 * c + b + 1)
                dst = aoT[:, c, b * T:(b + 1) * T]
                link(nc.vector.reciprocal(dst, ps[:, 4 + b, T:2 * T]))
                nc.vector.tensor_tensor(dst, ps[:, 4 + b, 0:T], dst, ALU.mult
                                        ).then_inc(S["o0_norm"], 1)

            layernorm("lat", x[:], normed, lambda: rotary(1, 0))
            for c in range(NPAIR):
                for u in range(4):
                    n = 4 * c + u
                    dve.wait_ge(S["e0_exp"], n + 1)
                    nc.vector.tensor_scalar(ex[:, n % 3, :], ex[:, n % 3, :], float(np.exp(CLIP)),
                                            float(np.exp(-CLIP)), ALU.min, ALU.max
                                            ).then_inc(S["e0_clip"], 1)
                    if u < 2 and 2 <= c + 1 < NPAIR or n == 1:
                        rotary(c + 1, u)
                    if u == 3:
                        normed0(c, 0)
                    if u == 1 and c:
                        normed0(c - 1, 1)
            normed0(NPAIR - 1, 1)
            add_and_norm(6, "y0_ps", 1, 3, "post1")

            dve.wait_ge(S["r0_ps"], 1)
            dve.wait_ge(consts, 7)
            link(nc.vector.tensor_copy(sc0[:, :, 0:E0], ps[:, 4, 0:NJ * E0].rearrange(
                "p (j e) -> p j e", j=NJ)))
            for j in range(NJ):
                ins = nc.vector.max(top0[:, j, :], sc0[:, j, 0:E0])
            link(ins)
            link(nc.vector.tensor_copy(pick0[:, :, 0:2], top0[:, :, 0:2]))
            for j in range(NJ):
                ins = nc.vector.match_replace(out=mark0[:, j, :], in_to_replace=pick0[:, j, :],
                                              in_values=sc0[:, j, :], imm_value=FAR)
            nc.vector.tensor_tensor(g0[:, 0], sc0[:, :, 0:E0],
                                    top0[:, :, 0:1].broadcast_to([P, NJ, E0]), ALU.subtract
                                    ).then_inc(S["r0_max"], 1)
            dve.wait_ge(S["r0_exp"], 1)
            dve.wait_ge(S["r0_max"], 1)
            link(nc.vector.scalar_tensor_tensor(g0[:, 2], mark0[:, :, 0:E0], 0.5 * FAR, g0[:, 1],
                                                ALU.is_ge, ALU.mult))
            link(nc.vector.tensor_reduce(den0[:, 0, :], g0[:, 2], AX.X, ALU.add))
            link(nc.vector.reciprocal(den0[:, 1, :], den0[:, 0, :]))
            link(nc.vector.tensor_tensor(
                g0[:, 3], g0[:, 2],
                den0[:, 1, :].rearrange("p (j o) -> p j o", o=1).broadcast_to([P, NJ, E0]), ALU.mult))
            for e in range(E0):
                dve.wait_ge(S["dn0_ps"], e + 1)
                if e:
                    dve.wait_ge(S["dn0_acc"], e)
                for j in range(NJ):
                    ins = nc.vector.scalar_tensor_tensor(
                        summed[:, j, :], ps[:, 5 + e % 2, j * D:(j + 1) * D], g0[:, 3, j, e:e + 1],
                        summed[:, j, :] if e else x[:, j, :], ALU.mult, ALU.add)
                ins.then_inc(S["dn0_acc"], 1)
                if e == 0:
                    dve.wait_ge(ld["mask"], 48)
                    nc.vector.tensor_scalar(mq[:], mq8[:], -BIG, None, ALU.mult
                                            ).then_inc(S["mask_done"], 1)
                    nc.vector.tensor_copy(mk[:], mk8[:]).then_inc(S["mask_done"], 1)
                if e == 1:
                    dve.wait_ge(S["kx_done"], 2)
                    dve.wait_ge(S["vx_ps"], 2)
                    split(kxf, [parts1["kx"][:, i, :] for i in range(3)], kxr, S["x_k_parts"])
            dve.wait_ge(S["dn0_acc"], E0)
            layernorm("post2", summed[:], x)

            def values_of(L):
                return v1[L][:, :, 0:H * 2 * DH].rearrange("p j (h w) -> p j h w", h=H)[:, :, :, 0:DH]

            def rotated(i, banks, biases, dst, done):
                dve.wait_ge(S["qk_ps"], 3 * i + 1)
                cos = rope1[:, 0:1, :].broadcast_to([P, B, T])
                sin = rope1[:, 1:2, :].broadcast_to([P, B, T])
                by_b = lambda t: t.rearrange("p (b t) -> p b t", b=B)
                nc.vector.scalar_tensor_tensor(by_b(dtmp[:, 0, :]), by_b(ps[:, banks[1], :]), v(biases[1]),
                                               cos, ALU.add, ALU.mult)
                dve.wait_ge(S["qk_ps"], 3 * i + 2)
                link(nc.vector.scalar_tensor_tensor(by_b(dtmp[:, 1, :]), by_b(ps[:, banks[2], :]),
                                                    v(biases[2]), sin, ALU.add, ALU.mult))
                dve.wait_ge(S["qk_ps"], 3 * i + 3)
                link(nc.vector.scalar_tensor_tensor(dtmp[:, 2, :], ps[:, banks[0], :], v(biases[0]),
                                                    dtmp[:, 0, :], ALU.add, ALU.add))
                nc.vector.tensor_tensor(dst, dtmp[:, 2, :], dtmp[:, 1, :], ALU.add).then_inc(done, 1)
                dve.wait_ge(done, i + 1)

            dve.wait_ge(S["ones"], 1)
            for i in range(2):
                dve.wait_ge(S["vx_ps"], i + 1)
                nc.vector.tensor_tensor(
                    values_of("x")[:, 4 * i:4 * i + 4],
                    ps[:, 7 - 4 * i, :].rearrange("p (j h d) -> p j h d", j=4, h=H),
                    rv4("bv").rearrange("p j (h d) -> p j h d", h=H), ALU.add
                ).then_inc(S["vx_done"], 1)
            dve.wait_ge(ld["a1"], 48)
            rotated(0, (1, 2, 7), ("Wu_k_b", "Wk_r_b", "Wk_s_b"), qf[:, 1, :], S["qk_done"])
            split(qf[:, 1, :], [parts1["ka"][:, i, :] for i in range(3)], cv[:, 1, :], S["a_k_parts"])
            rotated(1, (3, 4, 5), ("Wu_q_b", "Wq_r_b", "Wq_s_b"), qf[:, 0, :], S["qk_done"])
            split(qf[:, 0, :], [parts1["qa"][:, i, :] for i in range(3)], cv[:, 0, :], S["a_q_parts"])
            dve.wait_ge(S["a_q_parts"], PARTS)
            gather_fours("a", (0,))
            dve.wait_ge(S["va_ps"], 1)
            nc.vector.tensor_tensor(
                values_of("a"), ps[:, 6, :].rearrange("p (j h d) -> p j h d", j=NJ, h=H),
                rv4("Wu_v_b").rearrange("p j (h d) -> p j h d", h=H), ALU.add
            ).then_inc(S["va_done"], 1)
            gather_fours("a", (1, 2, 3))

            def row_max(L, m, k, i):
                heads, b = 512 // KEYS[L], k // 2
                q, h = divmod(i * heads, HB)
                h += HB * (k % 2)
                bank = row_bank(L, m)
                dve.wait_ge(S[f"{L}_smax_ps"], m + 1)
                dst = mx[L][:, 2 * b + q, h:h + heads]
                if L == "x":
                    nc.vector.tensor_tensor_reduce(ps[:, bank, :], ps[:, bank, :],
                                                   mq[:, 2 * b + q, :], 1.0, -FAR, ALU.add, ALU.max,
                                                   dst).then_inc(S[f"{L}_redmax"], 1)
                else:
                    nc.vector.tensor_reduce(
                        dst, ps[:, bank, :].rearrange("p (h k) -> p h k", h=heads), AX.X, ALU.max
                    ).then_inc(S[f"{L}_redmax"], 1)

            def minus_max(L, k):
                m = k % 2
                dve.wait_ge(S[f"{L}_mT_ps"], k + 1)
                if k >= 2:
                    dve.wait_ge(S[f"{L}_nm_stack{m}"], 16 * PARTS * (k // 2))
                split(ps[0:HB, MT_BANK[k], 0:T], [nmp[:, m, i, :] for i in range(3)],
                      nm[:, m, :], S[f"{L}_nm_done"], PARTS * k, ALU.mult, -1.0)

            def attend(L, factor):
                nk = KEYS[L] // P

                def normed_rows(g):
                    dve.wait_ge(S[f"{L}_oT_ps"], g + 1)
                    t = ps[:, 6 + g % 2, :].rearrange("p (j h r) -> p j h r", j=NJ, h=4)
                    rd = rden[:, :, 4 * g:4 * g + 4]
                    link(nc.vector.reciprocal(rd, t[:, :, :, DH]))
                    if factor != 1.0:
                        link(nc.vector.tensor_scalar(rd, rd, factor, None, ALU.mult))
                    for j in range(NJ):
                        ins = nc.vector.tensor_tensor(
                            ao1[:, j, 4 * g:4 * g + 4, :], t[:, j, :, 0:DH],
                            rden[:, j, 4 * g:4 * g + 4].rearrange("p (h o) -> p h o", o=1)
                            .broadcast_to([P, 4, DH]), ALU.mult)
                    ins.then_inc(S[f"{L}_o_norm"], 1)

                for m in range(row_steps(L) + AHEAD[L]):
                    k, i = divmod(m, row_steps(L))
                    row_max(L, m, k, i)
                    if i == row_steps(L) - 1:
                        minus_max(L, k)
                for n in range(B * 4 * nk):
                    for m, k, i in rows_beside(L, n):
                        row_max(L, m, k, i)
                    if n % nk == nk - 1:
                        i = n // nk
                        b, g = divmod(i, H // 4)
                        if b and g:
                            normed_rows(g - 1)
                        dve.wait_ge(S[f"{L}_e_used"], n + 1)
                        nc.vector.tensor_copy(og[:, g, b * T:(b + 1) * T], ps[:, 4 + i % 2, 0:T]
                                              ).then_inc(S[f"{L}_o_sb"], 1)
                    for k in last_rows(L, n):
                        minus_max(L, k)
                normed_rows(H // 4 - 1)

            attend("a", 1.0)
            add_and_norm(7, "a_y_ps", 1, 4, "post3")

            dve.wait_ge(S["qk_ps"], 7)
            split(ps[:, 4, :], [parts1["qx"][:, i, :] for i in range(3)], cv[:, 0, :], S["x_q_parts"],
                  0, ALU.add, v("bq"))
            dve.wait_ge(S["x_q_parts"], PARTS)
            gather_fours("x")
            attend("x", 1.0 / float(np.sqrt(np.float32(DH))))
            add_and_norm(7, "x_y_ps", 1, 5, "post4")

            dve.wait_ge(S["g1_exp"], 1)
            link(nc.vector.tensor_scalar(lg1[:, 1], lg1[:, 0], 1.0, None, ALU.add))
            link(nc.vector.reciprocal(lg1[:, 2], lg1[:, 1]))
            dve.wait_ge(ld["e1"], 16 * 6)
            link(nc.vector.tensor_tensor(lg1[:, 3], lg1[:, 2],
                                         eb[:, :].rearrange("p (o e) -> p o e", o=1)
                                         .broadcast_to([P, NJ, E1]), ALU.add))
            sc = lg1[:, 3].rearrange("p j (g i) -> p j g i", i=4)
            best, other = pr1[:, 0], pr1[:, 1]
            link(nc.vector.tensor_tensor(best, sc[:, :, :, 0], sc[:, :, :, 1], ALU.add))
            for i, k in ((0, 2), (0, 3), (1, 2), (1, 3), (2, 3)):
                link(nc.vector.tensor_tensor(other, sc[:, :, :, i], sc[:, :, :, k], ALU.add))
                link(nc.vector.tensor_tensor(best, best, other, ALU.max))
            dve.wait_ge(consts, 7)
            link(nc.vector.tensor_copy(r1[:, 0, :, 0:8], best))
            for j in range(NJ):
                ins = nc.vector.max(t1[:, 0, j, :], best[:, j, :])
            link(ins)
            link(nc.vector.tensor_copy(t1[:, 1, :, 0:4], t1[:, 0, :, 0:4]))
            for j in range(NJ):
                ins = nc.vector.match_replace(out=r1[:, 1, j, :], in_to_replace=t1[:, 1, j, :],
                                              in_values=r1[:, 0, j, :], imm_value=FAR)
            link(ins)
            link(nc.vector.tensor_scalar(best, r1[:, 1, :, 0:8], 0.5 * FAR, None, ALU.is_ge))
            for j in range(NJ):
                ins = nc.vector.tensor_tensor(
                    sel1[:, 0, j, 0:E1].rearrange("p (g i) -> p g i", i=4), sc[:, j],
                    best[:, j, :].rearrange("p (g o) -> p g o", o=1).broadcast_to([P, 8, 4]),
                    ALU.mult)
            link(ins)
            for j in range(NJ):
                ins = nc.vector.max(t1[:, 2, j, :], sel1[:, 0, j, 0:E1])
            link(ins)
            link(nc.vector.tensor_copy(t1[:, 3, :, 0:6], t1[:, 2, :, 0:6]))
            for j in range(NJ):
                ins = nc.vector.match_replace(out=sel1[:, 1, j, :], in_to_replace=t1[:, 3, j, :],
                                              in_values=sel1[:, 0, j, :], imm_value=FAR)
            link(ins)
            link(nc.vector.scalar_tensor_tensor(lg1[:, 0], sel1[:, 1, :, 0:E1], 0.5 * FAR, lg1[:, 2],
                                                ALU.is_ge, ALU.mult))
            link(nc.vector.tensor_reduce(den0[:, 0, :], lg1[:, 0], AX.X, ALU.add))
            link(nc.vector.tensor_scalar(den0[:, 0, :], den0[:, 0, :], 1e-20, None, ALU.add))
            link(nc.vector.reciprocal(den0[:, 1, :], den0[:, 0, :]))
            link(nc.vector.tensor_tensor(
                lg1[:, 1], lg1[:, 0],
                den0[:, 1, :].rearrange("p (j o) -> p j o", o=1).broadcast_to([P, NJ, E1]),
                ALU.mult))
            nc.vector.tensor_scalar(cmb[:], lg1[:, 1], 2.5, None, ALU.mult).then_inc(S["cmb_done"], 1)
            dve.wait_ge(S["cmbT_ps"], 1)
            link(nc.vector.tensor_copy(cmp_[:, 0, :], ps[0:E1, 4, :]))
            link(nc.vector.tensor_tensor(cmf[:, 1, :], ps[0:E1, 4, :], cmp_[:, 0, :], ALU.subtract))
            link(nc.vector.tensor_copy(cmp_[:, 1, :], cmf[:, 1, :]))
            link(nc.vector.tensor_tensor(cmp_[:, 2, :], cmf[:, 1, :], cmp_[:, 1, :], ALU.subtract))
            for i in range(PARTS):
                ins = nc.vector.tensor_copy(cms[E1 * i:E1 * (i + 1), :], cmp_[:, i, :])
            ins.then_inc(S["cms_done"], 1)
            for c in range(C1):
                dve.wait_ge(S["cb_ps"], c + 1)
                dve.wait_ge(S["sq_even"], (SH + c) // 2 + 1)
                if (SH + c) % 2:
                    dve.wait_ge(S["sq_odd"], (SH + c) // 2 + 1)
                nc.vector.tensor_tensor(hh[:, c, :], ps[:, 5 + c % 2, :], hh[:, c, :],
                                        ALU.mult).then_inc(S["h1_done"], 1)
            dve.wait_ge(S["y1_ps"], 1)
            link(nc.vector.tensor_tensor(flat(summed), ps[:, 7, :], flat(x), ALU.add))
            layernorm("post5", summed[:], normed)

        @block.tensor
        def _(pe):
            def mm(o, lhsT, rhs, start=True, stop=True, shared=False):
                return nc.tensor.matmul(o, lhsT, rhs, start=start, stop=stop, skip_group_check=shared)

            def to_cols(bank, src, done, norm=None):
                for j in range(NJ):
                    if norm:
                        pe.wait_ge(norm_out, normed_tiles(norm, j))
                    ins = nc.tensor.transpose(ps[:, bank, j * P:(j + 1) * P], src[:, j, :], ident[:])
                ins.then_inc(S[done], 1)

            def to_rows(bank, cols, w, done):
                for j in range(NJ):
                    for c, (lhs, rhs) in enumerate(zip(cols, w)):
                        ins = mm(ps[:, bank, j * D:(j + 1) * D], lhs[:, j * P:(j + 1) * P], rhs,
                                 c == 0, c == len(w) - 1)
                ins.then_inc(S[done], 1)

            pe.wait_ge(ld["ident"], 16)
            to_cols(0, normed, "xT_ps", "ln")
            pe.wait_ge(ld["mix"], 16)
            pe.wait_ge(S["xT_done"], 1)
            mm(ps[:, 1, :], w_mix[:, 0, :], xT[:]).then_inc(S["w1_ps"], 1)
            mm(ps[:, 2, :], w_mix[:, 1, :], xT[:]).then_inc(S["v1_ps"], 1)
            pe.wait_ge(norm_out, normed_tiles("ctx"))
            for i in range(2):
                to_cols(6 + i, cx[:, 4 * i:4 * i + 4, :], "cxnT_ps")
            pe.wait_ge(S["xc_done"], 1)
            mm(ps[:, 3, :], w_mix[:, 2, :], xc[:]).then_inc(S["dt_ps"], 1)
            mm(ps[:, 4, :], w_mix[:, 3, :], xc[:])
            mm(ps[:, 5, :], w_mix[:, 4, :], xc[:]).then_inc(S["BC_ps"], 1)
            pe.wait_ge(ld["sel"], 32)
            pe.wait_ge(S["delta_parts"], PARTS)
            pe.wait_ge(S["gate_done"], 1)

            def y_of(k):
                pe.wait_ge(S["hC_done"], SUMMED[k][-1] + 1)
                if k == 0:
                    pe.wait_ge(S["BC_done"], 2)
                for s in SUMMED[k]:
                    q, i = ORDER[s]
                    ins = mm(ps[32 * q:32 * q + 32, 4, :], sel_y[:, i, :], hC[:, s % 8, :],
                             i == 0, i == 3)
                ins.then_inc(S["y_ps"], 1)

            def project0(c, step):
                if step < 2:
                    n = B * c + step
                    for i in range(2):
                        if n:
                            pe.wait_ge(S["k0_mul"], 2 * (n - 1) + i + 1)
                        if step == 0:
                            pe.wait_ge(S["v0_done"], 2 * (c if c >= 2 else c + 1))
                            if c >= 2:
                                pe.wait_ge(S["q0_done"], c)
                        mm(ps[:, 6 + i, :], w_x0[:, c, i, :], cxnT[:, step * CS:(step + 1) * CS]
                           ).then_inc(S["k0_ps"], 1)
                elif step == 2:
                    pe.wait_ge(S["k0_mul"], 2 * (B * c + 1) + 2)
                    mm(ps[:, 6, :], w_x0[:, c, 3, :], xT[:]).then_inc(S["q0_ps"], 1)
                    values0(c, 0)
                else:
                    pe.wait_ge(S["q0_done"], c + 1)
                    values0(c, 1)

            def values0(c, i):
                for k in range(4):
                    t = 4 * i + k
                    ins = mm(ps[:, 7 - i, k * P:(k + 1) * P], cxnT[:, t * P:(t + 1) * P],
                             w_x0[:, c, 2, :])
                ins.then_inc(S["v0_ps"], 1)

            for s, (q, i) in enumerate(ORDER):
                if s >= 2:
                    pe.wait_ge(S["dA_done"], s - 1)
                if s < 2:
                    pe.wait_ge(S["delta_quads"], s + 1)
                elif s == 4:
                    pe.wait_ge(S["late_quads"], 16 * 4 * PARTS)
                mm(ps[:, s % 2, :], sel_g[:, i, :], quads[:, 0, q, :]).then_inc(S["spread_d"], 1)
                if s < 2:
                    pe.wait_ge(S["dx_quads"], s + 1)
                if s >= 2:
                    pe.wait_ge(S["dBx_done"], s - 1)
                mm(ps[:, 2 + s % 2, :], sel_g[:, i, :], quads[:, 1, q, :]
                   ).then_inc(S["spread_x"], 1)
                if s in (8, 10, 14):
                    y_of((8, 10, 14).index(s))
                if s == 12:
                    pe.wait_ge(ld["x0"], 16)
                    pe.wait_ge(S["cxnT_done"], 2)
                if s in (12, 13):
                    values0(0, s - 12)
            y_of(3)
            pe.wait_ge(S["yv_done"], 1)
            to_rows(5, [cv[:, 1, :]], [w_mix[:, 5, :]], "mo_ps")
            project0(0, 0)
            to_cols(0, normed, "xT_ps", "ln2")
            pe.wait_ge(ld["ff"], 16)
            pe.wait_ge(S["xT_done"], 2)
            for c in range(FF):
                mm(ps[:, 1 + c, :], w_ff[:, c, :], xT[:]).then_inc(S["ff_ps"], 1)
            project0(0, 1)
            pe.wait_ge(S["ff_act"], FF)
            to_rows(4, [ffh[:, c, :] for c in range(FF)], [w_ff[:, FF + c, :] for c in range(FF)],
                    "ff2_ps")
            def logits0(n):
                c, u = divmod(n, 4)
                b, s = divmod(u, 2)
                if n >= 2:
                    pe.wait_ge(S["e0_exp"], n - 1)
                for k in range(2):
                    for r in range(2):
                        at = b * CS + (2 * s + k) * P
                        ins = mm(ps[:, 2 * (n % 2) + r, k * T:(k + 1) * T],
                                 kT0[64 * r:64 * r + 64, c % 2, at:at + P],
                                 qT0[64 * r:64 * r + 64, c % 2, b * T:(b + 1) * T])
                ins.then_inc(S["s0_ps"], 1)

            def mix0(n):
                c, u = divmod(n, 4)
                b, s = divmod(u, 2)
                pe.wait_ge(S["e0_clip"], n + 1)
                if s == 0 and c:
                    pe.wait_ge(S["o0_norm"], 2 * (c - 1) + b + 1)
                for k in range(2):
                    for r in range(2):
                        e = ex[:, n % 3, r * 512 + k * T:r * 512 + (k + 1) * T]
                        ins = mm(ps[64 * r:64 * r + 64, 4 + b, 0:T],
                                 v0[:, c % 2, 4 * b + 2 * s + k, r, :], e, s == k == 0, False, True)
                ins.then_inc(S["e0_used"], 1)

            def output0(c):
                pe.wait_ge(S["o0_norm"], 2 * (c + 1))
                if c == 0:
                    pe.wait_ge(S["v0_done"], 2 * NPAIR)
                for j in range(NJ):
                    ins = mm(ps[:, 6, j * D:(j + 1) * D], aoT[:, c, j * P:(j + 1) * P],
                             w_x0[:, c, 4, :], c == j == 0, c == NPAIR - 1 and j == NJ - 1, True)
                return ins

            def denominators0(c, b):
                pe.wait_ge(S["e0_tot"], 2 * c + b + 1)
                for r in range(2):
                    ins = mm(ps[64 * r:64 * r + 64, 4 + b, T:2 * T], ones0,
                             etot[:, b, r * T:(r + 1) * T], False, True, True)
                ins.then_inc(S["o0_ps"], 1)

            pe.wait_ge(S["k0_mul"], 4)
            for i in range(B):
                values0(1, i)
            project0(1, 0)
            to_cols(0, normed, "xT_ps", "lat")
            pe.wait_ge(S["xT_done"], 3)
            mm(ps[:, 3, :], w_x0[:, 0, 3, :], xT[:]).then_inc(S["q0_ps"], 1)
            pe.wait_ge(S["k0_done"], 2)
            pe.wait_ge(S["q0_done"], 1)
            pe.wait_ge(consts, 7)
            logits0(0)
            for n in range(4 * NPAIR):
                c, u = divmod(n, 4)
                if 2 <= c + 1 < NPAIR or n == 1:
                    project0(c + 1, u)
                elif n == 2:
                    pe.wait_ge(S["k0_mul"], 8)
                    mm(ps[:, 6, :], w_x0[:, 1, 3, :], xT[:]).then_inc(S["q0_ps"], 1)
                elif c + 1 == NPAIR:
                    for i in range(2 * u, min(2 * u + 2, NPAIR - 1)):
                        output0(i)
                if n + 1 < 4 * NPAIR:
                    if u == 3:
                        pe.wait_ge(S["k0_done"], 2 * (c + 2))
                    logits0(n + 1)
                if u == 0:
                    pe.wait_ge(S["v0_done"], 2 * (c + 1))
                mix0(n)
                if u == 2:
                    denominators0(c, 0)
                if u == 0 and c:
                    denominators0(c - 1, 1)
            denominators0(NPAIR - 1, 1)
            output0(NPAIR - 1).then_inc(S["y0_ps"], 1)
            pe.wait_ge(ld["x1"], 16)
            pe.wait_ge(ld["cxT"], 16)
            for i in range(2):
                mm(ps[:, 4 + i, :], w_x1[:, 1, :], cxT[:, i * 512:(i + 1) * 512]
                   ).then_inc(S["kx_ps"], 1)
            for i in range(2):
                for k in range(4):
                    t = 4 * i + k
                    ins = mm(ps[:, 7 - 4 * i, k * P:(k + 1) * P], cxT[:, t * P:(t + 1) * P],
                             w_x1[:, 2, :])
                ins.then_inc(S["vx_ps"], 1)
            to_cols(0, x, "xT_ps", "post1")
            pe.wait_ge(ld["e0"], 48)
            pe.wait_ge(S["xT_done"], 4)
            pe.wait_ge(S["kx_done"], 2)
            for j in range(NJ):
                ins = mm(ps[:, 4, j * E0:(j + 1) * E0], xT[:, j * P:(j + 1) * P], w_r0[:])
            ins.then_inc(S["r0_ps"], 1)

            def up0(e):
                for c in range(F0):
                    n = F0 * e + c
                    if n >= 3:
                        pe.wait_ge(S["up0_act"], n - 2)
                    mm(ps[:, n % 3, :], w_up0[:, e, c * P:(c + 1) * P], xT[:]
                       ).then_inc(S["up0_ps"], 1)

            up0(0)
            for e in range(E0):
                if e + 1 < E0:
                    up0(e + 1)
                pe.wait_ge(S["up0_act"], F0 * (e + 1))
                if e >= 2:
                    pe.wait_ge(S["dn0_acc"], e - 1)
                to_rows(5 + e % 2, [eh0[:, e % 2, c, :] for c in range(F0)],
                        [w_dn0[:, e, c, :] for c in range(F0)], "dn0_ps")
            to_cols(0, x, "xT_ps", "post2")
            pe.wait_ge(ld["a1"], 48)
            pe.wait_ge(S["xT_done"], 5)
            mm(ps[:, 1, :], w_a1[:, 0:128], xT[:]).then_inc(S["cdown_ps"], 1)
            pe.wait_ge(S["vx_done"], 2)
            for i in range(2):
                mm(ps[:, (2, 7)[i], :], w_a1[:, (1 + i) * P:(2 + i) * P], xT[:]
                   ).then_inc(S["qk_ps"], 1)
            pe.wait_ge(S["cdown_done"], 1)
            mm(ps[:, 1, :], w_u1[64:128, 0, :], latent[64:128, :]).then_inc(S["qk_ps"], 1)
            for i in (1, 2, 0):
                mm(ps[:, 3 + i, :], w_u1[0:64, i, :], latent[0:64, :]).then_inc(S["qk_ps"], 1)
            for j in range(NJ):
                ins = mm(ps[:, 6, j * D:(j + 1) * D], latent[64:128, j * P:(j + 1) * P],
                         w_u1[64:128, 1, :])
            ins.then_inc(S["va_ps"], 1)

            def attend(L):
                heads, nk = 512 // KEYS[L], KEYS[L] // P
                heads_per_spread = 2 // heads
                pe.wait_ge(ld["sel_s"], 16)

                def spread(n):
                    b, h = divmod(2 * n, H)
                    pe.wait_ge(S[f"{L}_fours"], h // 4 + 1)
                    if L == "a" and n == 1:
                        pe.wait_ge(S["va_done"], 1)
                    if n >= 2:
                        pe.wait_ge(S[f"{L}_spread"], n - 1)
                    for r in range(2):
                        ins = mm(ps[:, 5 + n % 2, r * T:(r + 1) * T], sel_s[:, h % 4 + r, :],
                                 fours[:, h // 4, b * T:(b + 1) * T])
                    ins.then_inc(S[f"{L}_spread_ps"], 1)

                def rows(m, k, i):
                    b = k // 2
                    q, h0 = divmod(i * heads, HB)
                    h0 += HB * (k % 2)
                    j = 2 * b + q
                    bank = row_bank(L, m)
                    if m >= 4:
                        pe.wait_ge(S[f"{L}_redmax"], m - (1 if bank >= 6 else 3))
                    if bank == 7:
                        pe.wait_ge(S[f"{L}_nm_done"], PARTS * (k - 1) + 2)
                    if i < HB // heads:
                        pe.wait_ge(S[f"{L}_spread"], (b * H + h0) // 2 + 1)
                    for h in range(heads):
                        ins = mm(ps[:, bank, h * KEYS[L]:(h + 1) * KEYS[L]],
                                 qs[:, h0 + h, j * P:(j + 1) * P],
                                 ks[L][:, h0 + h, b * KEYS[L]:(b + 1) * KEYS[L]])
                    ins.then_inc(S[f"{L}_smax_ps"], 1)

                def max_cols(k):
                    b, h0 = k // 2, HB * (k % 2)
                    pe.wait_ge(S[f"{L}_redmax"], (k + 1) * row_steps(L))
                    for q in range(2):
                        ins = nc.tensor.transpose(ps[0:HB, MT_BANK[k], q * P:(q + 1) * P],
                                                  mx[L][:, 2 * b + q, h0:h0 + HB], ident[:])
                    ins.then_inc(S[f"{L}_mT_ps"], 1)

                def logits(n):
                    b, g, k = n // (4 * nk), n // nk % 4, n % nk
                    if n >= 2:
                        pe.wait_ge(S[f"{L}_e_exp"], n - 1)
                    if g % 2 == 0 and k == 0:
                        pe.wait_ge(S[f"{L}_nm_stack{g // 2}"], 16 * PARTS * (b + 1))
                    for r in range(2):
                        bank = 2 * (n % 2) + r
                        for i in range(2):
                            h = 4 * g + 2 * r + i
                            ins = mm(ps[:, bank, i * T:(i + 1) * T],
                                     ks[L][:, h, b * KEYS[L] + k * P:b * KEYS[L] + (k + 1) * P],
                                     qs[:, h, b * T:(b + 1) * T], L == "a" or i == 0, L == "a", L == "x")
                        if L == "x":
                            for i in range(2):
                                ins = mm(ps[:, bank, i * T:(i + 1) * T], neg_i[:], mk[:, b, k, :],
                                         False, i == 1, True)
                    ins.then_inc(S[f"{L}_s_ps"], 1)

                def values(n):
                    b, g, k = n // (4 * nk), n // nk % 4, n % nk
                    i = n // nk
                    pe.wait_ge(S[f"{L}_e_exp"], n + 1)
                    if k == 0 and i >= 2:
                        pe.wait_ge(S[f"{L}_o_sb"], i - 1)
                    if n == 0:
                        pe.wait_ge(S[f"{L}_nm_done"], PARTS)
                    for r in range(4):
                        ins = mm(ps[32 * r:32 * r + 32, 4 + i % 2, 0:T],
                                 v1[L][:, b * nk + k, 2 * DH * (4 * g + r):2 * DH * (4 * g + r) + 32],
                             ex1[:, n % 3, r * T:(r + 1) * T],
                                 k == 0, k == nk - 1)
                    ins.then_inc(S[f"{L}_e_used"], 1)

                def out_rows(g):
                    if g == 0:
                        pe.wait_ge(S[f"{L}_nm_done"], PARTS * NB)
                    pe.wait_ge(S[f"{L}_o_sb"], 4 + g + 1)
                    if g >= 2:
                        pe.wait_ge(S[f"{L}_o_norm"], g - 1)
                    for j in range(NJ):
                        ins = nc.tensor.transpose(ps[:, 6 + g % 2, j * P:(j + 1) * P],
                                                  og[:, g, j * P:(j + 1) * P], ident[:])
                    ins.then_inc(S[f"{L}_oT_ps"], 1)

                total = B * 4 * nk
                for n in range(2):
                    spread(n)
                pe.wait_ge(S[f"{L}_stack"], 16 * PARTS * PARTS)
                for m in range(row_steps(L) + AHEAD[L]):
                    k, i = divmod(m, row_steps(L))
                    rows(m, k, i)
                    n, more = divmod(m + 1, heads_per_spread)
                    if not more and n + 1 < SPREADS:
                        spread(n + 1)
                    if i == row_steps(L) - 1:
                        max_cols(k)
                pe.wait_ge(S[f"{L}_redmax"], row_steps(L) + AHEAD[L])
                pe.wait_ge(S[f"{L}_spread"], SPREADS)
                logits(0)
                for n in range(total):
                    if n + 1 < total:
                        logits(n + 1)
                    for m, k, i in rows_beside(L, n):
                        rows(m, k, i)
                    if n % nk == 1 and n // nk > H // 4:
                        out_rows(n // nk - H // 4 - 1)
                    values(n)
                    for k in last_rows(L, n):
                        max_cols(k)
                out_rows(H // 4 - 1)
                pe.wait_ge(S[f"{L}_o_norm"], 4)
                for j in range(NJ):
                    ins = nc.tensor.transpose(ps[:, 6, j * P:(j + 1) * P],
                                              ao1[:, j, :, :].rearrange("p h d -> p (h d)"), ident[:])
                ins.then_inc(S[f"{L}_aT_ps"], 1)
                pe.wait_ge(S[f"{L}_aT_done"], 1)
                w_o = w_a1[:, 384:512] if L == "a" else w_x1[:, 3, :]
                to_rows(7, [aoT1], [w_o], f"{L}_y_ps")

            attend("a")
            to_cols(0, x, "xT_ps", "post3")
            pe.wait_ge(S["xT_done"], 6)
            mm(ps[:, 4, :], w_x1[:, 0, :], xT[:]).then_inc(S["qk_ps"], 1)
            pe.wait_ge(S["mask_done"], 2)
            pe.wait_ge(S["vx_done"], 2)
            attend("x")
            to_cols(0, x, "xT_ps", "post4")
            pe.wait_ge(ld["e1"], 96)
            pe.wait_ge(S["xT_done"], 7)
            for j in range(NJ):
                ins = mm(ps[:, 1, j * E1:(j + 1) * E1], xT[:, j * P:(j + 1) * P], w_g1[:])
            ins.then_inc(S["g1_ps"], 1)

            def up1(m):
                if m == 3:
                    pe.wait_ge(S["g1_exp"], 1)
                if m >= 4:
                    pe.wait_ge(S["relu_done"], m - 3)
                w = w_sh[:, m, :] if m < SH else w_up1[:, m - SH, :]
                mm(ps[:, UP1[m % 4], :], w, xT[:]).then_inc(S["up1_ps"], 1)

            def down1(m):
                w = w_sh[:, SH + m, :] if m < SH else w_dn1[:, m - SH, :]
                for j in range(NJ):
                    ins = mm(ps[:, 7, j * D:(j + 1) * D], hidden(m)[:, j * P:(j + 1) * P], w,
                             m == j == 0, m == SH + C1 - 1 and j == NJ - 1, True)
                return ins

            EARLY = 12
            for m in range(EARLY):
                up1(m)
            pe.wait_ge(S["cmb_done"], 1)
            for j in range(NJ):
                ins = nc.tensor.transpose(ps[0:E1, 4, j * P:(j + 1) * P], cmb[:, j, :], ident[:])
            ins.then_inc(S["cmbT_ps"], 1)
            for m in range(EARLY, SH + C1):
                up1(m)
            pe.wait_ge(S["sq_even"], (SH + 1) // 2)
            pe.wait_ge(S["sq_odd"], SH // 2)
            for m in range(SH):
                down1(m)
            pe.wait_ge(S["cms_done"], 1)
            for c in range(C1 + 1):
                if c < C1:
                    if c >= 2:
                        pe.wait_ge(S["h1_done"], c - 1)
                    mm(ps[:, 5 + c % 2, :], sel_e[:, c, :], cms[:]).then_inc(S["cb_ps"], 1)
                if c:
                    pe.wait_ge(S["h1_done"], c)
                    ins = down1(SH + c - 1)
            ins.then_inc(S["y1_ps"], 1)


def _constants():
    bf16 = mybir.dt.np(mybir.dt.bfloat16)
    p = np.arange(P)
    c = {"ident": np.eye(P, dtype=np.float32), "neg_i": (-BIG * np.eye(P)).astype(bf16)}
    sel = np.zeros((PARTS, 32, 4, P))
    for i in range(4):
        sel[:, i * GD + p // STATE, i, p] = 1
    c["sel_g"] = sel.reshape(PARTS * 32, 4, P).astype(bf16)
    sel = np.zeros((P, NG // 4, 32), np.float32)
    for i in range(NG // 4):
        sel[p, i, GD * i + p // STATE] = 1
    c["sel_y"] = sel
    sel = np.zeros((PARTS, E1, C1, P))
    for i in range(C1):
        sel[:, 2 * i + p // I1, i, p] = 1
    c["sel_e"] = sel.reshape(PARTS * E1, C1, P).astype(bf16)
    sel = np.zeros((PARTS, 4, DH, 4, PARTS, PARTS, DH))
    for i in range(PARTS):
        for h in range(4):
            for d in range(DH):
                sel[i, h, d, h, :, i, d] = 1
    c["sel_s"] = np.zeros((PARTS * 32, 4, P), bf16)
    c["sel_s"][:, :, 0:STACK] = sel.reshape(PARTS * 32, 4, STACK)
    ids = np.arange(D // 2, dtype=np.float32)
    theta = np.float32(10000.0) ** (np.float32(-2.0) * ids) / np.float32(D // 2)
    r = np.arange(T, dtype=np.float32)[None, :] * theta[:, None].astype(np.float32)
    cos, sin = np.repeat(np.cos(r), 2, 0), np.repeat(np.sin(r), 2, 0)
    sign = np.where(p % 2 == 0, -1.0, 1.0)[:, None]
    c["rope1"] = np.stack([cos, sin * sign], 1).astype(np.float32)
    c["rope_sign"] = np.where(p % DH0 < DH0 // 2, -1.0, 1.0).astype(np.float32)[:, None]
    return c


def _layout(i):
    c = _constants()
    i = {k: np.asarray(x) for k, x in i.items()}
    L0, X0, F, L1, X1, F1 = (lambda k, q=q: i[q + k] for q in (
        "L0_attn_", "L0_xattn_", "L0_ffn_", "L1_attn_", "L1_xattn_", "L1_ffn_"))
    col = lambda x: x.reshape(-1, 1)
    half = np.arange(P) ^ (DH0 // 2)
    pair = np.arange(P) ^ 1
    a_log = L0("A_log")
    cols = {
        "w1_b": col(L0("w1_b")), "v1_b": col(L0("v1_b")), "ln_g": col(L0("ln_g")),
        "ln_b": col(L0("ln_b")), "conv": L0("conv_w")[:, 0, :], "dt_b": col(L0("dt_b")),
        "Bp_b": col(np.tile(L0("Bp_b"), GD)), "Cp_b": col(np.tile(L0("Cp_b"), GD)),
        "A_log": a_log.reshape(NG, P).T, "D_p": col(L0("D_p")),
        "ln2_g": col(L0("ln2_g")), "ln2_b": col(L0("ln2_b")), "ff1_b": L0("ff1_b").reshape(FF, P).T,
        "lat_g": col(X0("ln_lat_g")), "lat_b": col(X0("ln_lat_b")), "ctx_g": col(X0("ln_ctx_g")),
        "ctx_b": col(X0("ln_ctx_b")), "rope_sign": c.pop("rope_sign"), 
        "Wd_b": col(np.concatenate([L1("Wd_q_b"), L1("Wd_kv_b")])),
        "Wu_q_b": col(L1("Wu_q_b")), "Wq_r_b": col(L1("Wq_r_b")),
        "Wq_s_b": col(L1("Wq_r_b")[pair]), "Wu_k_b": col(L1("Wu_k_b")), "Wk_r_b": col(L1("Wk_r_b")),
        "Wk_s_b": col(L1("Wk_r_b")[pair]), "bq": col(X1("bq")), "bk": col(X1("bk")),
    }
    chunks = lambda w: w.reshape(-1, P, w.shape[-1]).transpose(1, 0, 2)
    a = dict(c)
    a["vec"] = np.concatenate([cols[k] for k in VEC], 1)
    a["rowv"] = np.stack([L0("ln1_g"), L0("ln1_b"), L0("w2_b"), L0("ff2_b"), X0("bo"), L1("Wu_v_b"),
                          L1("Wo_b"), X1("bv").reshape(D), X1("bo")])
    a["x"] = i["x"].reshape(NJ, P, D).transpose(1, 0, 2)
    a["cx"] = i["ctx_1024"].reshape(NC_TILES, P, D).transpose(1, 0, 2)
    a["cxT"] = i["ctx_1024"].reshape(B * CS, D).T
    a["w_mix"] = np.stack([L0("w1_w"), L0("v1_w"), L0("dt_w"), np.tile(L0("Bp_w"), (1, GD)),
                           np.tile(L0("Cp_w"), (1, GD)), L0("w2_w")], 1)
    a["w_ff"] = np.concatenate([L0("ff1_w").reshape(D, FF, P), chunks(L0("ff2_w"))], 1)
    a["rope0"] = np.stack([np.tile(X0("cos").T, (4, 1)), np.tile(X0("sin").T, (4, 1))], 1)
    wk, wv = X0("Wkv")[:, :1024].reshape(D, NPAIR, P), X0("Wkv")[:, 1024:].reshape(D, NPAIR, P)
    a["w_x0"] = np.stack([wk, wk[:, :, half], wv, X0("Wq").reshape(D, NPAIR, P), chunks(X0("Wo"))], 2)
    a["w_r0"] = F("router_w").T
    a["w_up0"] = F("expert_w1").transpose(2, 0, 1)
    a["w_dn0"] = F("expert_w2").reshape(E0, D, F0, P).transpose(3, 0, 2, 1)
    a["w_a1"] = np.concatenate([L1("Wd_q_w"), L1("Wd_kv_w"), L1("Wk_r_w"), L1("Wk_r_w")[:, pair],
                                L1("Wo_w")], 1)
    a["w_u1"] = np.concatenate([
        np.stack([L1("Wu_q_w"), L1("Wq_r_w"), L1("Wq_r_w")[:, pair]], 1),
        np.stack([L1("Wu_k_w"), L1("Wu_v_w"), np.zeros_like(L1("Wu_v_w"))], 1)])
    a["w_x1"] = np.stack([X1("Wq").reshape(D, D), X1("Wk").reshape(D, D), X1("Wv").reshape(D, D),
                          X1("Wo").reshape(D, D)], 1)
    mask = i["mask_BxSxS2_bk1"]
    a["mq8"] = mask.reshape(NJ, P, CS).transpose(1, 0, 2)
    a["mk8"] = mask.reshape(B, T, CS // P, P).transpose(3, 0, 2, 1)
    a["w_g1"] = F1("gate_w").T
    a["eb"] = F1("e_bias")
    a["w_up1"] = F1("up_w").reshape(C1, P, D).transpose(2, 0, 1)
    a["w_dn1"] = F1("down_w").transpose(0, 2, 1).reshape(C1, P, D).transpose(1, 0, 2)
    a["w_sh"] = np.concatenate([F1("shared_up_w").reshape(SH, P, D).transpose(2, 0, 1),
                                chunks(F1("shared_down_w").T)], 1)
    return {k: np.ascontiguousarray(x) for k, x in a.items()}


def kernel(**inputs):
    import concourse.bacc as bacc
    from concourse.bass_utils import run_bass_kernel_spmd

    nc = bacc.Bacc("TRN2", target_bir_lowering=False, num_devices=1)
    arrays = _layout(inputs)
    aps = {k: nc.dram_tensor(f"in_{k}", x.shape, mybir.dt.from_np(x.dtype), kind="ExternalInput").ap()
           for k, x in arrays.items()}
    out = nc.dram_tensor("out", (P, NJ, D), mybir.dt.float32, kind="ExternalOutput").ap()
    program(nc, aps, out)
    r = run_bass_kernel_spmd(nc, [{f"in_{k}": x for k, x in arrays.items()}], core_ids=[0])
    return r.results[0]["out"].transpose(1, 0, 2).reshape(B, T, D)
```
